# Optimizing a Trainium2 kernel written in Bass

```python
import numpy as np
import jax
import jax.numpy as jnp

def _softmax(x, axis=-1):
    return jax.nn.softmax(x, axis=axis)

def _gelu(x):
    return jax.nn.gelu(x, approximate=True)

def _silu(x):
    return jax.nn.silu(x)

def _sigmoid(x):
    return jax.nn.sigmoid(x)

def _layernorm(x, axis=-1, eps=1e-05):
    m = jnp.mean(x, axis=axis, keepdims=True)
    v = jnp.var(x, axis=axis, keepdims=True)
    return (x - m) / jnp.sqrt(v + eps)

def _scatter_add(tgt, idx, src, axis=0):
    return tgt.at[idx].add(src)

def _segment_sum(src, seg, n):
    return jax.ops.segment_sum(src, seg, n)
kernel_name = 'mk_macaron_d1_jaxref_r8_261d13'

def setup_inputs(seed: int=0):
    np.random.seed(seed)
    _w = jnp.asarray

    def _L0_attn_setup():
        import jax, jax.numpy as jnp
        import numpy as np
        D_HEAD = 64
        MASK_FILL = -1000000.0
        key = jax.random.key(seed)
        ks = jax.random.split(key, 5)
        batch, seq, d_model, n_heads, d_head = (4, 256, 128, 16, D_HEAD)
        bound_qkv = float(np.sqrt(6.0 / (d_model + n_heads * d_head)))
        bound_out = float(np.sqrt(6.0 / (d_head + n_heads * d_model)))
        return {'resid': jax.random.normal(ks[0], (batch, seq, d_model), dtype=jnp.float32), 'W_Q': jax.random.uniform(ks[1], (d_model, n_heads, d_head), jnp.float32, -bound_qkv, bound_qkv), 'W_K': jax.random.uniform(ks[2], (d_model, n_heads, d_head), jnp.float32, -bound_qkv, bound_qkv), 'W_V': jax.random.uniform(ks[3], (d_model, n_heads, d_head), jnp.float32, -bound_qkv, bound_qkv), 'W_out': jax.random.uniform(ks[4], (d_head, n_heads, d_model), jnp.float32, -bound_out, bound_out), 'b_out': jnp.zeros((d_model,), dtype=jnp.float32)}
    _L0_attn_in = _L0_attn_setup()

    def _L0_ffn_setup():
        import jax, jax.numpy as jnp
        import numpy as np
        DIM = 128
        DEPTH = 2
        HEADS = 8
        DIM_HEAD = 64
        WINDOW = 64
        INNER = HEADS * DIM_HEAD
        HID = int(DIM * 4 * 2 / 3)
        B, N = (2, 1024)
        QK_SCALE = 8.0

        def shift_token(t):
            t1, t2 = jnp.split(t, 2, axis=-1)
            t2 = jnp.pad(t2, ((0, 0), (1, 0), (0, 0)))[:, :-1]
            return jnp.concatenate([t1, t2], axis=-1)

        def l2norm(t):
            return t / jnp.clip(jnp.linalg.norm(t, axis=-1, keepdims=True), 1e-12)

        def rotate_half(x):
            x1, x2 = jnp.split(x, 2, axis=-1)
            return jnp.concatenate([-x2, x1], axis=-1)

        def rotary_xpos(q, k):
            n = q.shape[-2]
            half_idx = jnp.arange(0, DIM_HEAD, 2, dtype=jnp.float32)
            inv_freq = 1.0 / 10000.0 ** (half_idx / DIM_HEAD)
            t = jnp.arange(n, dtype=jnp.float32)
            freqs = t[:, None] * inv_freq[None, :]
            freqs = jnp.concatenate([freqs, freqs], axis=-1)
            base = (half_idx + 0.4 * DIM_HEAD) / (1.4 * DIM_HEAD)
            power = (t - n // 2) / float(WINDOW // 2)
            scale = base[None, :] ** power[:, None]
            scale = jnp.concatenate([scale, scale], axis=-1)
            cos, sin = (jnp.cos(freqs), jnp.sin(freqs))
            q = q * cos * scale + rotate_half(q) * sin * scale
            k = k * cos / scale + rotate_half(k) * sin / scale
            return (q, k)

        def local_attention(q, k, v):
            b, h, n, d = q.shape
            w = n // WINDOW
            bq = q.reshape(b, h, w, WINDOW, d) * QK_SCALE
            bk = k.reshape(b, h, w, WINDOW, d)
            bv = v.reshape(b, h, w, WINDOW, d)

            def look_around(t):
                p = jnp.pad(t, ((0, 0), (0, 0), (1, 0), (0, 0), (0, 0)))
                return jnp.concatenate([p[:, :, :w], p[:, :, 1:]], axis=3)
            bk, bv = (look_around(bk), look_around(bv))
            bt = jnp.arange(n).reshape(w, WINDOW)
            btp = jnp.pad(bt, ((1, 0), (0, 0)), constant_values=-1)
            btk = jnp.concatenate([btp[:w], btp[1:]], axis=1)
            sim = jnp.einsum('bhwid,bhwjd->bhwij', bq, bk)
            i = bt[:, :, None]
            j = btk[:, None, :]
            mask = (i < j) | (i > j + WINDOW) | (j == -1)
            sim = jnp.where(mask, -jnp.finfo(sim.dtype).max, sim)
            attn = jax.nn.softmax(sim, axis=-1)
            out = jnp.einsum('bhwij,bhwjd->bhwid', attn, bv)
            return out.reshape(b, h, n, d)

        def _layer(x, wqkv, qs, ksc, wo, lg, lb, w1, b1, w2, b2):
            b, n, _ = x.shape
            h = shift_token(x)
            qkv = h @ wqkv
            q, k, v = jnp.split(qkv, 3, axis=-1)
            to_heads = lambda t: t.reshape(b, n, HEADS, DIM_HEAD).transpose(0, 2, 1, 3)
            q, k, v = (to_heads(q), to_heads(k), to_heads(v))
            q = l2norm(q) * qs
            k = l2norm(k) * ksc
            q, k = rotary_xpos(q, k)
            o = local_attention(q, k, v)
            o = o.transpose(0, 2, 1, 3).reshape(b, n, INNER)
            x = x + o @ wo
            h = shift_token(x)
            mu = h.mean(-1, keepdims=True)
            var = h.var(-1, keepdims=True)
            h = (h - mu) / jnp.sqrt(var + 1e-05) * lg + lb
            h = h @ w1 + b1
            a, g = jnp.split(h, 2, axis=-1)
            h = a * jax.nn.gelu(g, approximate=False)
            x = x + h @ w2 + b2
            return x
        key = jax.random.key(seed)
        ks = jax.random.split(key, 6)
        return {'x': jax.random.normal(ks[0], (B, N, DIM), jnp.float32), 'wqkv': jax.random.normal(ks[1], (DEPTH, DIM, 3 * INNER), jnp.float32) * 0.02, 'q_scale': jnp.ones((DEPTH, DIM_HEAD), jnp.float32), 'k_scale': jnp.ones((DEPTH, DIM_HEAD), jnp.float32), 'wo': jax.random.normal(ks[2], (DEPTH, INNER, DIM), jnp.float32) * 0.02, 'ln_g': jnp.ones((DEPTH, DIM), jnp.float32), 'ln_b': jnp.zeros((DEPTH, DIM), jnp.float32), 'w1': jax.random.normal(ks[3], (DEPTH, DIM, 2 * HID), jnp.float32) * 0.02, 'b1': jnp.zeros((DEPTH, 2 * HID), jnp.float32), 'w2': jax.random.normal(ks[4], (DEPTH, HID, DIM), jnp.float32) * 0.02, 'b2': jnp.zeros((DEPTH, DIM), jnp.float32)}
    _L0_ffn_in = _L0_ffn_setup()
    _d = {'L0_attn_resid': _L0_attn_in['resid'], 'L0_attn_W_Q': _L0_attn_in['W_Q'], 'L0_attn_W_K': _L0_attn_in['W_K'], 'L0_attn_W_V': _L0_attn_in['W_V'], 'L0_attn_W_out': _L0_attn_in['W_out'], 'L0_attn_b_out': _L0_attn_in['b_out'], 'L0_ffn_wqkv': _L0_ffn_in['wqkv'], 'L0_ffn_q_scale': _L0_ffn_in['q_scale'], 'L0_ffn_k_scale': _L0_ffn_in['k_scale'], 'L0_ffn_wo': _L0_ffn_in['wo'], 'L0_ffn_ln_g': _L0_ffn_in['ln_g'], 'L0_ffn_ln_b': _L0_ffn_in['ln_b'], 'L0_ffn_w1': _L0_ffn_in['w1'], 'L0_ffn_b1': _L0_ffn_in['b1'], 'L0_ffn_w2': _L0_ffn_in['w2'], 'L0_ffn_b2': _L0_ffn_in['b2']}
    _x0 = _d['L0_attn_resid']
    _d['L0_attn_resid'] = jax.random.normal(jax.random.fold_in(jax.random.key(seed), 1), (4, 1024, 128), dtype=_x0.dtype)
    del _x0
    return _d

def reference(L0_attn_resid, L0_attn_W_Q, L0_attn_W_K, L0_attn_W_V, L0_attn_W_out, L0_attn_b_out, L0_ffn_wqkv, L0_ffn_q_scale, L0_ffn_k_scale, L0_ffn_wo, L0_ffn_ln_g, L0_ffn_ln_b, L0_ffn_w1, L0_ffn_b1, L0_ffn_w2, L0_ffn_b2):

    def _L0_attn_ref(resid, W_Q, W_K, W_V, W_out, b_out):
        import jax, jax.numpy as jnp
        import numpy as np
        D_HEAD = 64
        MASK_FILL = -1000000.0
        seq = resid.shape[1]
        d_head = W_Q.shape[-1]
        q = jnp.einsum('bsd,dhk->bshk', resid, W_Q)
        k = jnp.einsum('bsd,dhk->bshk', resid, W_K)
        v = jnp.einsum('bsd,dhk->bshk', resid, W_V)
        scores = jnp.einsum('bqhk,bkhd->bhqd', q, k.astype(q.dtype)) if False else jnp.einsum('bqhc,bshc->bhqs', q, k)
        scores = scores / jnp.sqrt(jnp.asarray(d_head, dtype=scores.dtype))
        causal_mask = jnp.triu(jnp.ones((seq, seq), dtype=bool), k=1)
        scores = jnp.where(causal_mask, MASK_FILL, scores)
        probs = jax.nn.softmax(scores, axis=-1)
        z = jnp.einsum('bhqs,bshc->bqhc', probs, v)
        out = jnp.einsum('bqhc,chd->bqd', z, W_out) + b_out
        return out

    def _L0_ffn_ref(x, wqkv, q_scale, k_scale, wo, ln_g, ln_b, w1, b1, w2, b2):
        import jax, jax.numpy as jnp
        import numpy as np
        DIM = 128
        DEPTH = 2
        HEADS = 8
        DIM_HEAD = 64
        WINDOW = 64
        INNER = HEADS * DIM_HEAD
        HID = int(DIM * 4 * 2 / 3)
        B, N = (2, 1024)
        QK_SCALE = 8.0

        def shift_token(t):
            t1, t2 = jnp.split(t, 2, axis=-1)
            t2 = jnp.pad(t2, ((0, 0), (1, 0), (0, 0)))[:, :-1]
            return jnp.concatenate([t1, t2], axis=-1)

        def l2norm(t):
            return t / jnp.clip(jnp.linalg.norm(t, axis=-1, keepdims=True), 1e-12)

        def rotate_half(x):
            x1, x2 = jnp.split(x, 2, axis=-1)
            return jnp.concatenate([-x2, x1], axis=-1)

        def rotary_xpos(q, k):
            n = q.shape[-2]
            half_idx = jnp.arange(0, DIM_HEAD, 2, dtype=jnp.float32)
            inv_freq = 1.0 / 10000.0 ** (half_idx / DIM_HEAD)
            t = jnp.arange(n, dtype=jnp.float32)
            freqs = t[:, None] * inv_freq[None, :]
            freqs = jnp.concatenate([freqs, freqs], axis=-1)
            base = (half_idx + 0.4 * DIM_HEAD) / (1.4 * DIM_HEAD)
            power = (t - n // 2) / float(WINDOW // 2)
            scale = base[None, :] ** power[:, None]
            scale = jnp.concatenate([scale, scale], axis=-1)
            cos, sin = (jnp.cos(freqs), jnp.sin(freqs))
            q = q * cos * scale + rotate_half(q) * sin * scale
            k = k * cos / scale + rotate_half(k) * sin / scale
            return (q, k)

        def local_attention(q, k, v):
            b, h, n, d = q.shape
            w = n // WINDOW
            bq = q.reshape(b, h, w, WINDOW, d) * QK_SCALE
            bk = k.reshape(b, h, w, WINDOW, d)
            bv = v.reshape(b, h, w, WINDOW, d)

            def look_around(t):
                p = jnp.pad(t, ((0, 0), (0, 0), (1, 0), (0, 0), (0, 0)))
                return jnp.concatenate([p[:, :, :w], p[:, :, 1:]], axis=3)
            bk, bv = (look_around(bk), look_around(bv))
            bt = jnp.arange(n).reshape(w, WINDOW)
            btp = jnp.pad(bt, ((1, 0), (0, 0)), constant_values=-1)
            btk = jnp.concatenate([btp[:w], btp[1:]], axis=1)
            sim = jnp.einsum('bhwid,bhwjd->bhwij', bq, bk)
            i = bt[:, :, None]
            j = btk[:, None, :]
            mask = (i < j) | (i > j + WINDOW) | (j == -1)
            sim = jnp.where(mask, -jnp.finfo(sim.dtype).max, sim)
            attn = jax.nn.softmax(sim, axis=-1)
            out = jnp.einsum('bhwij,bhwjd->bhwid', attn, bv)
            return out.reshape(b, h, n, d)

        def _layer(x, wqkv, qs, ksc, wo, lg, lb, w1, b1, w2, b2):
            b, n, _ = x.shape
            h = shift_token(x)
            qkv = h @ wqkv
            q, k, v = jnp.split(qkv, 3, axis=-1)
            to_heads = lambda t: t.reshape(b, n, HEADS, DIM_HEAD).transpose(0, 2, 1, 3)
            q, k, v = (to_heads(q), to_heads(k), to_heads(v))
            q = l2norm(q) * qs
            k = l2norm(k) * ksc
            q, k = rotary_xpos(q, k)
            o = local_attention(q, k, v)
            o = o.transpose(0, 2, 1, 3).reshape(b, n, INNER)
            x = x + o @ wo
            h = shift_token(x)
            mu = h.mean(-1, keepdims=True)
            var = h.var(-1, keepdims=True)
            h = (h - mu) / jnp.sqrt(var + 1e-05) * lg + lb
            h = h @ w1 + b1
            a, g = jnp.split(h, 2, axis=-1)
            h = a * jax.nn.gelu(g, approximate=False)
            x = x + h @ w2 + b2
            return x
        for l in range(DEPTH):
            x = _layer(x, wqkv[l], q_scale[l], k_scale[l], wo[l], ln_g[l], ln_b[l], w1[l], b1[l], w2[l], b2[l])
        return x
    x = L0_attn_resid
    x = x + 0.5 * _L0_ffn_ref(_layernorm(x, axis=-1), L0_ffn_wqkv, L0_ffn_q_scale, L0_ffn_k_scale, L0_ffn_wo, L0_ffn_ln_g, L0_ffn_ln_b, L0_ffn_w1, L0_ffn_b1, L0_ffn_w2, L0_ffn_b2)
    x = x + _L0_attn_ref(_layernorm(x, axis=-1), L0_attn_W_Q, L0_attn_W_K, L0_attn_W_V, L0_attn_W_out, L0_attn_b_out)
    x = x + 0.5 * _L0_ffn_ref(_layernorm(x, axis=-1), L0_ffn_wqkv, L0_ffn_q_scale, L0_ffn_k_scale, L0_ffn_wo, L0_ffn_ln_g, L0_ffn_ln_b, L0_ffn_w1, L0_ffn_b1, L0_ffn_w2, L0_ffn_b2)
    return x

_drawn_inputs = setup_inputs


def setup_inputs(seed=0):
    import zlib

    import numpy as np

    out = dict(_drawn_inputs(seed))
    spreads = {'L0_attn_b_out': (0.0, 0.291),
     'L0_ffn_q_scale': (1.0, 0.6),
     'L0_ffn_k_scale': (1.0, 0.6),
     'L0_ffn_ln_g': (1.0, 0.6),
     'L0_ffn_ln_b': (0.0, 0.8),
     'L0_ffn_b1': (0.0, 0.8),
     'L0_ffn_b2': (0.0, 0.1)}
    factors = {'L0_attn_W_Q': 7.044,
     'L0_attn_W_K': 7.121,
     'L0_ffn_wqkv': 3.353,
     'L0_ffn_wo': 3.331,
     'L0_ffn_w1': 5.301,
     'L0_ffn_w2': 5.221}
    for name, (base, spread) in spreads.items():
        noise = np.random.default_rng([zlib.crc32(name.encode()), seed]).standard_normal(out[name].shape)
        drawn = base * np.exp(spread * noise) if base else spread * noise
        out[name] = jnp.asarray(drawn.astype(out[name].dtype))
    for name, factor in factors.items():
        out[name] = (out[name] * factor).astype(out[name].dtype)
    return out
```

```python
from contextlib import ExitStack

import concourse.bass as bass
from concourse import mybir

F32 = mybir.dt.float32
BF16 = mybir.dt.bfloat16
ACT = mybir.ActivationFunctionType
ALU = mybir.AluOpType
AX = mybir.AxisListType

P = 128
BANK = 512
GROUP = BANK // P
LN_EPS = 1e-5
NORM_FLOOR = 1e-24
MASKED = -1e30


def build_program(nc, x_in, wq_t, wk_t, wv, w_out, b_out, wqkv, qk_scale, wo, ln_g, ln_b,
                  w1, b1, w2, b2, rot_cos, rot_sin, local_mask, not_first, causal_mask, identity,
                  out):
    B, TOKENS, DIM = x_in.shape
    T = TOKENS // P
    DEPTH, _, INNER3 = wqkv.shape
    INNER = INNER3 // 3
    DH = qk_scale.shape[3]
    HEADS = INNER // DH
    PAIRS = HEADS // 2
    HID = w2.shape[1]
    HC = (HID + P - 1) // P
    HROWS = [min(P, HID - P * j) for j in range(HC)]
    NT = DEPTH * T
    W = P // 2
    AH = wq_t.shape[1]
    ADH = wq_t.shape[0]
    APAIRS = AH // 2
    CAUSAL_SCALE = float(ADH) ** -0.5
    assert DIM == P and DH == W and ADH == W and B * P == BANK and INNER == BANK

    with ExitStack() as ctx:
        def sb(name, shape, dt=F32, at=ctx):
            return at.enter_context(nc.sbuf_tensor(name, shape, dt))

        def sem(name):
            return ctx.enter_context(nc.semaphore(name))

        x = sb("x", [P, B, T, P])
        ident = sb("ident", [P, P])
        ident_bf = sb("ident_bf", [P, P], BF16)
        wqkv_sb = sb("wqkv_sb", [P, DEPTH, 3 * INNER])
        wo_sb = sb("wo_sb", [P, DEPTH, PAIRS, P])
        w2_sb = sb("w2_sb", [P, DEPTH, HC, P])
        g_col = sb("g_col", [P, DEPTH])
        b_col = sb("b_col", [P, DEPTH])
        b1_col = sb("b1_col", [P, DEPTH, 2, HC])
        b2_row = sb("b2_row", [P, DEPTH, P])
        bout_row = sb("bout_row", [P, P])
        scale_row = sb("scale_row", [P, DEPTH, 2, DH])
        cos_t = sb("cos_t", [P, NT, 2, DH])
        sin_t = sb("sin_t", [P, NT, 2, DH])
        lmask = sb("lmask", [P, NT, P], BF16)
        notfirst = sb("notfirst", [P, NT])
        cmask = sb("cmask", [P, P], BF16)
        minus_half = sb("minus_half", [P, 2 * HEADS])
        eps_t = sb("eps_t", [P, T])
        spare = sb("spare", [P, 1])
        stats = sb("stats", [P, T, 6])
        mv = sb("mv", [P, T, 2])
        veps = sb("veps", [P, T])
        rstd = sb("rstd", [P, T])

        local = ExitStack()
        y = sb("y", [P, B, NT + T, P], at=local)
        a_in = sb("a_in", [P, B, P], at=local)
        h_t = sb("h_t", [P, B, P + 1], at=local)
        sq = sb("sq", [P, 2, HEADS, DH], at=local)
        qn = sb("qn", [P, 2, HEADS, DH], at=local)
        qkr = sb("qkr", [P, 2, HEADS, DH], at=local)
        ss = sb("ss", [P, 2 * HEADS], at=local)
        rn = sb("rn", [P, 2 * HEADS], at=local)
        q_t = sb("q_t", [P, B, HEADS, P], at=local)
        k_t = sb("k_t", [P, B, PAIRS, 3, W], at=local)
        v_cur = sb("v_cur", [P, B, INNER], at=local)
        v_mix = sb("v_mix", [P, B, INNER], at=local)
        probs = sb("probs", [P, 2, HEADS, P], at=local)
        probs_t = sb("probs_t", [P, HEADS, P], at=local)
        nmax = sb("nmax", [P, 2, HEADS], at=local)
        rsum = sb("rsum", [P, 2, HEADS], at=local)
        rinv = sb("rinv", [P, 2, HEADS], at=local)
        z_t = sb("z_t", [P, PAIRS, P], at=local)
        y1 = sb("y1", [P, B, P], at=local)
        h2_t = sb("h2_t", [P, B, P + 1], at=local)
        hn = sb("hn", [P, B, P], at=local)
        hn_t = sb("hn_t", [P, B, P], at=local)
        w1_cur = sb("w1_cur", [P, 2 * HID], at=local)
        u_t = sb("u_t", [P, HC, B * P], at=local)
        local.close()

        causal = ExitStack()
        wq_sb = sb("wq_sb", [ADH, AH, P], at=causal)
        wk_sb = sb("wk_sb", [ADH, AH, P], at=causal)
        m_sb = sb("m_sb", [P, AH, P], at=causal)
        m_cur = sb("m_cur", [P, 2, 2, P], at=causal)
        wv_sb = sb("wv_sb", [P, AH * ADH], at=causal)
        wout_sb = sb("wout_sb", [P, APAIRS, P], at=causal)
        xn = sb("xn", [P, T, P], at=causal)
        xn_t = sb("xn_t", [P, T * P], at=causal)
        qm = sb("qm", [P, 2, 2, T * P], at=causal)
        va = sb("va", [P, 2, T, P], at=causal)
        ca_p = sb("ca_p", [P, 2, 2, T * P], at=causal)
        ca_pt = sb("ca_pt", [P, 2, 2, T, P], at=causal)
        ca_nmax = sb("ca_nmax", [P, 2, T, 2], at=causal)
        ca_rsum = sb("ca_rsum", [P, 2, T, 2], at=causal)
        ca_rinv = sb("ca_rinv", [P, T // 2, 2, ADH], at=causal)
        ca_rt = sb("ca_rt", [P, BANK], at=causal)
        ca_z = sb("ca_z", [P, BANK], at=causal)
        causal.close()

        def bank(name, n=1):
            return ctx.enter_context(nc.psum_tensor(name, [P, n * BANK], F32))

        ps_qk = bank("ps_qk", 2)
        ps_v = bank("ps_v")
        ps_t = bank("ps_t")
        ps_s = bank("ps_s", 2)
        ps_w = bank("ps_w")
        ps_z = bank("ps_z")

        x_loaded, const_loaded, heads_loaded = sem("x_loaded"), sem("const_loaded"), sem("heads_loaded")
        stored = sem("stored")
        tables_ready, powers_ready = sem("tables_ready"), sem("powers_ready")
        q_zeroed = sem("q_zeroed")
        stack_done = sem("stack_done")
        causal_done = sem("causal_done")
        names = """bias_in ln_stats ln_aggr ln_veps ln_rstd ln_out
            a_copied a_turned h_lo h_ready qk_made v_made squared summed clamped normed_r qk_normed
            rot_sin_done rot_cos_done rotated q_turned k_turned q_ready k_kept k_ready v_kept v_ready
            s_made max_ready exp_done rinv_ready p_ready p_turned pt_ready z_made z_ready o_made
            y1_ready t1_made h2_lo h2_ready t2_made c_stats c_agg c_eps c_rstd hn_ready t3_made
            hn_t_ready w1_copied gv_made gelu_done u_done w2_made bias_added y2_done
            m_made ca_stats ca_aggr ca_veps ca_rstd ca_xn ca_turned ca_xn_t m_copied
            ca_proj ca_q_ready ca_v_ready ca_s ca_max ca_exp ca_pt ca_pt_dve ca_pt_act ca_pv
            ca_rinv_ready ca_r_made ca_rt_ready ca_z_ready ca_o ca_x_added""".split()
        S = {n: sem(n) for n in names}

        def wait(eng, s, n):
            if not isinstance(n, int) or n > 0:
                eng.wait_ge(s, n)

        def stack(eng, body):
            body(0, True, False, False, True)
            body(1, True, True, False, True)
            body(2, True, True, True, True)
            with eng.Fori(3, NT - 1) as i:
                body(i, True, True, True, True)
            body(NT - 1, True, True, True, False)
            body(NT, False, True, True, False)
            body(NT + 1, False, False, True, False)

        def pe_stack(pe, p):
            def turn_tile(i):
                step = NT * p + i
                pe.wait_ge(S["a_copied"], 16 * step + 16)
                wait(pe, S["v_ready"], step * B)
                for b in range(B):
                    mm = pe.transpose(ps_v[:, P * b:P * b + P], a_in[:, b, :], ident[:])
                mm.then_inc(S["a_turned"], 1)

            def body(i, a, b_, c, more):
                step = NT * p + i
                nA, nB, mC = step * B, (step - 1) * B, step - 2
                def scores(k):
                    pe.wait_ge(S["q_ready"], nB + k + 1)
                    pe.wait_ge(S["k_ready"], nB + k + 1)
                    wait(pe, S["exp_done"], nB + k)
                    if k == 0:
                        wait(pe, S["u_done"], (step - 2) * HC)
                    for g in range(HEADS // GROUP):
                        pe.matmul(ps_s[:, BANK * g:BANK * g + BANK], ident_bf[:],
                                  lmask[:, i - 1, :].unsqueeze(1).broadcast_to([P, GROUP, P]),
                                  start=True, stop=False, skip_group_check=True)
                    for h in range(HEADS):
                        keys = k_t[:, k, h // 2, :, :]
                        for w in range(2):
                            mm = pe.matmul(ps_s[W * w:W * w + W, P * h:P * h + P],
                                           q_t[:, k, h, W * w:W * w + W],
                                           keys[:, 0:2, :] if w else keys[:, 0:3:2, :],
                                           start=False, stop=True, skip_group_check=True)
                    mm.then_inc(S["s_made"], 1)

                def project_qk(k):
                    if k == 0:
                        pe.wait_ge(S["h_ready"], step + 1)
                        wait(pe, S["u_done"], (step - 2) * HC)
                    wait(pe, S["qk_normed"], nA + k)
                    for c_ in range(2):
                        mm = pe.matmul(ps_qk[:, INNER * c_:INNER * c_ + INNER], h_t[:, k, 0:P],
                                       wqkv_sb[:, i // T, INNER * c_:INNER * c_ + INNER],
                                       start=True, stop=True)
                    mm.then_inc(S["qk_made"], 1)

                def turn_probs(k):
                    pe.wait_ge(S["p_ready"], nB + k + 1)
                    wait(pe, S["y1_ready"], nB + k)
                    if a and k:
                        wait(pe, S["k_ready"], nA + k)
                    else:
                        wait(pe, S["k_ready"], min(nA, NT * (p + 1) * B) if isinstance(nA, int) else nA)
                    for h in range(HEADS):
                        dst = (ps_w, ps_z)[h // GROUP]
                        mm = pe.transpose(dst[:, P * (h % GROUP):P * (h % GROUP) + P],
                                          probs[:, k % 2, h, :], ident[:])
                    mm.then_inc(S["p_turned"], 1)

                def values(k):
                    pe.wait_ge(S["pt_ready"], nB + k + 1)
                    pe.wait_ge(S["v_ready"], nB + k + 1)
                    for h in range(HEADS):
                        r = W * (h % 2)
                        for w in range(2):
                            v = (v_mix, v_cur)[w]
                            mm = pe.matmul(ps_z[r:r + W, P * (h // 2) + W * w:P * (h // 2) + W * w + W],
                                           v[:, k, DH * h:DH * h + DH], probs_t[:, h, W * w:W * w + W],
                                           start=True, stop=True, skip_group_check=True)
                    mm.then_inc(S["z_made"], 1)

                def project_v(k):
                    wait(pe, S["v_ready"], nA + k)
                    pe.matmul(ps_v[:, :], h_t[:, k, 0:P], wqkv_sb[:, i // T, 2 * INNER:3 * INNER],
                              start=True, stop=True).then_inc(S["v_made"], 1)

                def turn_qk(k):
                    pe.wait_ge(S["rotated"], nA + k + 1)
                    wait(pe, S["q_ready"], nA + k)
                    if c and k < 2:
                        pe.wait_ge(S["hn_t_ready"] if k else S["hn_ready"], mC + 1)
                    for c_, dst, done in ((0, ps_t, "q_turned"), (1, ps_z, "k_turned")):
                        if c_ and b_:
                            pe.wait_ge(S["z_ready"], nB + k + 1)
                        elif c_:
                            wait(pe, S["k_ready"], nA + k)
                        for j in range(PAIRS):
                            mm = pe.transpose(dst[:, P * j:P * j + P],
                                              qkr[:, c_, 2 * j:2 * j + 2, :], ident[:])
                        mm.then_inc(S[done], 1)

                def project_out(k):
                    pe.wait_ge(S["z_ready"], nB + k + 1)
                    for j in range(PAIRS):
                        mm = pe.matmul(ps_w[:, 0:P], z_t[:, j, :], wo_sb[:, (i - 1) // T, j, :],
                                       start=(j == 0), stop=(j == PAIRS - 1))
                    mm.then_inc(S["o_made"], 1)

                def c_turn(src, ready, need, made):
                    pe.wait_ge(S[ready], need)
                    for b in range(B):
                        mm = pe.transpose(ps_t[:, P * b:P * b + P], src[:, b, 0:P], ident[:])
                    mm.then_inc(S[made], 1)

                def widen(j):
                    two = (ps_s, ps_qk, ps_s)[j]
                    if j == 0:
                        pe.wait_ge(S["hn_t_ready"], mC + 1)
                        pe.wait_ge(S["w1_copied"], 16 * mC + 16)
                    if j == 0 and b_:
                        pe.wait_ge(S["exp_done"], nB + B)
                    if j == 1 and a:
                        pe.wait_ge(S["qk_normed"], nA + B)
                    if j == 2:
                        pe.wait_ge(S["u_done"], mC * HC + 1)
                    for c_ in range(2):
                        mm = pe.matmul(two[0:HROWS[j], BANK * c_:BANK * c_ + BANK],
                                       w1_cur[:, HID * c_ + P * j:HID * c_ + P * j + HROWS[j]],
                                       hn_t[:, :, :], start=True, stop=True)
                    mm.then_inc(S["gv_made"], 1)

                def narrow():
                    if a:
                        pe.wait_ge(S["q_ready"], nA + B)
                    pe.wait_ge(S["u_done"], (mC + 1) * HC)
                    for b in range(B):
                        for j in range(HC):
                            mm = pe.matmul(ps_t[:, P * b:P * b + P], u_t[0:HROWS[j], j, P * b:P * b + P],
                                           w2_sb[0:HROWS[j], (i - 2) // T, j, :],
                                           start=(j == 0), stop=(j == HC - 1))
                    mm.then_inc(S["w2_made"], 1)

                if isinstance(i, int) and i == 0:
                    turn_tile(0)
                for k in range(B + 1):
                    if b_ and k < B:
                        scores(k)
                    if a and k < B:
                        project_qk(k)
                    if c and k == 0:
                        wait(pe, S["y2_done"], mC)
                        wait(pe, S["q_ready"], min(nA, NT * (p + 1) * B) if isinstance(nA, int) else nA)
                        c_turn(y1, "y1_ready", (mC + 1) * B, "t1_made")
                    if c and k == 1:
                        c_turn(h2_t, "h2_ready", mC + 1, "t2_made")
                    if c and k == 2:
                        if a:
                            pe.wait_ge(S["q_ready"], nA + 1)
                        c_turn(hn, "hn_ready", mC + 1, "t3_made")
                    if b_ and k:
                        turn_probs(k - 1)
                    if c and k == B:
                        widen(0)
                    if a and k:
                        project_v(k - 1)
                    if b_ and k:
                        values(k - 1)
                    if c and k == B:
                        widen(1)
                    if a and k:
                        turn_qk(k - 1)
                    if b_ and k:
                        project_out(k - 1)
                if c:
                    widen(2)
                if more:
                    turn_tile(i + 1)
                if c:
                    narrow()

            stack(pe, body)

        def act_stack(act, p):
            sc = nc.scalar

            def shift(src, dst, lo_done, done, count, i):
                wait(act, S[done], count)
                sc.activation(dst[W:P, :, 0], dst[W:P, :, P], ACT.Copy, scale=notfirst[W:P, bass.ds(i, 1)])
                sc.copy(dst[0:W, :, 0:P], src[0:W, :].rearrange("p (b t) -> p b t", b=B))\
                  .then_inc(S[lo_done], 1)
                act.wait_ge(S[lo_done], count + 1)
                sc.copy(dst[W:P, :, 1:P + 1], src[W:P, :].rearrange("p (b t) -> p b t", b=B))\
                  .then_inc(S[done], 1)

            def shift_tile(i):
                act.wait_ge(S["a_turned"], NT * p + i + 1)
                shift(ps_v, h_t, "h_lo", "h_ready", NT * p + i, i)

            def body(i, a, b_, c, more):
                step = NT * p + i
                nA, nB, mC = step * B, (step - 1) * B, step - 2
                def gelu(j):
                    two = (ps_s, ps_qk, ps_s)[j]
                    act.wait_ge(S["gv_made"], mC * HC + j + 1)
                    if j == 0:
                        wait(act, S["w2_made"], mC)
                    sc.activation(u_t[0:HROWS[j], j, :], two[0:HROWS[j], BANK:2 * BANK], ACT.Gelu,
                                  bias=b1_col[0:HROWS[j], bass.ds((i - 2) // T, 1), 1, j])\
                      .then_inc(S["gelu_done"], 1)

                if isinstance(i, int) and i == 0:
                    shift_tile(0)
                for k in range(B + 1):
                    if a and k < B:
                        act.wait_ge(S["qk_made"], nA + k + 1)
                        wait(act, S["summed"], nA + k)
                        sc.activation(sq[:, :, :, :], ps_qk[:, :], ACT.Square).then_inc(S["squared"], 1)
                    if c and k == 0:
                        act.wait_ge(S["t1_made"], mC + 1)
                        shift(ps_t, h2_t, "h2_lo", "h2_ready", mC, i - 2)
                    if b_ and k < B:
                        act.wait_ge(S["max_ready"], nB + k + 1)
                        for h in range(HEADS):
                            e = sc.activation(probs[:, k % 2, h, :], ps_s[:, P * h:P * h + P], ACT.Exp,
                                              bias=nmax[:, k % 2, h:h + 1],
                                              accum_out=rsum[:, k % 2, h:h + 1])
                        e.then_inc(S["exp_done"], 1)
                    if c and k == B:
                        gelu(0)
                    if c and k == 2:
                        act.wait_ge(S["t3_made"], mC + 1)
                        lay = (i - 2) // T
                        sc.activation(hn_t[:, :, :], ps_t[:, :], ACT.Identity,
                                      scale=g_col[:, bass.ds(lay, 1)], bias=b_col[:, bass.ds(lay, 1)])\
                          .then_inc(S["hn_t_ready"], 1)
                    if b_ and k:
                        act.wait_ge(S["z_made"], nB + k)
                        sc.copy(z_t[:, :, :], ps_z[:, :]).then_inc(S["z_ready"], 1)
                    if a and k:
                        act.wait_ge(S["v_made"], nA + k)
                        if not (isinstance(i, int) and i == 0):
                            sc.copy(v_mix[W:P, k - 1, :], v_cur[W:P, k - 1, :]).then_inc(S["v_kept"], 1)
                        else:
                            sc.copy(v_mix[W:P, k - 1, :], ps_v[W:P, :]).then_inc(S["v_kept"], 1)
                        sc.copy(v_mix[0:W, k - 1, :], ps_v[0:W, :])
                        act.wait_ge(S["v_kept"], nA + k)
                        sc.copy(v_cur[:, k - 1, :], ps_v[:, :]).then_inc(S["v_ready"], 1)
                    if c and k == B:
                        gelu(1)
                    if a and k:
                        act.wait_ge(S["q_turned"], nA + k)
                        src = ps_t[:, :].rearrange("p (j t) -> p j t", j=PAIRS)
                        sc.copy(q_t[0:W, k - 1, 0:HEADS:2, :], src[0:W])
                        sc.copy(q_t[W:P, k - 1, 1:HEADS:2, :], src[W:P]).then_inc(S["q_ready"], 1)
                if c:
                    gelu(2)
                if more:
                    shift_tile(i + 1)

            stack(act, body)

        def dve_stack(dve, p):
            v = nc.vector

            def body(i, a, b_, c, more):
                step = NT * p + i
                nA, nB, mC = step * B, (step - 1) * B, step - 2
                def gate(j):
                    two = (ps_s, ps_qk, ps_s)[j]
                    dve.wait_ge(S["gelu_done"], mC * HC + j + 1)
                    v.scalar_tensor_tensor(u_t[0:HROWS[j], j, :], two[0:HROWS[j], 0:BANK],
                                           b1_col[0:HROWS[j], bass.ds((i - 2) // T, 1), 0, j],
                                           u_t[0:HROWS[j], j, :], ALU.add, ALU.mult)\
                     .then_inc(S["u_done"], 1)

                for k in range(B + 1):
                    if a and k:
                        n = nA + k
                        dve.wait_ge(S["normed_r"], n)
                        wait(dve, S["rotated"], n - 1)
                        r = rn[:, :].rearrange("p (c h) -> p c h", c=2).unsqueeze(3)
                        v.tensor_tensor(qn[:, :, :, :], ps_qk[:, :].rearrange("p (c h d) -> p c h d", c=2, h=HEADS),
                                        r.broadcast_to([P, 2, HEADS, DH]), ALU.mult).then_inc(S["qk_normed"], 1)
                        dve.wait_ge(S["qk_normed"], n)
                        wait(dve, S["k_turned"], n - 1)
                        half = DH // 2
                        for lo, hi in ((0, half), (half, 0)):
                            rot = v.tensor_tensor(
                                qkr[:, :, :, lo:lo + half], qn[:, :, :, hi:hi + half],
                                sin_t[:, i, :, lo:lo + half].unsqueeze(2).broadcast_to([P, 2, HEADS, half]),
                                ALU.mult)
                        rot.then_inc(S["rot_sin_done"], 1)
                    if b_ and k < B:
                        dve.wait_ge(S["s_made"], nB + k + 1)
                        wait(dve, S["exp_done"], nB + k - 1)
                        v.tensor_reduce(nmax[:, k % 2, :], ps_s[:, :].rearrange("p (h c) -> p h c", h=HEADS),
                                        AX.X, ALU.max, negate=True).then_inc(S["max_ready"], 1)
                    if a and k:
                        dve.wait_ge(S["rot_sin_done"], nA + k)
                        v.tensor_tensor(qn[:, :, :, :], qn[:, :, :, :],
                                        cos_t[:, i, :, :].unsqueeze(2).broadcast_to([P, 2, HEADS, DH]),
                                        ALU.mult).then_inc(S["rot_cos_done"], 1)
                    if c and k == 1:
                        dve.wait_ge(S["t2_made"], mC + 1)
                        wait(dve, S["hn_ready"], mC)
                        for b in range(B):
                            st = v.bn_stats(stats[:, b, :], ps_t[:, P * b:P * b + P])
                        st.then_inc(S["c_stats"], 1)
                        dve.wait_ge(S["c_stats"], mC + 1)
                        v.memset(spare[:, :], 0.0)
                        for b in range(B):
                            st = v.bn_aggr(mv[:, b, :], stats[:, b, :])
                        st.then_inc(S["c_agg"], 1)
                    if b_ and k:
                        dve.wait_ge(S["p_turned"], nB + k)
                        v.tensor_copy(probs_t[:, 0:GROUP, :], ps_w[:, :])
                        v.tensor_copy(probs_t[:, GROUP:HEADS, :], ps_z[:, :]).then_inc(S["pt_ready"], 1)
                    if a and k < B:
                        dve.wait_ge(S["squared"], nA + k + 1)
                        wait(dve, S["normed_r"], nA + k)
                        v.tensor_reduce(ss[:, :], sq[:, :, :, :].rearrange("p c h d -> p (c h) d"),
                                        AX.X, ALU.add).then_inc(S["summed"], 1)
                        dve.wait_ge(S["summed"], nA + k + 1)
                        v.tensor_scalar(ss[:, :], ss[:, :], NORM_FLOOR, None, ALU.max).then_inc(S["clamped"], 1)
                    if c and k == 1:
                        dve.wait_ge(S["c_rstd"], mC + 1)
                        for b in range(B):
                            st = v.tensor_scalar(hn[:, b, :], ps_t[:, P * b:P * b + P], mv[:, b, 0:1],
                                                 rstd[:, b:b + 1], ALU.subtract, ALU.mult)
                        st.then_inc(S["hn_ready"], 1)
                    if c and k == B:
                        gate(0)
                    if b_ and k < B:
                        dve.wait_ge(S["exp_done"], nB + k + 1)
                        wait(dve, S["p_ready"], nB + k - 1)
                        v.reciprocal(rinv[:, k % 2, :], rsum[:, k % 2, :]).then_inc(S["rinv_ready"], 1)
                    if a and k:
                        dve.wait_ge(S["k_turned"], nA + k)
                        src = ps_z[:, :].rearrange("p (j w t) -> p j w t", j=PAIRS, w=2)
                        if not (isinstance(i, int) and i == 0):
                            v.tensor_copy(k_t[:, k - 1, :, 2, :], k_t[:, k - 1, :, 1, :]).then_inc(S["k_kept"], 1)
                        else:
                            v.tensor_copy(k_t[:, k - 1, :, 2, :], src[:, :, 1, :]).then_inc(S["k_kept"], 1)
                        dve.wait_ge(S["k_kept"], nA + k)
                        v.tensor_copy(k_t[:, k - 1, :, 0:2, :], src).then_inc(S["k_ready"], 1)
                    if c and k == B:
                        gate(1)
                    if b_ and k:
                        dve.wait_ge(S["o_made"], nB + k)
                        if c and k == 1:
                            dve.wait_ge(S["bias_added"], mC + 1)
                        v.tensor_tensor(y1[:, k - 1, :], y[:, k - 1, i - 1, :], ps_w[:, 0:P],
                                        ALU.add).then_inc(S["y1_ready"], 1)
                if c:
                    gate(2)
                    dve.wait_ge(S["w2_made"], mC + 1)
                    dve.wait_ge(S["bias_added"], mC + 1)
                    v.tensor_tensor(y[:, :, i + T - 2, :], y[:, :, i + T - 2, :],
                                    ps_t[:, :].rearrange("p (b f) -> p b f", b=B),
                                    ALU.add).then_inc(S["y2_done"], 1)

            stack(dve, body)

        def dve_enter(dve, p):
            v = nc.vector
            if p == 1:
                v.tensor_tensor(x[:, :, :, :].rearrange("p b t d -> p (b t) d"),
                                x[:, :, :, :].rearrange("p b t d -> p (b t) d"),
                                bout_row[:, :].unsqueeze(1).broadcast_to([P, B * T, P]),
                                ALU.add).then_inc(S["bias_in"], 1)
                dve.wait_ge(S["bias_in"], 1)
            for carried in (h_t, h2_t):
                v.memset(carried[W:P, :, P], 0.0)
            with dve.Fori(0, T) as t:
                n = T * p + t
                for b in range(B):
                    st = v.bn_stats(stats[:, b, :], x[:, b, t, :])
                st.then_inc(S["ln_stats"], 1)
                dve.wait_ge(S["ln_stats"], n + 1)
                v.memset(spare[:, :], 0.0)
                for b in range(B):
                    st = v.bn_aggr(mv[:, b, :], stats[:, b, :])
                st.then_inc(S["ln_aggr"], 1)
                dve.wait_ge(S["ln_rstd"], n + 1)
                for b in range(B):
                    st = v.tensor_scalar(y[:, b, t, :], x[:, b, t, :], mv[:, b, 0:1], rstd[:, b:b + 1],
                                         ALU.subtract, ALU.mult)
                st.then_inc(S["ln_out"], 1)
                dve.wait_ge(S["ln_out"], n + 1)

        def pool_enter(pool, p):
            with pool.Fori(0, T) as t:
                n = T * p + t
                pool.wait_ge(S["ln_aggr"], n + 1)
                nc.gpsimd.tensor_tensor(veps[:, 0:B], mv[:, 0:B, 1], eps_t[:, 0:B], ALU.add)\
                  .then_inc(S["ln_veps"], 1)
                pool.wait_ge(S["ln_veps"], n + 1)
                nc.gpsimd.tensor_tensor(rstd[:, 0:B], veps[:, 0:B], minus_half[:, 0:B], ALU.pow)\
                  .then_inc(S["ln_rstd"], 1)

        def pool_stack(pool, p):
            g = nc.gpsimd

            def body(i, a, b_, c, more):
                step = NT * p + i
                nA, nB, mC = step * B, (step - 1) * B, step - 2
                if c:
                    lay = (i - 2) // T
                    pool.wait_ge(S["y1_ready"], (mC + 1) * B)
                    g.tensor_tensor(y[:, :, i + T - 2, :], y1[:, :, :],
                                    b2_row[:, bass.ds(lay, 1), :].broadcast_to([P, B, P]),
                                    ALU.add).then_inc(S["bias_added"], 1)
                for k in range(B + 1):
                    if a and k:
                        pool.wait_ge(S["rot_cos_done"], nA + k)
                        g.tensor_tensor(qkr[:, :, :, :], qn[:, :, :, :], qkr[:, :, :, :], ALU.add)\
                         .then_inc(S["rotated"], 1)
                    if c and k == 1:
                        pool.wait_ge(S["c_agg"], mC + 1)
                        g.tensor_tensor(veps[:, 0:B], mv[:, 0:B, 1], eps_t[:, 0:B], ALU.add).then_inc(S["c_eps"], 1)
                        pool.wait_ge(S["c_eps"], mC + 1)
                        g.tensor_tensor(rstd[:, 0:B], veps[:, 0:B], minus_half[:, 0:B], ALU.pow)\
                         .then_inc(S["c_rstd"], 1)
                    if a and k < B:
                        pool.wait_ge(S["clamped"], nA + k + 1)
                        wait(pool, S["qk_normed"], nA + k)
                        g.tensor_tensor(rn[:, :], ss[:, :], minus_half[:, :], ALU.pow)\
                         .then_inc(S["normed_r"], 1)
                    if b_ and k < B:
                        pool.wait_ge(S["rinv_ready"], nB + k + 1)
                        g.tensor_tensor(probs[:, k % 2, :, :], probs[:, k % 2, :, :],
                                        rinv[:, k % 2, :].unsqueeze(2).broadcast_to([P, HEADS, P]),
                                        ALU.mult).then_inc(S["p_ready"], 1)

            stack(pool, body)

        HALF = T // 2
        UNITS = 2 * T
        assert HALF == GROUP and T * P == 2 * BANK

        def groups(i):
            return (i + GROUP) // GROUP

        def groups_before(i, h=0, g=0):
            return sum(2 * groups(m) for m in range(i)) + h * groups(i) + g

        EV = groups_before(T) // 2

        def causal(eng, start, pair_body, flush):
            with eng.Fori(0, B) as b:
                start(b, APAIRS * b)
                pair_body(b, 0, APAIRS * b, 0, True, False)
                with eng.Fori(0, (APAIRS - 2) // 2) as j:
                    pair_body(b, 2 * j + 1, APAIRS * b + 2 * j + 1, 1, True, True)
                    pair_body(b, 2 * j + 2, APAIRS * b + 2 * j + 2, 0, True, True)
                pair_body(b, APAIRS - 1, APAIRS * b + APAIRS - 1, 1, False, True)
                flush(b, APAIRS * b + APAIRS)

        def pe_causal(pe):
            pe.wait_ge(heads_loaded, 16 * 4)
            for h in range(AH):
                dst = (ps_qk, ps_s)[h // (2 * GROUP)]
                c0 = P * (h % (2 * GROUP))
                pe.matmul(dst[:, c0:c0 + P], wq_sb[:, h, :], wk_sb[:, h, :], start=True, stop=True)\
                  .then_inc(S[{0: "ca_r_made", 1: "ca_turned", 2: "ca_proj"}.get(h, "m_made")], 1)

            def scores(n, par, i, h, tail):
                dst = (ps_qk, ps_s)[h]
                if i == 0:
                    pe.wait_ge(S["ca_q_ready"], 4 * n + 4)
                if i or tail:
                    pe.wait_ge(S["ca_exp"], 1 + UNITS * n + 2 * i + h - 1)
                keys = (i + 1) * P
                for c0 in range(0, keys, BANK):
                    c1 = min(keys, c0 + BANK)
                    pe.matmul(dst[:, c0:c1], qm[:, par, h, P * i:P * i + P], xn_t[:, c0:c1],
                              start=True, stop=c1 < keys, skip_group_check=True)
                pe.matmul(dst[:, P * i:P * i + P], ident_bf[:], cmask[:], start=False, stop=True,
                          skip_group_check=True).then_inc(S["ca_s"], 1)

            def turn(n, i, h):
                pe.wait_ge(S["ca_exp"], 1 + UNITS * n + 2 * i + h + 1)
                for g in range(groups(i)):
                    k = groups_before(i, h, g)
                    dst, read = ((ps_v, "ca_pt_dve"), (ps_t, "ca_pt_act"))[k % 2]
                    pe.wait_ge(S[read], 1 + EV * n + k // 2)
                    for kt in range(GROUP * g, min(i + 1, GROUP * g + GROUP)):
                        mm = pe.transpose(dst[:, P * (kt % GROUP):P * (kt % GROUP) + P],
                                          ca_p[:, i % 2, h, P * kt:P * kt + P], ident[:])
                    mm.then_inc(S["ca_pt"], 1)

            def values(n, par, i):
                k = groups_before(i + 1)
                pe.wait_ge(S["ca_pt_dve"], 1 + EV * n + (k + 1) // 2)
                pe.wait_ge(S["ca_pt_act"], 1 + EV * n + k // 2)
                if i == 0:
                    pe.wait_ge(S["ca_v_ready"], 2 * n + 2)
                if i % HALF == 0:
                    pe.wait_ge(S["ca_z_ready"], 1 + 2 * n + i // HALF)
                for kt in range(i + 1):
                    for h in range(2):
                        mm = pe.matmul(ps_z[W * h:W * h + W, P * (i % HALF):P * (i % HALF) + P],
                                       va[:, par, kt, W * h:W * h + W], ca_pt[:, i % 2, h, kt, :],
                                       start=(kt == 0), stop=(kt == i), skip_group_check=True)
                mm.then_inc(S["ca_pv"], 1)

            def spread_inverses(n, half):
                pe.wait_ge(S["ca_rinv_ready"], 2 * n + half + 1)
                for i in range(HALF * half, HALF * half + HALF):
                    mm = pe.transpose(ps_w[:, P * (i % HALF):P * (i % HALF) + P],
                                      ca_rinv[:, i % HALF, :, :], ident[:])
                mm.then_inc(S["ca_r_made"], 1)

            def project_out(n, pair, half):
                pe.wait_ge(S["ca_z_ready"], 1 + 2 * n + half + 1)
                for i in range(HALF):
                    mm = pe.matmul(ps_w[:, P * i:P * i + P], ca_z[:, P * i:P * i + P],
                                   wout_sb[:, pair, :], start=True, stop=True)
                mm.then_inc(S["ca_o"], 1)

            def project(n, pair, par, g):
                if g == 0:
                    pe.wait_ge(S["m_copied"], 16 * n + 16)
                if g < 4:
                    mm = pe.matmul(ps_w[:, :], m_cur[:, par, g // 2, :],
                                   xn_t[:, BANK * (g % 2):BANK * (g % 2) + BANK], start=True, stop=True)
                else:
                    for kt in range(GROUP * (g - 4), GROUP * (g - 3)):
                        mm = pe.matmul(ps_w[:, P * (kt % GROUP):P * (kt % GROUP) + P],
                                       xn_t[:, P * kt:P * kt + P],
                                       wv_sb[:, bass.ds(pair * P, P)], start=True, stop=True)
                mm.then_inc(S["ca_proj"], 1)

            def start(b, n):
                pe.wait_ge(S["ca_exp"], 1 + UNITS * n)
                pe.wait_ge(S["ca_xn"], b + 1)
                for t in range(T):
                    mm = pe.transpose(ps_qk[:, P * t:P * t + P], xn[:, t, :], ident[:])
                mm.then_inc(S["ca_turned"], 1)
                pe.wait_ge(S["ca_xn_t"], b + 1)
                for g in range(6):
                    if g == 0:
                        pe.wait_ge(S["ca_x_added"], 1 + 2 * n)
                    elif g < 5:
                        pe.wait_ge(S["ca_q_ready"], 4 * n + g)
                    else:
                        pe.wait_ge(S["ca_v_ready"], 2 * n + 1)
                    project(n, 0, 0, g)

            def pair_body(b, pair, n, par, ahead, tail):
                for i in range(T):
                    if i == 3 and ahead:
                        pe.wait_ge(S["ca_x_added"] if tail else S["ca_v_ready"], 2 * n + 1 if tail else 2 * n + 2)
                        project(n + 1, pair + 1, 1 - par, 0)
                    if i == 4 and ahead:
                        pe.wait_ge(S["ca_q_ready"], 4 * n + 5)
                        project(n + 1, pair + 1, 1 - par, 1)
                    for h in range(2):
                        scores(n, par, i, h, tail)
                        if i:
                            turn(n, i - 1, h)
                        elif tail:
                            turn(n - 1, T - 1, h)
                        if i == 7 and h == 0 and ahead:
                            pe.wait_ge(S["ca_q_ready"], 4 * n + 8)
                            project(n + 1, pair + 1, 1 - par, 4)
                    if i == 0 and tail:
                        values(n - 1, 1 - par, T - 2)
                    if i == 1 and tail:
                        values(n - 1, 1 - par, T - 1)
                        pe.wait_ge(S["ca_v_ready"], 2 * n + 2)
                        spread_inverses(n - 1, 1)
                    if i == 2 and tail:
                        project_out(n - 1, pair - 1, 1)
                    if i == 6:
                        project_out(n, pair, 0)
                    if i >= 2:
                        values(n, par, i - 2)
                    if i == 4 and ahead:
                        pe.wait_ge(S["ca_q_ready"], 4 * n + 6)
                        project(n + 1, pair + 1, 1 - par, 2)
                    if i == 5:
                        pe.wait_ge(S["ca_q_ready"] if ahead else S["ca_x_added"], 4 * n + 7 if ahead else 2 * n + 1)
                        spread_inverses(n, 0)
                    if i == 6 and ahead:
                        pe.wait_ge(S["ca_x_added"], 1 + 2 * n + 1)
                        project(n + 1, pair + 1, 1 - par, 3)
                    if i == 7 and ahead:
                        pe.wait_ge(S["ca_v_ready"], 2 * n + 3)
                        project(n + 1, pair + 1, 1 - par, 5)

            def flush(b, n):
                for h in range(2):
                    turn(n - 1, T - 1, h)
                values(n - 1, 1, T - 2)
                values(n - 1, 1, T - 1)
                pe.wait_ge(S["ca_x_added"], 1 + 2 * n - 1)
                spread_inverses(n - 1, 1)
                project_out(n - 1, APAIRS - 1, 1)

            causal(pe, start, pair_body, flush)

        def act_causal(act):
            sc = nc.scalar
            act.wait_ge(S["m_made"], AH - 3)
            for h, done in ((0, "ca_pt_act"), (GROUP, "ca_exp")):
                sc.copy(m_sb[:, h:h + GROUP, :], ps_qk[:, P * h:P * h + BANK]).then_inc(S[done], 1)

            def evacuate(n, i, h):
                for g in range(groups(i)):
                    k = groups_before(i, h, g)
                    if k % 2:
                        act.wait_ge(S["ca_pt"], 2 * EV * n + k + 1)
                        k1 = min(i + 1, GROUP * g + GROUP)
                        sc.copy(ca_pt[:, i % 2, h, GROUP * g:k1, :], ps_t[:, 0:P * (k1 - GROUP * g)])\
                          .then_inc(S["ca_pt_act"], 1)

            def q_out(n, par, g):
                act.wait_ge(S["ca_proj"], 1 + 6 * n + g + 1)
                sc.activation(qm[:, par, g // 2, BANK * (g % 2):BANK * (g % 2) + BANK], ps_w[:, :],
                              ACT.Copy, scale=CAUSAL_SCALE).then_inc(S["ca_q_ready"], 1)

            def spread_out(n, half):
                act.wait_ge(S["ca_r_made"], 1 + 2 * n + half + 1)
                sc.copy(ca_rt[:, :], ps_w[:, :]).then_inc(S["ca_rt_ready"], 1)

            def start(b, n):
                act.wait_ge(S["ca_turned"], 1 + b + 1)
                sc.copy(xn_t[:, :], ps_qk[:, :]).then_inc(S["ca_xn_t"], 1)
                for g in range(4):
                    q_out(n, 0, g)

            def pair_body(b, pair, n, par, ahead, tail):
                for i in range(T):
                    for h in range(2):
                        act.wait_ge(S["ca_max"], UNITS * n + 2 * i + h + 1)
                        sc.activation(ca_p[:, i % 2, h, 0:(i + 1) * P], (ps_qk, ps_s)[h][:, 0:(i + 1) * P],
                                      ACT.Exp, bias=ca_nmax[:, par, i, h:h + 1],
                                      accum_out=ca_rsum[:, par, i, h:h + 1]).then_inc(S["ca_exp"], 1)
                        if i == 3 and h == 0 and ahead:
                            q_out(n + 1, 1 - par, 0)
                        if i == 4 and h == 0 and ahead:
                            q_out(n + 1, 1 - par, 1)
                        if i:
                            evacuate(n, i - 1, h)
                        elif tail:
                            evacuate(n - 1, T - 1, h)
                    if i == 1 and tail:
                        spread_out(n - 1, 1)
                    if i == 4 and ahead:
                        q_out(n + 1, 1 - par, 2)
                    if i == 5:
                        spread_out(n, 0)
                    if i == 6 and ahead:
                        q_out(n + 1, 1 - par, 3)

            def flush(b, n):
                for h in range(2):
                    evacuate(n - 1, T - 1, h)
                spread_out(n - 1, 1)

            causal(act, start, pair_body, flush)

        def dve_causal(dve):
            v = nc.vector
            dve.wait_ge(S["m_made"], AH - 3)
            for h, done in ((0, "ca_x_added"), (3, "ca_pt_dve"), (6, "ca_z_ready")):
                h1 = min(h + 3, 2 * GROUP)
                v.tensor_copy(m_sb[:, 2 * GROUP + h:2 * GROUP + h1, :], ps_s[:, P * h:P * h1])\
                 .then_inc(S[done], 1)

            def evacuate(n, i, h):
                for g in range(groups(i)):
                    k = groups_before(i, h, g)
                    if k % 2 == 0:
                        dve.wait_ge(S["ca_pt"], 2 * EV * n + k + 1)
                        k1 = min(i + 1, GROUP * g + GROUP)
                        v.tensor_copy(ca_pt[:, i % 2, h, GROUP * g:k1, :], ps_v[:, 0:P * (k1 - GROUP * g)])\
                         .then_inc(S["ca_pt_dve"], 1)

            def v_out(n, par, g):
                dve.wait_ge(S["ca_proj"], 1 + 6 * n + g + 1)
                v.tensor_copy(va[:, par, GROUP * (g - 4):GROUP * (g - 3), :], ps_w[:, :])\
                 .then_inc(S["ca_v_ready"], 1)

            def invert(n, par, half):
                dve.wait_ge(S["ca_exp"], 1 + UNITS * n + UNITS // 2 * (half + 1))
                wait(dve, S["ca_r_made"], 1 + 2 * n + half)
                sums = ca_rsum[:, par, HALF * half:HALF * half + HALF, :]
                v.reciprocal(ca_rinv[:, :, :, :], sums.unsqueeze(3).broadcast_to([P, HALF, 2, W]))\
                 .then_inc(S["ca_rinv_ready"], 1)

            def z_out(n, half):
                dve.wait_ge(S["ca_rt_ready"], 2 * n + half + 1)
                dve.wait_ge(S["ca_pv"], T * n + HALF * (half + 1))
                v.tensor_tensor(ca_z[:, :], ps_z[:, :], ca_rt[:, :], ALU.mult).then_inc(S["ca_z_ready"], 1)

            def x_add(b, n, half):
                dve.wait_ge(S["ca_o"], 2 * n + half + 1)
                dve.wait_ge(S["ca_x_added"], 1 + 2 * n + half)
                tiles = x[:, bass.ds(b, 1), HALF * half:HALF * half + HALF, :]
                v.tensor_tensor(tiles, tiles, ps_w[:, :], ALU.add).then_inc(S["ca_x_added"], 1)

            def start(b, n):
                for t in range(T):
                    st = v.bn_stats(stats[:, t, :], x[:, bass.ds(b, 1), t, :])
                st.then_inc(S["ca_stats"], 1)
                dve.wait_ge(S["ca_stats"], b + 1)
                v.memset(spare[:, :], 0.0)
                for t in range(T):
                    st = v.bn_aggr(mv[:, t, :], stats[:, t, :])
                st.then_inc(S["ca_aggr"], 1)
                dve.wait_ge(S["ca_rstd"], b + 1)
                dve.wait_ge(S["ca_turned"], 1 + b)
                for t in range(T):
                    st = v.tensor_scalar(xn[:, t, :], x[:, bass.ds(b, 1), t, :], mv[:, t, 0:1],
                                         rstd[:, t:t + 1], ALU.subtract, ALU.mult)
                st.then_inc(S["ca_xn"], 1)
                for g in (4, 5):
                    v_out(n, 0, g)

            def pair_body(b, pair, n, par, ahead, tail):
                for i in range(T):
                    for h in range(2):
                        dve.wait_ge(S["ca_s"], UNITS * n + 2 * i + h + 1)
                        v.tensor_reduce(ca_nmax[:, par, i, h:h + 1], (ps_qk, ps_s)[h][:, 0:(i + 1) * P],
                                        AX.X, ALU.max, negate=True).then_inc(S["ca_max"], 1)
                        if i:
                            evacuate(n, i - 1, h)
                        elif tail:
                            evacuate(n - 1, T - 1, h)
                        if i == 7 and h == 0 and ahead:
                            v_out(n + 1, 1 - par, 4)
                    if i == 0 and tail:
                        invert(n - 1, 1 - par, 1)
                    if i == 1 and tail:
                        z_out(n - 1, 1)
                    if i == 2 and tail:
                        x_add(b, n - 1, 1)
                    if i == 4:
                        invert(n, par, 0)
                    if i == 5:
                        z_out(n, 0)
                    if i == 6:
                        x_add(b, n, 0)
                    if i == 7 and ahead:
                        v_out(n + 1, 1 - par, 5)

            def flush(b, n):
                for h in range(2):
                    evacuate(n - 1, T - 1, h)
                invert(n - 1, 1, 1)
                z_out(n - 1, 1)
                x_add(b, n - 1, 1)

            causal(dve, start, pair_body, flush)

        def pool_causal(pool):
            g = nc.gpsimd

            def start(b, n):
                pool.wait_ge(S["ca_aggr"], b + 1)
                g.tensor_tensor(veps[:, :], mv[:, :, 1], eps_t[:, :], ALU.add).then_inc(S["ca_veps"], 1)
                pool.wait_ge(S["ca_veps"], b + 1)
                g.tensor_tensor(rstd[:, :], veps[:, :], minus_half[:, 0:T], ALU.pow).then_inc(S["ca_rstd"], 1)

            with pool.Fori(0, B) as b:
                start(b, APAIRS * b)

        def sp_stack(sp, p):
            def body(i, a, b_, c, more):
                step = NT * p + i
                mC = step - 2
                if a:
                    if isinstance(i, int) and i == 0:
                        sp.wait_ge(S["ln_out"], T * (p + 1))
                    wait(sp, S["a_turned"], step)
                    sp.dma_start(a_in[:, :, :], y[:, :, i, :]).then_inc(S["a_copied"], 16)
                if c:
                    lay = (i - 2) // T
                    lay = lay if isinstance(lay, int) else sp.snap(lay)
                    wait(sp, S["gv_made"], mC * HC)
                    sp.dma_start(w1_cur[:, :], w1[bass.ds(lay, 1), :, :].rearrange("l k n -> k (l n)"))\
                      .then_inc(S["w1_copied"], 16)

            stack(sp, body)

        def sp_causal(sp):
            def start(b, n):
                sp.wait_ge(S["ca_exp"], 1 + UNITS * n)
                sp.wait_ge(S["ca_z_ready"], 1 + 2 * n)
                sp.wait_ge(S["ca_proj"], 1 + 6 * n)
                sp.dma_start(m_cur[:, 0, :, :], m_sb[:, 0:2, :]).then_inc(S["m_copied"], 16)

            def pair_body(b, pair, n, par, ahead, tail):
                if ahead:
                    sp.wait_ge(S["ca_proj"], 1 + 6 * n + 1)
                    sp.dma_start(m_cur[:, 1 - par, :, :], m_sb[:, bass.ds(2 * pair + 2, 2), :])\
                      .then_inc(S["m_copied"], 16)

            causal(sp, start, pair_body, lambda b, n: None)

        block = ctx.enter_context(nc.Block())

        @block.sync
        def _(sp):
            sp.dma_start(x[:, :, :, :], x_in.rearrange("b (t p) d -> p b t d", p=P)).then_inc(x_loaded, 16)
            for dst, src in ((ident[:, :], identity), (wqkv_sb[:, :, :], wqkv.rearrange("l k n -> k l n")),
                             (wo_sb[:, :, :, :], wo.rearrange("l (j k) n -> k l j n", k=P)),
                             (g_col[:, :], ln_g), (b_col[:, :], ln_b), (b1_col[:, :, :, :], b1),
                             (b2_row[:, :, :], b2), (bout_row[:, :], b_out), (scale_row[:, :, :, :], qk_scale),
                             (notfirst[:, :], not_first), (probs[:, 0, 0:2, :], local_mask),
                             (probs[:, 1, 0, :], causal_mask)):
                sp.dma_start(dst, src).then_inc(const_loaded, 16)
            for j in range(HC):
                sp.dma_start(w2_sb[0:HROWS[j], :, j, :],
                             w2[:, P * j:P * j + HROWS[j], :].rearrange("l k n -> k l n")).then_inc(const_loaded, 16)
            for lay in range(DEPTH):
                for table, base in ((cos_t, rot_cos), (sin_t, rot_sin)):
                    sp.dma_start(table[:, lay * T:lay * T + T, :, :],
                                 base.rearrange("(t p) c d -> p t c d", p=P)).then_inc(const_loaded, 16)
            sp_stack(sp, 0)
            sp.wait_ge(stack_done, 1)
            for dst, src in ((wq_sb[:, :, :], wq_t), (wk_sb[:, :, :], wk_t), (wv_sb[:, :], wv),
                             (wout_sb[:, :, :], w_out)):
                sp.dma_start(dst, src).then_inc(heads_loaded, 16)
            sp_causal(sp)
            sp_stack(sp, 1)
            sp.wait_ge(stack_done, 2)
            sp.dma_start(out.rearrange("b (t p) d -> p b t d", p=P), x[:, :, :, :]).then_inc(stored, 16)
            sp.wait_ge(stored, 16)

        CONSTS = 16 * (12 + HC + 2 * DEPTH)

        @block.tensor
        def _(pe):
            pe.wait_ge(tables_ready, 1)
            pe_stack(pe, 0)
            pe_causal(pe)
            pe_stack(pe, 1)

        @block.scalar
        def _(act):
            act.wait_ge(tables_ready, 1)
            act.wait_ge(q_zeroed, 2)
            act_stack(act, 0)
            act_causal(act)
            act.wait_ge(q_zeroed, 4)
            act_stack(act, 1)

        @block.vector
        def _(dve):
            v = nc.vector
            dve.wait_ge(const_loaded, CONSTS)
            v.tensor_copy(ident_bf[:, :], ident[:, :])
            v.tensor_copy(cmask[:, :], probs[:, 1, 0, :])
            masks = lmask[:, :, :].rearrange("p (l t) k -> p l t k", l=DEPTH)
            for lay in range(DEPTH):
                v.tensor_copy(masks[:, lay, 0, :], probs[:, 0, 0, :])
                v.tensor_copy(masks[:, lay, 1:T, :],
                              probs[:, 0, 1, :].unsqueeze(1).broadcast_to([P, T - 1, P]))
                half = DH // 2
                tiles = slice(lay * T, lay * T + T)
                v.tensor_tensor(cos_t[:, tiles, :, :], cos_t[:, tiles, :, :],
                                scale_row[:, lay, :, :].unsqueeze(1).broadcast_to([P, T, 2, DH]), ALU.mult)
                for lo, hi in ((0, half), (half, 0)):
                    last = v.tensor_tensor(sin_t[:, tiles, :, lo:lo + half], sin_t[:, tiles, :, lo:lo + half],
                                           scale_row[:, lay, :, hi:hi + half].unsqueeze(1)
                                           .broadcast_to([P, T, 2, half]), ALU.mult)
            last.then_inc(tables_ready, 1)
            dve.wait_ge(tables_ready, 1)
            dve.wait_ge(x_loaded, 16)
            for p in range(2):
                dve_enter(dve, p)
                dve_stack(dve, p)
                dve.wait_ge(S["y2_done"], NT * (p + 1))
                v.scalar_tensor_tensor(x[:, :, :, :], y[:, :, NT:NT + T, :], 0.5, x[:, :, :, :],
                                       ALU.mult, ALU.add).then_inc(stack_done, 1)
                dve.wait_ge(stack_done, p + 1)
                if p == 0:
                    dve_causal(dve)
                    dve.wait_ge(S["ca_x_added"], 1 + 2 * APAIRS * B)

        @block.gpsimd
        def _(pool):
            g = nc.gpsimd
            g.memset(minus_half[:, :], -0.5)
            g.memset(eps_t[:, :], LN_EPS).then_inc(powers_ready, 1)
            pool.wait_ge(powers_ready, 1)
            pool.wait_ge(tables_ready, 1)
            for p in range(2):
                if p == 1:
                    pool.wait_ge(S["ca_x_added"], 1 + 2 * APAIRS * B)
                g.memset(q_t[0:W, :, 1:HEADS:2, :], 0.0).then_inc(q_zeroed, 1)
                pool.wait_ge(q_zeroed, 2 * p + 1)
                g.memset(q_t[W:P, :, 0:HEADS:2, :], 0.0).then_inc(q_zeroed, 1)
                pool.wait_ge(q_zeroed, 2 * p + 2)
                pool_enter(pool, p)
                pool_stack(pool, p)
                if p == 0:
                    pool.wait_ge(stack_done, 1)
                    pool_causal(pool)


def kernel(L0_attn_resid, L0_attn_W_Q, L0_attn_W_K, L0_attn_W_V, L0_attn_W_out, L0_attn_b_out,
           L0_ffn_wqkv, L0_ffn_q_scale, L0_ffn_k_scale, L0_ffn_wo, L0_ffn_ln_g, L0_ffn_ln_b,
           L0_ffn_w1, L0_ffn_b1, L0_ffn_w2, L0_ffn_b2):
    import numpy as np
    import concourse.bacc as bacc
    from concourse import mybir as mb
    from concourse.bass_utils import run_bass_kernel_spmd

    f = np.float32
    batches, tokens, dim = L0_attn_resid.shape
    depth, inner3 = L0_ffn_wqkv.shape[0], L0_ffn_wqkv.shape[2]
    dh = L0_ffn_q_scale.shape[1]
    hid = L0_ffn_w2.shape[1]
    heads, adh = L0_attn_W_Q.shape[1:]

    half_idx = np.arange(0, dh, 2, dtype=f)
    inv_freq = (f(1.0) / f(10000.0) ** (half_idx / f(dh))).astype(f)
    t = np.arange(tokens, dtype=f)
    freqs = t[:, None] * inv_freq[None, :]
    power = (t - f(tokens // 2)) / f(dh // 2)
    xpos = ((half_idx + f(0.4 * dh)) / f(1.4 * dh))[None, :].astype(f) ** power[:, None]
    cos, sin = np.cos(freqs), np.sin(freqs)
    pair = lambda a, b: np.concatenate([a, b], axis=1)
    rot_cos = np.stack([8 * pair(cos * xpos, cos * xpos), pair(cos / xpos, cos / xpos)], 1).astype(f)
    rot_sin = np.stack([8 * pair(-sin * xpos, sin * xpos), pair(-sin / xpos, sin / xpos)], 1).astype(f)

    w = dim // 2
    i, j = np.arange(w)[:, None], np.arange(w)[None, :]
    own, before = np.where(j <= i, 0.0, MASKED), np.where(j >= i, 0.0, MASKED)
    nothing = np.full((w, w), MASKED)
    second = np.concatenate([before, own], axis=1)
    masks = np.stack([np.concatenate([np.concatenate([own, nothing], 1), second], 0),
                      np.concatenate([np.concatenate([own, before], 1), second], 0)], 1).astype(f)
    i, j = np.arange(dim)[:, None], np.arange(dim)[None, :]
    not_first = np.ones((dim, depth, tokens // dim), f)
    not_first[:, :, 0] = 0.0

    rows = lambda a: np.broadcast_to(a, (dim, *a.shape))
    b1 = np.zeros((depth, 2, -(-hid // dim) * dim), f)
    b1[:, :, :hid] = np.asarray(L0_ffn_b1).reshape(depth, 2, hid)
    arrays = {
        "x_in": L0_attn_resid,
        "wq_t": np.transpose(L0_attn_W_Q, (2, 1, 0)),
        "wk_t": np.transpose(L0_attn_W_K, (2, 1, 0)),
        "wv": np.reshape(L0_attn_W_V, (dim, heads * adh)),
        "w_out": np.transpose(L0_attn_W_out, (1, 0, 2)).reshape(heads * adh // dim, dim, dim).transpose(1, 0, 2),
        "b_out": rows(np.asarray(L0_attn_b_out)),
        "wqkv": L0_ffn_wqkv,
        "qk_scale": rows(np.stack([L0_ffn_q_scale, L0_ffn_k_scale], 1)),
        "wo": L0_ffn_wo,
        "ln_g": np.transpose(L0_ffn_ln_g), "ln_b": np.transpose(L0_ffn_ln_b),
        "w1": L0_ffn_w1,
        "b1": b1.reshape(depth, 2, -1, dim).transpose(3, 0, 1, 2),
        "w2": L0_ffn_w2, "b2": rows(np.asarray(L0_ffn_b2)),
        "rot_cos": rot_cos, "rot_sin": rot_sin,
        "local_mask": masks, "not_first": not_first.reshape(dim, -1),
        "causal_mask": np.where(j <= i, 0.0, MASKED).astype(f),
        "identity": np.eye(dim, dtype=f),
    }
    arrays = {k: np.ascontiguousarray(a) for k, a in arrays.items()}
    nc = bacc.Bacc("TRN2", target_bir_lowering=False, num_devices=1)
    args = [nc.dram_tensor(f"in_{k}", a.shape, mb.dt.from_np(a.dtype), kind="ExternalInput").ap()
            for k, a in arrays.items()]
    result = nc.dram_tensor("result", (batches, tokens, dim), mb.dt.float32, kind="ExternalOutput").ap()
    build_program(nc, *args, result)
    r = run_bass_kernel_spmd(nc, [{f"in_{k}": a for k, a in arrays.items()}], core_ids=[0])
    return r.results[0]["result"]
```

```python
from contextlib import ExitStack

import concourse.bass as bass
from concourse import mybir

F32 = mybir.dt.float32
BF16 = mybir.dt.bfloat16
ACT = mybir.ActivationFunctionType
ALU = mybir.AluOpType
AX = mybir.AxisListType

P = 128
BANK = 512
GROUP = BANK // P
LN_EPS = 1e-5
NORM_FLOOR = 1e-24
MASKED = -1e30


def build_program(nc, x_in, wq_t, wk_t, wv, w_out, b_out, wqkv, qk_scale, wo, ln_g, ln_b,
                  w1, b1, w2, b2, rot_cos, rot_sin, local_mask, not_first, causal_mask, identity,
                  out):
    B, TOKENS, DIM = x_in.shape
    T = TOKENS // P
    DEPTH, _, INNER3 = wqkv.shape
    INNER = INNER3 // 3
    DH = qk_scale.shape[3]
    HEADS = INNER // DH
    PAIRS = HEADS // 2
    HID = w2.shape[1]
    HC = (HID + P - 1) // P
    HROWS = [min(P, HID - P * j) for j in range(HC)]
    NT = DEPTH * T
    W = P // 2
    AH = wq_t.shape[1]
    ADH = wq_t.shape[0]
    APAIRS = AH // 2
    CAUSAL_SCALE = float(ADH) ** -0.5
    assert DIM == P and DH == W and ADH == W and B * P == BANK and INNER == BANK

    with ExitStack() as ctx:
        def sb(name, shape, dt=F32, at=ctx):
            return at.enter_context(nc.sbuf_tensor(name, shape, dt))

        def sem(name):
            return ctx.enter_context(nc.semaphore(name))

        x = sb("x", [P, B, T, P])
        ident = sb("ident", [P, P])
        ident_bf = sb("ident_bf", [P, P], BF16)
        wqkv_sb = sb("wqkv_sb", [P, DEPTH, 3 * INNER])
        wo_sb = sb("wo_sb", [P, DEPTH, PAIRS, P])
        w2_sb = sb("w2_sb", [P, DEPTH, HC, P])
        g_col = sb("g_col", [P, DEPTH])
        b_col = sb("b_col", [P, DEPTH])
        b1_col = sb("b1_col", [P, DEPTH, 2, HC])
        b2_row = sb("b2_row", [P, DEPTH, P])
        bout_row = sb("bout_row", [P, P])
        scale_row = sb("scale_row", [P, DEPTH, 2, DH])
        cos_t = sb("cos_t", [P, NT, 2, DH])
        sin_t = sb("sin_t", [P, NT, 2, DH])
        lmask = sb("lmask", [P, NT, P], BF16)
        notfirst = sb("notfirst", [P, 2, NT])
        cmask = sb("cmask", [P, P], BF16)
        minus_half = sb("minus_half", [P, 2 * HEADS])
        eps_t = sb("eps_t", [P, T])
        spare = sb("spare", [P, 1])
        warm = sb("warm", [P, 2])
        stats = sb("stats", [P, T, 6])
        mv = sb("mv", [P, T, 2])
        veps = sb("veps", [P, T])
        rstd = sb("rstd", [P, T])

        local = ExitStack()
        y = sb("y", [P, B, NT + T, P], at=local)
        a_in = sb("a_in", [P, B, P], at=local)
        h_t = sb("h_t", [P, B, P], at=local)
        h_last = sb("h_last", [P, P], at=local)
        sq = sb("sq", [P, 2, HEADS, DH], at=local)
        qn = sb("qn", [P, 2, HEADS, DH], at=local)
        qkr = sb("qkr", [P, 2, HEADS, DH], at=local)
        ss = sb("ss", [P, 2 * HEADS], at=local)
        rn = sb("rn", [P, 2 * HEADS], at=local)
        q_t = sb("q_t", [P, B, HEADS, P], at=local)
        k_t = sb("k_t", [P, B, PAIRS, 3, W], at=local)
        v_cur = sb("v_cur", [P, B, INNER], at=local)
        v_mix = sb("v_mix", [P, B, INNER], at=local)
        probs = sb("probs", [P, 2, HEADS, P], at=local)
        probs_t = sb("probs_t", [P, HEADS, P], at=local)
        nmax = sb("nmax", [P, 2, HEADS], at=local)
        rsum = sb("rsum", [P, 2, HEADS], at=local)
        rinv = sb("rinv", [P, 2, HEADS], at=local)
        z_t = sb("z_t", [P, PAIRS, P], at=local)
        y1 = sb("y1", [P, B, P], at=local)
        h2 = sb("h2", [P, B, P], at=local)
        carry = sb("carry", [1, B, W], at=local)
        hn = sb("hn", [P, B, P], at=local)
        hn_t = sb("hn_t", [P, B, P], at=local)
        w1_cur = sb("w1_cur", [P, 2 * HID], at=local)
        u_t = sb("u_t", [P, HC, B * P], at=local)
        local.close()

        causal = ExitStack()
        wq_sb = sb("wq_sb", [ADH, AH, P], at=causal)
        wk_sb = sb("wk_sb", [ADH, AH, P], at=causal)
        m_sb = sb("m_sb", [P, AH, P], at=causal)
        m_cur = sb("m_cur", [P, 2, 2, P], at=causal)
        wv_sb = sb("wv_sb", [P, AH * ADH], at=causal)
        wout_sb = sb("wout_sb", [P, APAIRS, P], at=causal)
        xn = sb("xn", [P, T, P], at=causal)
        xn_t = sb("xn_t", [P, T * P], at=causal)
        qm = sb("qm", [P, 2, 2, T * P], at=causal)
        va = sb("va", [P, 2, T, P], at=causal)
        ca_p = sb("ca_p", [P, 2, 2, T * P], at=causal)
        ca_pt = sb("ca_pt", [P, 2, 2, T, P], at=causal)
        ca_nmax = sb("ca_nmax", [P, 2, T, 2], at=causal)
        ca_rsum = sb("ca_rsum", [P, 2, T, 2], at=causal)
        ca_inv = sb("ca_inv", [P, T // 2, 2], at=causal)
        ca_rinv = sb("ca_rinv", [P, T // 2, 2, ADH], at=causal)
        ca_rt = sb("ca_rt", [P, BANK], at=causal)
        ca_z = sb("ca_z", [P, BANK], at=causal)
        causal.close()

        def bank(name, n=1):
            return ctx.enter_context(nc.psum_tensor(name, [P, n * BANK], F32))

        ps_qk = bank("ps_qk", 2)
        ps_v = bank("ps_v")
        ps_t = bank("ps_t")
        ps_s = bank("ps_s", 2)
        ps_w = bank("ps_w")
        ps_z = bank("ps_z")

        x0_loaded, x_loaded = sem("x0_loaded"), sem("x_loaded")
        first_loaded, const_loaded = sem("first_loaded"), sem("const_loaded")
        heads_loaded = sem("heads_loaded")
        stored = sem("stored")
        tables_ready, masks_ready, powers_ready = sem("tables_ready"), sem("masks_ready"), sem("powers_ready")
        q_zeroed = sem("q_zeroed")
        stack_done = sem("stack_done")
        causal_done = sem("causal_done")
        names = """ln_stats ln_aggr ln_veps ln_rstd ln_out
            a_copied a_turned h_saved h_ready qk_made v_made squared summed clamped normed_r qk_normed
            rot_sin_done rot_cos_done rotated q_turned k_turned q_ready k_kept k_ready v_kept v_ready
            s_made max_ready exp_done rinv_ready p_ready p_turned pt_lo pt_hi z_made z_ready o_made
            y1_ready first_row h2_copied carry_copied c_stats c_agg c_eps c_rstd hn_ready t3_made
            hn_t_ready w1_copied gv_made gelu_done u_done w2_made bias_added y2_done
            m_made ca_stats ca_aggr ca_veps ca_rstd ca_xn ca_bias ca_turned ca_xn_t m_copied
            ca_proj ca_q_ready ca_v_ready ca_s ca_max ca_exp ca_pt ca_pt_dve ca_pt_act ca_pv
            ca_inverted ca_rinv_ready ca_r_made ca_rt_ready ca_z_ready ca_o ca_x_added""".split()
        S = {n: sem(n) for n in names}

        def wait(eng, s, n):
            if not isinstance(n, int) or n > 0:
                eng.wait_ge(s, n)

        FIRST = 16 * 6
        CONSTS = 16 * (8 + 2 * (DEPTH - 1) + DEPTH - 1 + HC)

        def live(i, lag):
            return not isinstance(i, int) or lag <= i < NT + lag

        def stack(eng, body):
            for i in range(4):
                body(i, True)
            with eng.Fori(4, NT - 1) as i:
                body(i, True)
            for i in range(NT - 1, NT + 3):
                body(i, False)

        def wide_banks(j):
            return ((ps_s[:, 0:BANK], ps_s[:, BANK:2 * BANK]), (ps_w, ps_z), (ps_v, ps_t))[j]

        def pe_stack(pe, p):
            def turn_tile(i):
                pe.wait_ge(S["a_copied"], 48 * (NT * p + i + 1))
                for b in range(B):
                    mm = pe.transpose(ps_v[:, P * b:P * b + P], a_in[:, b, :], ident[:])
                mm.then_inc(S["a_turned"], 1)

            def body(i, more):
                step = NT * p + i
                if isinstance(i, int) and i == 1 and p == 0:
                    pe.wait_ge(const_loaded, CONSTS)
                    pe.wait_ge(masks_ready, 1)
                nA, nB, mC, mD = step * B, (step - 1) * B, step - 2, step - 3

                def project_qk(k):
                    if k == 0:
                        pe.wait_ge(S["h_ready"], step + 1)
                    wait(pe, S["qk_normed"], nA + k)
                    for c_ in range(2):
                        mm = pe.matmul(ps_qk[:, INNER * c_:INNER * c_ + INNER], h_t[:, k, :],
                                       wqkv_sb[:, i // T, INNER * c_:INNER * c_ + INNER],
                                       start=True, stop=True)
                    mm.then_inc(S["qk_made"], 1)

                def scores(k):
                    pe.wait_ge(S["q_ready"], nB + k + 1)
                    pe.wait_ge(S["k_ready"], nB + k + 1)
                    wait(pe, S["exp_done"], nB + k)
                    if k == B - 1 and live(i, 2):
                        pe.wait_ge(S["u_done"], mC * HC + 1)
                    for g in range(HEADS // GROUP):
                        pe.matmul(ps_s[:, BANK * g:BANK * g + BANK], ident_bf[:],
                                  lmask[:, i - 1, :].unsqueeze(1).broadcast_to([P, GROUP, P]),
                                  start=True, stop=False, skip_group_check=True)
                    for h in range(HEADS):
                        keys = k_t[:, k, h // 2, :, :]
                        for w in range(2):
                            mm = pe.matmul(ps_s[W * w:W * w + W, P * h:P * h + P],
                                           q_t[:, k, h, W * w:W * w + W],
                                           keys[:, 0:2, :] if w else keys[:, 0:3:2, :],
                                           start=False, stop=True, skip_group_check=True)
                    mm.then_inc(S["s_made"], 1)

                def turn_probs(k, ia, ib):
                    pe.wait_ge(S["p_ready"], ib + 1)
                    wait(pe, S["y1_ready"], ib)
                    if k == 0 and live(i, 3):
                        pe.wait_ge(S["y2_done"], mD + 1)
                    for h in range(HEADS):
                        if h == GROUP and k == 0 and live(i, 1):
                            pe.wait_ge(S["k_ready"], ia + 1)
                        elif h == GROUP and k and live(i, 0):
                            wait(pe, S["k_ready"], ia)
                        dst = (ps_w, ps_z)[h // GROUP]
                        mm = pe.transpose(dst[:, P * (h % GROUP):P * (h % GROUP) + P],
                                          probs[:, (k - 1) % 2, h, :], ident[:])
                    mm.then_inc(S["p_turned"], 1)

                def values(k, ib):
                    b = (k - 1) % B
                    pe.wait_ge(S["v_ready"], ib + 1)
                    for h in range(HEADS):
                        if h % GROUP == 0:
                            pe.wait_ge(S["pt_hi" if h else "pt_lo"], ib + 1)
                        r = W * (h % 2)
                        for w in range(2):
                            v = (v_mix, v_cur)[w]
                            mm = pe.matmul(ps_w[r:r + W, P * (h // 2) + W * w:P * (h // 2) + W * w + W],
                                           v[:, b, DH * h:DH * h + DH], probs_t[:, h, W * w:W * w + W],
                                           start=True, stop=True, skip_group_check=True)
                    mm.then_inc(S["z_made"], 1)

                def project_v(k, ia):
                    wait(pe, S["v_ready"], ia)
                    if k:
                        left, tile = h_t[:, k - 1, :], i
                    else:
                        pe.wait_ge(S["h_saved"], step)
                        left, tile = h_last[:, :], i - 1
                    pe.matmul(ps_v[:, :], left, wqkv_sb[:, tile // T, 2 * INNER:3 * INNER],
                              start=True, stop=True).then_inc(S["v_made"], 1)

                def turn_qk(ia):
                    pe.wait_ge(S["rotated"], ia + 1)
                    for c_, dst, free, done in ((0, ps_t, "q_ready", "q_turned"),
                                                (1, ps_z, "k_ready", "k_turned")):
                        wait(pe, S[free], ia)
                        for j in range(PAIRS):
                            mm = pe.transpose(dst[:, P * j:P * j + P],
                                              qkr[:, c_, 2 * j:2 * j + 2, :], ident[:])
                        mm.then_inc(S[done], 1)

                def project_out(k, ib):
                    tile = i - 1 if k else i - 2
                    pe.wait_ge(S["z_ready"], ib + 1)
                    for j in range(PAIRS):
                        mm = pe.matmul(ps_w[:, 0:P], z_t[:, j, :], wo_sb[:, tile // T, j, :],
                                       start=(j == 0), stop=(j == PAIRS - 1))
                    mm.then_inc(S["o_made"], 1)

                def turn_hidden():
                    pe.wait_ge(S["hn_ready"], mC + 1)
                    if live(i, 1):
                        pe.wait_ge(S["exp_done"], nB + B - 1)
                    for b in range(B):
                        mm = pe.transpose(ps_s[:, P * b:P * b + P], hn[:, b, :], ident[:])
                    mm.then_inc(S["t3_made"], 1)

                def widen(j):
                    if j == 0:
                        pe.wait_ge(S["hn_t_ready"], mC + 1)
                        pe.wait_ge(S["w1_copied"], 16 * mC + 16)
                    if j == 1:
                        if live(i, 1):
                            pe.wait_ge(S["y1_ready"], nB + B - 1)
                        if live(i, 0):
                            pe.wait_ge(S["k_ready"], nA + B - 1)
                    if j == 2:
                        if more:
                            pe.wait_ge(S["h_ready"], step + 2)
                        if live(i, 0):
                            pe.wait_ge(S["v_ready"], nA + B - 1)
                            pe.wait_ge(S["q_ready"], nA + B - 1)
                    for c_, dst in enumerate(wide_banks(j)):
                        mm = pe.matmul(dst[0:HROWS[j], :],
                                       w1_cur[:, HID * c_ + P * j:HID * c_ + P * j + HROWS[j]],
                                       hn_t[:, :, :], start=True, stop=True)
                    mm.then_inc(S["gv_made"], 1)

                def narrow():
                    pe.wait_ge(S["u_done"], (mD + 1) * HC)
                    for b in range(B):
                        for j in range(HC):
                            mm = pe.matmul(ps_w[:, P * b:P * b + P], u_t[0:HROWS[j], j, P * b:P * b + P],
                                           w2_sb[0:HROWS[j], (i - 3) // T, j, :],
                                           start=(j == 0), stop=(j == HC - 1))
                    mm.then_inc(S["w2_made"], 1)

                if isinstance(i, int) and i == 0:
                    turn_tile(0)
                for k in range(B):
                    ia, ib = nA + k - 1, nB + k - 1
                    late_a, late_b = live(i, 0 if k else 1), live(i, 1 if k else 2)
                    if k == B - 1 and live(i, 2):
                        turn_hidden()
                    if live(i, 0):
                        project_qk(k)
                    if k == 0:
                        if live(i, 3):
                            narrow()
                        if late_a:
                            project_v(k, ia)
                            turn_qk(ia)
                    if k < B - 1 and live(i, 1):
                        scores(k)
                    if k == B - 1 and live(i, 2):
                        widen(0)
                    if late_b:
                        turn_probs(k, ia, ib)
                    if k and late_a:
                        project_v(k, ia)
                    if late_b:
                        values(k, ib)
                    if k and late_a:
                        turn_qk(ia)
                    if late_b:
                        project_out(k, ib)
                if more:
                    pe.wait_ge(S["v_ready"], nA + B - 1)
                    turn_tile(i + 1)
                if live(i, 2):
                    widen(1)
                    widen(2)
                if live(i, 1):
                    scores(B - 1)

            stack(pe, body)

        def act_stack(act, p):
            sc = nc.scalar

            def place_tile(i):
                act.wait_ge(S["a_turned"], NT * p + i + 1)
                src = ps_v[:, :].rearrange("p (b t) -> p b t", b=B)
                sc.copy(h_t[:, :, 1:P], src[:, :, 1:P])
                sc.activation(h_t[:, :, 0], src[:, :, 0], ACT.Copy, scale=notfirst[:, 0, bass.ds(i, 1)])\
                  .then_inc(S["h_ready"], 1)

            def body(i, more):
                step = NT * p + i
                nA, nB, mC = step * B, (step - 1) * B, step - 2

                def square(k):
                    act.wait_ge(S["qk_made"], nA + k + 1)
                    wait(act, S["summed"], nA + k)
                    sc.activation(sq[:, :, :, :], ps_qk[:, :], ACT.Square).then_inc(S["squared"], 1)

                def exponentials(k, h0, h1):
                    act.wait_ge(S["max_ready"], nB + k + 1)
                    for h in range(h0, h1):
                        e = sc.activation(probs[:, k % 2, h, :], ps_s[:, P * h:P * h + P], ACT.Exp,
                                          bias=nmax[:, k % 2, h:h + 1],
                                          accum_out=rsum[:, k % 2, h:h + 1])
                    if h1 == HEADS:
                        e.then_inc(S["exp_done"], 1)

                def p_out(ib):
                    act.wait_ge(S["p_turned"], ib + 1)
                    sc.copy(probs_t[:, GROUP:HEADS, :], ps_z[:, :]).then_inc(S["pt_hi"], 1)

                def z_out(ib):
                    act.wait_ge(S["z_made"], ib + 1)
                    sc.copy(z_t[:, :, :], ps_w[:, :]).then_inc(S["z_ready"], 1)

                def v_out(k, ia):
                    b = (k - 1) % B
                    act.wait_ge(S["v_made"], ia + 1)
                    if isinstance(i, int) and (i == 0 or (i == 1 and k == 0)):
                        sc.copy(v_mix[W:P, b, :], ps_v[W:P, :]).then_inc(S["v_kept"], 1)
                    else:
                        sc.copy(v_mix[W:P, b, :], v_cur[W:P, b, :]).then_inc(S["v_kept"], 1)
                    sc.copy(v_mix[0:W, b, :], ps_v[0:W, :])
                    act.wait_ge(S["v_kept"], ia + 1)
                    sc.copy(v_cur[:, b, :], ps_v[:, :]).then_inc(S["v_ready"], 1)

                def k_out(j):
                    b, n = j % B, nA + j
                    act.wait_ge(S["k_turned"], n + 1)
                    src = ps_z[:, :].rearrange("p (j w t) -> p j w t", j=PAIRS, w=2)
                    first = isinstance(i, int) and (i == 0 or (i == 1 and j < 0))
                    sc.copy(k_t[:, b, :, 2, :], src[:, :, 1, :] if first else k_t[:, b, :, 1, :])\
                      .then_inc(S["k_kept"], 1)
                    act.wait_ge(S["k_kept"], n + 1)
                    sc.copy(k_t[:, b, :, 0:2, :], src).then_inc(S["k_ready"], 1)

                def q_out(j):
                    b, n = j % B, nA + j
                    act.wait_ge(S["q_turned"], n + 1)
                    src = ps_t[:, :].rearrange("p (j t) -> p j t", j=PAIRS)
                    sc.copy(q_t[0:W, b, 0:HEADS:2, :], src[0:W])
                    sc.copy(q_t[W:P, b, 1:HEADS:2, :], src[W:P]).then_inc(S["q_ready"], 1)

                def gelu(j):
                    act.wait_ge(S["gv_made"], mC * HC + j + 1)
                    if j == 0:
                        wait(act, S["w2_made"], mC)
                    sc.activation(u_t[0:HROWS[j], j, :], wide_banks(j)[1][0:HROWS[j], :], ACT.Gelu,
                                  bias=b1_col[0:HROWS[j], bass.ds((i - 2) // T, 1), 1, j])\
                      .then_inc(S["gelu_done"], 1)

                if isinstance(i, int) and i == 1 and p == 0:
                    act.wait_ge(const_loaded, CONSTS)
                if isinstance(i, int) and i == 0:
                    place_tile(0)
                for k in range(B):
                    ia, ib = nA + k - 1, nB + k - 1
                    late_a, late_b = live(i, 0 if k else 1), live(i, 1 if k else 2)
                    last = k == B - 1
                    if last and live(i, 2):
                        act.wait_ge(S["t3_made"], mC + 1)
                        lay = (i - 2) // T
                        sc.activation(hn_t[:, :, :], ps_s[:, 0:BANK], ACT.Identity,
                                      scale=g_col[:, bass.ds(lay, 1)], bias=b_col[:, bass.ds(lay, 1)])\
                          .then_inc(S["hn_t_ready"], 1)
                    if live(i, 0):
                        square(k)
                    if last and live(i, 0):
                        wait(act, S["v_made"], nA)
                        sc.copy(h_last[:, :], h_t[:, B - 1, :]).then_inc(S["h_saved"], 1)
                    if last and live(i, 2):
                        sc.activation(warm[:, 0:1], eps_t[:, 0:1], ACT.Gelu)
                        gelu(0)
                    if k == 0 and live(i, 1):
                        k_out(-1)
                        q_out(-1)
                    if k == B - 2 and live(i, 0):
                        k_out(0)
                        q_out(0)
                    if last and live(i, 0):
                        q_out(B - 3)
                    if late_b:
                        p_out(ib)
                    if not last and live(i, 1):
                        exponentials(k, 0, GROUP)
                    if late_b:
                        z_out(ib)
                    if not last and live(i, 1):
                        exponentials(k, GROUP, HEADS)
                    if late_a:
                        v_out(k, ia)
                    if k >= B - 2 and live(i, 0):
                        k_out(k - 1)
                    if last and live(i, 0):
                        q_out(B - 2)
                if more:
                    act.wait_ge(S["h_saved"], step + 1)
                    place_tile(i + 1)
                if live(i, 2):
                    gelu(1)
                    gelu(2)
                if live(i, 1):
                    sc.activation(warm[:, 1:2], eps_t[:, 0:1], ACT.Exp)
                    exponentials(B - 1, 0, HEADS)

            stack(act, body)

        def make_masks(dve):
            v = nc.vector
            dve.wait_ge(const_loaded, CONSTS)
            dve.wait_ge(x_loaded, 16 * B)
            v.tensor_copy(ident_bf[:, :], ident[:, :])
            v.tensor_copy(cmask[:, :], probs[:, 1, 0, :])
            masks = lmask[:, :, :].rearrange("p (l t) k -> p l t k", l=DEPTH)
            for lay in range(DEPTH):
                v.tensor_copy(masks[:, lay, 0, :], probs[:, 0, 0, :])
                last = v.tensor_copy(masks[:, lay, 1:T, :],
                                     probs[:, 0, 1, :].unsqueeze(1).broadcast_to([P, T - 1, P]))
            last.then_inc(masks_ready, 1)

        def scale_tables(dve, lay):
            v = nc.vector
            half, tiles = DH // 2, slice(lay * T, lay * T + T)
            v.tensor_tensor(cos_t[:, tiles, :, :], cos_t[:, tiles, :, :],
                            scale_row[:, lay, :, :].unsqueeze(1).broadcast_to([P, T, 2, DH]), ALU.mult)
            for lo, hi in ((0, half), (half, 0)):
                last = v.tensor_tensor(sin_t[:, tiles, :, lo:lo + half], sin_t[:, tiles, :, lo:lo + half],
                                       scale_row[:, lay, :, hi:hi + half].unsqueeze(1)
                                       .broadcast_to([P, T, 2, half]), ALU.mult)
            last.then_inc(tables_ready, 1)
            dve.wait_ge(tables_ready, lay + 1)

        def dve_stack(dve, p):
            v = nc.vector

            def body(i, more):
                step = NT * p + i
                nA, nB, mC, mD = step * B, (step - 1) * B, step - 2, step - 3

                def sum_squares(k):
                    dve.wait_ge(S["squared"], nA + k + 1)
                    wait(dve, S["normed_r"], nA + k)
                    v.tensor_reduce(ss[:, :], sq[:, :, :, :].rearrange("p c h d -> p (c h) d"),
                                    AX.X, ALU.add).then_inc(S["summed"], 1)
                    dve.wait_ge(S["summed"], nA + k + 1)
                    v.tensor_scalar(ss[:, :], ss[:, :], NORM_FLOOR, None, ALU.max).then_inc(S["clamped"], 1)

                def norm(k):
                    dve.wait_ge(S["normed_r"], nA + k + 1)
                    wait(dve, S["rotated"], nA + k)
                    r = rn[:, :].rearrange("p (c h) -> p c h", c=2).unsqueeze(3)
                    v.tensor_tensor(qn[:, :, :, :], ps_qk[:, :].rearrange("p (c h d) -> p c h d", c=2, h=HEADS),
                                    r.broadcast_to([P, 2, HEADS, DH]), ALU.mult).then_inc(S["qk_normed"], 1)

                def rotate_sin(k):
                    dve.wait_ge(S["qk_normed"], nA + k + 1)
                    wait(dve, S["k_turned"], nA + k)
                    half = DH // 2
                    for lo, hi in ((0, half), (half, 0)):
                        rot = v.tensor_tensor(
                            qkr[:, :, :, lo:lo + half], qn[:, :, :, hi:hi + half],
                            sin_t[:, i, :, lo:lo + half].unsqueeze(2).broadcast_to([P, 2, HEADS, half]),
                            ALU.mult)
                    rot.then_inc(S["rot_sin_done"], 1)

                def rotate_cos(k):
                    dve.wait_ge(S["rot_sin_done"], nA + k + 1)
                    v.tensor_tensor(qn[:, :, :, :], qn[:, :, :, :],
                                    cos_t[:, i, :, :].unsqueeze(2).broadcast_to([P, 2, HEADS, DH]),
                                    ALU.mult).then_inc(S["rot_cos_done"], 1)

                def row_max(k):
                    dve.wait_ge(S["s_made"], nB + k + 1)
                    wait(dve, S["exp_done"], nB + k - 1)
                    v.tensor_reduce(nmax[:, k % 2, :], ps_s[:, :].rearrange("p (h c) -> p h c", h=HEADS),
                                    AX.X, ALU.max, negate=True).then_inc(S["max_ready"], 1)

                def invert(k):
                    dve.wait_ge(S["exp_done"], nB + k + 1)
                    wait(dve, S["p_ready"], nB + k - 1)
                    v.reciprocal(rinv[:, k % 2, :], rsum[:, k % 2, :]).then_inc(S["rinv_ready"], 1)

                def probs_out(ib):
                    dve.wait_ge(S["p_turned"], ib + 1)
                    v.tensor_copy(probs_t[:, 0:GROUP, :], ps_w[:, :]).then_inc(S["pt_lo"], 1)

                def add_attention(k, ib):
                    b, tile = (k - 1) % B, i - 1 if k else i - 2
                    dve.wait_ge(S["o_made"], ib + 1)
                    if k == 1 and live(i, 2):
                        dve.wait_ge(S["bias_added"], mC + 1)
                        dve.wait_ge(S["h2_copied"], 32 * (mC + 1))
                        dve.wait_ge(S["carry_copied"], 16 * (mC + 1))
                    v.tensor_tensor(y1[:, b, :], y[:, b, tile, :], ps_w[:, 0:P],
                                    ALU.add).then_inc(S["y1_ready"], 1)

                def hidden_stats():
                    dve.wait_ge(S["h2_copied"], 32 * (mC + 1))
                    dve.wait_ge(S["first_row"], mC + 1)
                    for b in range(B):
                        st = v.bn_stats(stats[:, b, :], h2[:, b, :])
                    st.then_inc(S["c_stats"], 1)
                    dve.wait_ge(S["c_stats"], mC + 1)
                    v.memset(spare[:, :], 0.0)
                    for b in range(B):
                        st = v.bn_aggr(mv[:, b, :], stats[:, b, :])
                    st.then_inc(S["c_agg"], 1)

                def norm_hidden():
                    dve.wait_ge(S["c_rstd"], mC + 1)
                    for b in range(B):
                        st = v.tensor_scalar(hn[:, b, :], h2[:, b, :], mv[:, b, 0:1],
                                             rstd[:, b:b + 1], ALU.subtract, ALU.mult)
                    st.then_inc(S["hn_ready"], 1)

                def gate(j):
                    dve.wait_ge(S["gelu_done"], mC * HC + j + 1)
                    v.scalar_tensor_tensor(u_t[0:HROWS[j], j, :], wide_banks(j)[0][0:HROWS[j], :],
                                           b1_col[0:HROWS[j], bass.ds((i - 2) // T, 1), 0, j],
                                           u_t[0:HROWS[j], j, :], ALU.add, ALU.mult)\
                     .then_inc(S["u_done"], 1)

                def add_ffn():
                    dve.wait_ge(S["w2_made"], mD + 1)
                    dve.wait_ge(S["bias_added"], mD + 1)
                    v.tensor_tensor(y[:, :, i + T - 3, :], y[:, :, i + T - 3, :],
                                    ps_w[:, :].rearrange("p (b f) -> p b f", b=B),
                                    ALU.add).then_inc(S["y2_done"], 1)

                for k in range(B):
                    ib = nB + k - 1
                    late_b = live(i, 1 if k else 2)
                    last = k == B - 1
                    if k == B - 2 and live(i, 2):
                        hidden_stats()
                    if live(i, 0):
                        sum_squares(k)
                    if k == 0 and live(i, 3):
                        add_ffn()
                    if not last and live(i, 1):
                        row_max(k)
                    if late_b:
                        probs_out(ib)
                    if last and live(i, 2):
                        gate(0)
                    if live(i, 0):
                        norm(k)
                    if k == B - 2 and live(i, 2):
                        norm_hidden()
                    if last and late_b:
                        add_attention(k, ib)
                    if live(i, 0):
                        rotate_sin(k)
                    if not last and live(i, 1):
                        invert(k)
                    if not last and late_b:
                        add_attention(k, ib)
                    if live(i, 0):
                        rotate_cos(k)
                    if isinstance(i, int) and i == 0:
                        if p == 0 and k == 0:
                            make_masks(dve)
                        dve_enter(dve, p, k + 1)
                        if p == 0 and k == B - 1:
                            scale_tables(dve, 1)
                if live(i, 2):
                    gate(1)
                    gate(2)
                if live(i, 1):
                    row_max(B - 1)
                    invert(B - 1)

            stack(dve, body)

        CHUNKS = [(0,)] + [tuple(range(t, min(t + 2, T))) for t in range(1, T, 2)]

        def dve_enter(dve, p, c):
            v = nc.vector
            n, cols = len(CHUNKS) * p + c, [(t, b) for t in CHUNKS[c] for b in range(B)]
            for j, (t, b) in enumerate(cols):
                st = v.bn_stats(stats[:, j, :], x[:, b, t, :])
            st.then_inc(S["ln_stats"], 1)
            dve.wait_ge(S["ln_stats"], n + 1)
            for j in range(len(cols)):
                st = v.bn_aggr(mv[:, j, :], stats[:, j, :])
            st.then_inc(S["ln_aggr"], 1)
            dve.wait_ge(S["ln_rstd"], n + 1)
            for j, (t, b) in enumerate(cols):
                st = v.tensor_scalar(y[:, b, t, :], x[:, b, t, :], mv[:, j, 0:1], rstd[:, j:j + 1],
                                     ALU.subtract, ALU.mult)
            st.then_inc(S["ln_out"], 1)
            dve.wait_ge(S["ln_out"], n + 1)

        def pool_enter(pool, p, c):
            n, m = len(CHUNKS) * p + c, B * len(CHUNKS[c])
            pool.wait_ge(S["ln_aggr"], n + 1)
            nc.gpsimd.tensor_tensor(veps[:, 0:m], mv[:, 0:m, 1], eps_t[:, 0:m], ALU.add)\
              .then_inc(S["ln_veps"], 1)
            pool.wait_ge(S["ln_veps"], n + 1)
            nc.gpsimd.tensor_tensor(rstd[:, 0:m], veps[:, 0:m], minus_half[:, 0:m], ALU.pow)\
              .then_inc(S["ln_rstd"], 1)

        def pool_stack(pool, p):
            g = nc.gpsimd

            def body(i, more):
                step = NT * p + i
                nA, nB, mC = step * B, (step - 1) * B, step - 2

                def power(k):
                    pool.wait_ge(S["clamped"], nA + k + 1)
                    wait(pool, S["qk_normed"], nA + k)
                    g.tensor_tensor(rn[:, :], ss[:, :], minus_half[:, :], ALU.pow)\
                     .then_inc(S["normed_r"], 1)

                def scale_probs(k):
                    pool.wait_ge(S["rinv_ready"], nB + k + 1)
                    g.tensor_tensor(probs[:, k % 2, :, :], probs[:, k % 2, :, :],
                                    rinv[:, k % 2, :].unsqueeze(2).broadcast_to([P, HEADS, P]),
                                    ALU.mult).then_inc(S["p_ready"], 1)

                def add_rotated(k):
                    pool.wait_ge(S["rot_cos_done"], nA + k + 1)
                    g.tensor_tensor(qkr[:, :, :, :], qn[:, :, :, :], qkr[:, :, :, :], ALU.add)\
                     .then_inc(S["rotated"], 1)

                def first_row():
                    pool.wait_ge(S["y1_ready"], (mC + 1) * B)
                    wait(pool, S["carry_copied"], 16 * mC)
                    wait(pool, S["hn_ready"], mC)
                    g.tensor_tensor(h2[0:1, :, W:P], carry[:, :, :],
                                    notfirst[0:1, 1, bass.ds(i - 2, 1)].unsqueeze(2).broadcast_to([1, B, W]),
                                    ALU.mult).then_inc(S["first_row"], 1)

                def add_bias():
                    pool.wait_ge(S["y1_ready"], (mC + 1) * B)
                    g.tensor_tensor(y[:, :, i + T - 2, :], y1[:, :, :],
                                    b2_row[:, bass.ds((i - 2) // T, 1), :].broadcast_to([P, B, P]),
                                    ALU.add).then_inc(S["bias_added"], 1)

                def hidden_rstd():
                    pool.wait_ge(S["c_agg"], mC + 1)
                    g.tensor_tensor(veps[:, 0:B], mv[:, 0:B, 1], eps_t[:, 0:B], ALU.add).then_inc(S["c_eps"], 1)
                    pool.wait_ge(S["c_eps"], mC + 1)
                    g.tensor_tensor(rstd[:, 0:B], veps[:, 0:B], minus_half[:, 0:B], ALU.pow)\
                     .then_inc(S["c_rstd"], 1)

                for k in range(B):
                    if k == B - 2 and live(i, 2):
                        hidden_rstd()
                    if k == 1 and live(i, 2):
                        first_row()
                    if live(i, 0):
                        power(k)
                    if k == 1 and live(i, 2):
                        add_bias()
                    if k < B - 1 and live(i, 1):
                        scale_probs(k)
                    if live(i, 0):
                        add_rotated(k)
                    if isinstance(i, int) and i == 0:
                        pool_enter(pool, p, k + 1)
                if live(i, 1):
                    scale_probs(B - 1)

            stack(pool, body)

        HALF = T // 2
        UNITS = 2 * T
        assert HALF == GROUP and T * P == 2 * BANK

        def groups(i):
            return (i + GROUP) // GROUP

        def groups_before(i, h=0, g=0):
            return sum(2 * groups(m) for m in range(i)) + h * groups(i) + g

        EV = groups_before(T) // 2

        def causal(eng, start, pair_body, flush):
            with eng.Fori(0, B) as b:
                start(b, APAIRS * b)
                pair_body(b, 0, APAIRS * b, 0, True, False)
                with eng.Fori(0, (APAIRS - 2) // 2) as j:
                    pair_body(b, 2 * j + 1, APAIRS * b + 2 * j + 1, 1, True, True)
                    pair_body(b, 2 * j + 2, APAIRS * b + 2 * j + 2, 0, True, True)
                pair_body(b, APAIRS - 1, APAIRS * b + APAIRS - 1, 1, False, True)
                flush(b, APAIRS * b + APAIRS)

        def pe_causal(pe):
            pe.wait_ge(heads_loaded, 16 * 4)
            for h in range(AH):
                dst = (ps_qk, ps_s)[h // (2 * GROUP)]
                c0 = P * (h % (2 * GROUP))
                pe.matmul(dst[:, c0:c0 + P], wq_sb[:, h, :], wk_sb[:, h, :], start=True, stop=True)\
                  .then_inc(S[{0: "ca_r_made", 1: "ca_turned", 2: "ca_proj"}.get(h, "m_made")], 1)

            def scores(n, par, i, h, tail):
                dst = (ps_qk, ps_s)[h]
                if i == 0:
                    pe.wait_ge(S["ca_q_ready"], 4 * n + 4)
                if i or tail:
                    pe.wait_ge(S["ca_exp"], 1 + UNITS * n + 2 * i + h - 1)
                keys = (i + 1) * P
                for c0 in range(0, keys, BANK):
                    c1 = min(keys, c0 + BANK)
                    pe.matmul(dst[:, c0:c1], qm[:, par, h, P * i:P * i + P], xn_t[:, c0:c1],
                              start=True, stop=c1 < keys, skip_group_check=True)
                pe.matmul(dst[:, P * i:P * i + P], ident_bf[:], cmask[:], start=False, stop=True,
                          skip_group_check=True).then_inc(S["ca_s"], 1)

            def turn(n, i, h):
                pe.wait_ge(S["ca_exp"], 1 + UNITS * n + 2 * i + h + 1)
                for g in range(groups(i)):
                    k = groups_before(i, h, g)
                    dst, read = ((ps_v, "ca_pt_dve"), (ps_t, "ca_pt_act"))[k % 2]
                    pe.wait_ge(S[read], 1 + EV * n + k // 2)
                    for kt in range(GROUP * g, min(i + 1, GROUP * g + GROUP)):
                        mm = pe.transpose(dst[:, P * (kt % GROUP):P * (kt % GROUP) + P],
                                          ca_p[:, i % 2, h, P * kt:P * kt + P], ident[:])
                    mm.then_inc(S["ca_pt"], 1)

            def values(n, par, i):
                k = groups_before(i + 1)
                pe.wait_ge(S["ca_pt_dve"], 1 + EV * n + (k + 1) // 2)
                pe.wait_ge(S["ca_pt_act"], 1 + EV * n + k // 2)
                if i == 0:
                    pe.wait_ge(S["ca_v_ready"], 2 * n + 2)
                if i % HALF == 0:
                    pe.wait_ge(S["ca_z_ready"], 1 + 2 * n + i // HALF)
                for kt in range(i + 1):
                    for h in range(2):
                        mm = pe.matmul(ps_z[W * h:W * h + W, P * (i % HALF):P * (i % HALF) + P],
                                       va[:, par, kt, W * h:W * h + W], ca_pt[:, i % 2, h, kt, :],
                                       start=(kt == 0), stop=(kt == i), skip_group_check=True)
                mm.then_inc(S["ca_pv"], 1)

            def spread_inverses(n, half):
                pe.wait_ge(S["ca_rinv_ready"], 2 * n + half + 1)
                for i in range(HALF * half, HALF * half + HALF):
                    mm = pe.transpose(ps_w[:, P * (i % HALF):P * (i % HALF) + P],
                                      ca_rinv[:, i % HALF, :, :], ident[:])
                mm.then_inc(S["ca_r_made"], 1)

            def project_out(n, pair, half):
                pe.wait_ge(S["ca_z_ready"], 1 + 2 * n + half + 1)
                for i in range(HALF):
                    mm = pe.matmul(ps_w[:, P * i:P * i + P], ca_z[:, P * i:P * i + P],
                                   wout_sb[:, pair, :], start=True, stop=True)
                mm.then_inc(S["ca_o"], 1)

            def project(n, pair, par, g):
                if g == 0:
                    pe.wait_ge(S["m_copied"], 16 * n + 16)
                if g < 4:
                    mm = pe.matmul(ps_w[:, :], m_cur[:, par, g // 2, :],
                                   xn_t[:, BANK * (g % 2):BANK * (g % 2) + BANK], start=True, stop=True)
                else:
                    for kt in range(GROUP * (g - 4), GROUP * (g - 3)):
                        mm = pe.matmul(ps_w[:, P * (kt % GROUP):P * (kt % GROUP) + P],
                                       xn_t[:, P * kt:P * kt + P],
                                       wv_sb[:, bass.ds(pair * P, P)], start=True, stop=True)
                mm.then_inc(S["ca_proj"], 1)

            def start(b, n):
                pe.wait_ge(S["ca_exp"], 1 + UNITS * n)
                pe.wait_ge(S["ca_xn"], b + 1)
                for t in range(T):
                    mm = pe.transpose(ps_qk[:, P * t:P * t + P], xn[:, t, :], ident[:])
                mm.then_inc(S["ca_turned"], 1)
                pe.wait_ge(S["ca_xn_t"], b + 1)
                for g in range(6):
                    if g == 0:
                        pe.wait_ge(S["ca_x_added"], 1 + 2 * n)
                    elif g < 5:
                        pe.wait_ge(S["ca_q_ready"], 4 * n + g)
                    else:
                        pe.wait_ge(S["ca_v_ready"], 2 * n + 1)
                    project(n, 0, 0, g)

            def pair_body(b, pair, n, par, ahead, tail):
                for i in range(T):
                    if i == 3 and ahead:
                        pe.wait_ge(S["ca_x_added"] if tail else S["ca_v_ready"], 2 * n + 1 if tail else 2 * n + 2)
                        project(n + 1, pair + 1, 1 - par, 0)
                    if i == 4 and ahead:
                        pe.wait_ge(S["ca_q_ready"], 4 * n + 5)
                        project(n + 1, pair + 1, 1 - par, 1)
                    for h in range(2):
                        scores(n, par, i, h, tail)
                        if i:
                            turn(n, i - 1, h)
                        elif tail:
                            turn(n - 1, T - 1, h)
                        if i == 7 and h == 0 and ahead:
                            pe.wait_ge(S["ca_q_ready"], 4 * n + 8)
                            project(n + 1, pair + 1, 1 - par, 4)
                    if i == 0 and tail:
                        values(n - 1, 1 - par, T - 2)
                    if i == 1 and tail:
                        values(n - 1, 1 - par, T - 1)
                        pe.wait_ge(S["ca_v_ready"], 2 * n + 2)
                        spread_inverses(n - 1, 1)
                    if i == 2 and tail:
                        project_out(n - 1, pair - 1, 1)
                    if i == 6:
                        project_out(n, pair, 0)
                    if i >= 2:
                        values(n, par, i - 2)
                    if i == 4 and ahead:
                        pe.wait_ge(S["ca_q_ready"], 4 * n + 6)
                        project(n + 1, pair + 1, 1 - par, 2)
                    if i == 5:
                        pe.wait_ge(S["ca_q_ready"] if ahead else S["ca_x_added"], 4 * n + 7 if ahead else 2 * n + 1)
                        spread_inverses(n, 0)
                    if i == 6 and ahead:
                        pe.wait_ge(S["ca_x_added"], 1 + 2 * n + 1)
                        project(n + 1, pair + 1, 1 - par, 3)
                    if i == 7 and ahead:
                        pe.wait_ge(S["ca_v_ready"], 2 * n + 3)
                        project(n + 1, pair + 1, 1 - par, 5)

            def flush(b, n):
                for h in range(2):
                    turn(n - 1, T - 1, h)
                values(n - 1, 1, T - 2)
                values(n - 1, 1, T - 1)
                pe.wait_ge(S["ca_x_added"], 1 + 2 * n - 1)
                spread_inverses(n - 1, 1)
                project_out(n - 1, APAIRS - 1, 1)

            causal(pe, start, pair_body, flush)

        def act_causal(act):
            sc = nc.scalar
            act.wait_ge(S["m_made"], AH - 3)
            for h, done in ((0, "ca_pt_act"), (GROUP, "ca_exp")):
                sc.copy(m_sb[:, h:h + GROUP, :], ps_qk[:, P * h:P * h + BANK]).then_inc(S[done], 1)

            def evacuate(n, i, h):
                for g in range(groups(i)):
                    k = groups_before(i, h, g)
                    if k % 2:
                        act.wait_ge(S["ca_pt"], 2 * EV * n + k + 1)
                        k1 = min(i + 1, GROUP * g + GROUP)
                        sc.copy(ca_pt[:, i % 2, h, GROUP * g:k1, :], ps_t[:, 0:P * (k1 - GROUP * g)])\
                          .then_inc(S["ca_pt_act"], 1)

            def q_out(n, par, g):
                act.wait_ge(S["ca_proj"], 1 + 6 * n + g + 1)
                sc.activation(qm[:, par, g // 2, BANK * (g % 2):BANK * (g % 2) + BANK], ps_w[:, :],
                              ACT.Copy, scale=CAUSAL_SCALE).then_inc(S["ca_q_ready"], 1)

            def spread_out(n, half):
                act.wait_ge(S["ca_r_made"], 1 + 2 * n + half + 1)
                sc.copy(ca_rt[:, :], ps_w[:, :]).then_inc(S["ca_rt_ready"], 1)

            def start(b, n):
                act.wait_ge(S["ca_turned"], 1 + b + 1)
                sc.copy(xn_t[:, :], ps_qk[:, :]).then_inc(S["ca_xn_t"], 1)
                for g in range(4):
                    q_out(n, 0, g)

            def pair_body(b, pair, n, par, ahead, tail):
                for i in range(T):
                    for h in range(2):
                        act.wait_ge(S["ca_max"], UNITS * n + 2 * i + h + 1)
                        sc.activation(ca_p[:, i % 2, h, 0:(i + 1) * P], (ps_qk, ps_s)[h][:, 0:(i + 1) * P],
                                      ACT.Exp, bias=ca_nmax[:, par, i, h:h + 1],
                                      accum_out=ca_rsum[:, par, i, h:h + 1]).then_inc(S["ca_exp"], 1)
                        if i == 3 and h == 0 and ahead:
                            q_out(n + 1, 1 - par, 0)
                        if i == 4 and h == 0 and ahead:
                            q_out(n + 1, 1 - par, 1)
                        if i:
                            evacuate(n, i - 1, h)
                        elif tail:
                            evacuate(n - 1, T - 1, h)
                    if i == 1 and tail:
                        spread_out(n - 1, 1)
                    if i == 4 and ahead:
                        q_out(n + 1, 1 - par, 2)
                    if i == 5:
                        spread_out(n, 0)
                    if i == 6 and ahead:
                        q_out(n + 1, 1 - par, 3)

            def flush(b, n):
                for h in range(2):
                    evacuate(n - 1, T - 1, h)
                spread_out(n - 1, 1)

            causal(act, start, pair_body, flush)

        def dve_causal(dve):
            v = nc.vector
            dve.wait_ge(S["m_made"], AH - 3)
            for h, done in ((0, "ca_x_added"), (3, "ca_pt_dve"), (6, "ca_z_ready")):
                h1 = min(h + 3, 2 * GROUP)
                v.tensor_copy(m_sb[:, 2 * GROUP + h:2 * GROUP + h1, :], ps_s[:, P * h:P * h1])\
                 .then_inc(S[done], 1)

            def evacuate(n, i, h):
                for g in range(groups(i)):
                    k = groups_before(i, h, g)
                    if k % 2 == 0:
                        dve.wait_ge(S["ca_pt"], 2 * EV * n + k + 1)
                        k1 = min(i + 1, GROUP * g + GROUP)
                        v.tensor_copy(ca_pt[:, i % 2, h, GROUP * g:k1, :], ps_v[:, 0:P * (k1 - GROUP * g)])\
                         .then_inc(S["ca_pt_dve"], 1)

            def v_out(n, par, g):
                dve.wait_ge(S["ca_proj"], 1 + 6 * n + g + 1)
                v.tensor_copy(va[:, par, GROUP * (g - 4):GROUP * (g - 3), :], ps_w[:, :])\
                 .then_inc(S["ca_v_ready"], 1)

            def invert(n, par, half):
                dve.wait_ge(S["ca_exp"], 1 + UNITS * n + UNITS // 2 * (half + 1))
                wait(dve, S["ca_r_made"], 1 + 2 * n + half)
                v.reciprocal(ca_inv[:, :, :], ca_rsum[:, par, HALF * half:HALF * half + HALF, :])\
                 .then_inc(S["ca_inverted"], 1)
                dve.wait_ge(S["ca_inverted"], 2 * n + half + 1)
                v.tensor_copy(ca_rinv[:, :, :, :], ca_inv[:, :, :].unsqueeze(3).broadcast_to([P, HALF, 2, W]))\
                 .then_inc(S["ca_rinv_ready"], 1)

            def z_out(n, half):
                dve.wait_ge(S["ca_rt_ready"], 2 * n + half + 1)
                dve.wait_ge(S["ca_pv"], T * n + HALF * (half + 1))
                v.tensor_tensor(ca_z[:, :], ps_z[:, :], ca_rt[:, :], ALU.mult).then_inc(S["ca_z_ready"], 1)

            def x_add(b, n, half):
                dve.wait_ge(S["ca_o"], 2 * n + half + 1)
                dve.wait_ge(S["ca_bias"], b + 1)
                dve.wait_ge(S["ca_x_added"], 1 + 2 * n + half)
                tiles = x[:, bass.ds(b, 1), HALF * half:HALF * half + HALF, :]
                v.tensor_tensor(tiles, tiles, ps_w[:, :], ALU.add).then_inc(S["ca_x_added"], 1)

            def start(b, n):
                for t in range(T):
                    st = v.bn_stats(stats[:, t, :], x[:, bass.ds(b, 1), t, :])
                st.then_inc(S["ca_stats"], 1)
                dve.wait_ge(S["ca_stats"], b + 1)
                v.memset(spare[:, :], 0.0)
                for t in range(T):
                    st = v.bn_aggr(mv[:, t, :], stats[:, t, :])
                st.then_inc(S["ca_aggr"], 1)
                dve.wait_ge(S["ca_rstd"], b + 1)
                dve.wait_ge(S["ca_turned"], 1 + b)
                for t in range(T):
                    st = v.tensor_scalar(xn[:, t, :], x[:, bass.ds(b, 1), t, :], mv[:, t, 0:1],
                                         rstd[:, t:t + 1], ALU.subtract, ALU.mult)
                st.then_inc(S["ca_xn"], 1)
                for g in (4, 5):
                    v_out(n, 0, g)

            def pair_body(b, pair, n, par, ahead, tail):
                for i in range(T):
                    for h in range(2):
                        dve.wait_ge(S["ca_s"], UNITS * n + 2 * i + h + 1)
                        v.tensor_reduce(ca_nmax[:, par, i, h:h + 1], (ps_qk, ps_s)[h][:, 0:(i + 1) * P],
                                        AX.X, ALU.max, negate=True).then_inc(S["ca_max"], 1)
                        if i:
                            evacuate(n, i - 1, h)
                        elif tail:
                            evacuate(n - 1, T - 1, h)
                        if i == 7 and h == 0 and ahead:
                            v_out(n + 1, 1 - par, 4)
                    if i == 0 and tail:
                        invert(n - 1, 1 - par, 1)
                    if i == 1 and tail:
                        z_out(n - 1, 1)
                    if i == 2 and tail:
                        x_add(b, n - 1, 1)
                    if i == 4:
                        invert(n, par, 0)
                    if i == 5:
                        z_out(n, 0)
                    if i == 6:
                        x_add(b, n, 0)
                    if i == 7 and ahead:
                        v_out(n + 1, 1 - par, 5)

            def flush(b, n):
                for h in range(2):
                    evacuate(n - 1, T - 1, h)
                invert(n - 1, 1, 1)
                z_out(n - 1, 1)
                x_add(b, n - 1, 1)

            causal(dve, start, pair_body, flush)

        def pool_causal(pool):
            g = nc.gpsimd

            def start(b, n):
                pool.wait_ge(S["ca_aggr"], b + 1)
                g.tensor_tensor(veps[:, :], mv[:, :, 1], eps_t[:, :], ALU.add).then_inc(S["ca_veps"], 1)
                pool.wait_ge(S["ca_veps"], b + 1)
                g.tensor_tensor(rstd[:, :], veps[:, :], minus_half[:, 0:T], ALU.pow).then_inc(S["ca_rstd"], 1)

                pool.wait_ge(S["ca_xn"], b + 1)
                tokens = x[:, bass.ds(b, 1), :, :].rearrange("p b t d -> p (b t) d")
                g.tensor_tensor(tokens, tokens, bout_row[:, :].unsqueeze(1).broadcast_to([P, T, P]),
                                ALU.add).then_inc(S["ca_bias"], 1)

            with pool.Fori(0, B) as b:
                start(b, APAIRS * b)

        tables = [(table[:, lay * T:lay * T + T, :, :], base.rearrange("(t p) c d -> p t c d", p=P))
                  for lay in range(DEPTH) for table, base in ((cos_t, rot_cos), (sin_t, rot_sin))]
        def load_rest(sp):
            for b in range(B):
                sp.dma_start(x[:, b, 1:T, :], x_in[b, P:, :].rearrange("(t p) d -> p t d", p=P))\
                  .then_inc(x_loaded, 16)
            rest = [(probs[:, 0, 0:2, :], local_mask), (probs[:, 1, 0, :], causal_mask),
                    (wo_sb[:, :, :, :], wo.rearrange("l (j k) n -> k l j n", k=P)),
                    (g_col[:, :], ln_g), (b_col[:, :], ln_b), (b1_col[:, :, :, :], b1),
                    (b2_row[:, :, :], b2), (bout_row[:, :], b_out), *tables[2:],
                    *((wqkv_sb[:, lay, :], wqkv[lay, :, :]) for lay in range(1, DEPTH)),
                    *((w2_sb[0:HROWS[j], :, j, :],
                       w2[:, P * j:P * j + HROWS[j], :].rearrange("l k n -> k l n")) for j in range(HC))]
            assert len(rest) * 16 == CONSTS
            for dst, src in rest:
                sp.dma_start(dst, src).then_inc(const_loaded, 16)

        def sp_stack(sp, p):
            def fetch_tile(i):
                step = NT * p + i
                wait(sp, S["a_turned"], step)
                before = i - 1 if not isinstance(i, int) or i else 0
                for dst, src in ((a_in[:, :, 0:W], y[:, :, i, 0:W]),
                                 (a_in[1:P, :, W:P], y[0:P - 1, :, i, W:P]),
                                 (a_in[0:1, :, W:P], y[P - 1:P, :, before, W:P])):
                    sp.dma_start(dst, src).then_inc(S["a_copied"], 16)

            def body(i, more):
                step = NT * p + i
                mC = step - 2
                if isinstance(i, int) and i < 2:
                    sp.wait_ge(S["ln_out"], len(CHUNKS) * p + 1 if i == 0 else len(CHUNKS) * (p + 1))
                if isinstance(i, int) and i == 0:
                    fetch_tile(0)
                    if p == 0:
                        load_rest(sp)
                    sp.wait_ge(S["ln_out"], len(CHUNKS) * p + 2)
                if more:
                    fetch_tile(i + 1)
                if live(i, 2):
                    lay = (i - 2) // T
                    lay = lay if isinstance(lay, int) else sp.snap(lay)
                    wait(sp, S["gv_made"], mC * HC)
                    sp.dma_start(w1_cur[:, :], w1[bass.ds(lay, 1), :, :].rearrange("l k n -> k (l n)"))\
                      .then_inc(S["w1_copied"], 16)
                    sp.wait_ge(S["y1_ready"], (mC + 1) * B)
                    sp.wait_ge(S["first_row"], mC + 1)
                    sp.dma_start(h2[:, :, 0:W], y1[:, :, 0:W]).then_inc(S["h2_copied"], 16)
                    sp.dma_start(h2[1:P, :, W:P], y1[0:P - 1, :, W:P]).then_inc(S["h2_copied"], 16)
                    sp.dma_start(carry[:, :, :], y1[P - 1:P, :, W:P]).then_inc(S["carry_copied"], 16)

            stack(sp, body)

        def sp_causal(sp):
            def start(b, n):
                sp.wait_ge(S["ca_exp"], 1 + UNITS * n)
                sp.wait_ge(S["ca_z_ready"], 1 + 2 * n)
                sp.wait_ge(S["ca_proj"], 1 + 6 * n)
                sp.dma_start(m_cur[:, 0, :, :], m_sb[:, 0:2, :]).then_inc(S["m_copied"], 16)

            def pair_body(b, pair, n, par, ahead, tail):
                if ahead:
                    sp.wait_ge(S["ca_proj"], 1 + 6 * n + 1)
                    sp.dma_start(m_cur[:, 1 - par, :, :], m_sb[:, bass.ds(2 * pair + 2, 2), :])\
                      .then_inc(S["m_copied"], 16)

            causal(sp, start, pair_body, lambda b, n: None)

        block = ctx.enter_context(nc.Block())

        @block.sync
        def _(sp):
            sp.dma_start(x[:, :, 0, :], x_in[:, 0:P, :].rearrange("b p d -> p b d")).then_inc(x0_loaded, 16)
            first = [(ident[:, :], identity), (scale_row[:, :, :, :], qk_scale), *tables[0:2],
                     (notfirst[:, :, :], not_first), (wqkv_sb[:, 0, :], wqkv[0, :, :])]
            assert len(first) * 16 == FIRST
            for dst, src in first:
                sp.dma_start(dst, src).then_inc(first_loaded, 16)
            sp_stack(sp, 0)
            sp.wait_ge(stack_done, 1)
            for dst, src in ((wq_sb[:, :, :], wq_t), (wk_sb[:, :, :], wk_t), (wv_sb[:, :], wv),
                             (wout_sb[:, :, :], w_out)):
                sp.dma_start(dst, src).then_inc(heads_loaded, 16)
            sp_causal(sp)
            sp_stack(sp, 1)
            sp.wait_ge(stack_done, 2)
            sp.wait_ge(S["carry_copied"], 16 * 2 * NT)
            sp.dma_start(out.rearrange("b (t p) d -> p b t d", p=P), x[:, :, :, :]).then_inc(stored, 16)
            sp.wait_ge(stored, 16)

        @block.tensor
        def _(pe):
            pe.wait_ge(first_loaded, FIRST)
            pe_stack(pe, 0)
            pe_causal(pe)
            pe_stack(pe, 1)

        @block.scalar
        def _(act):
            act.wait_ge(first_loaded, FIRST)
            act.wait_ge(powers_ready, 1)
            act.wait_ge(q_zeroed, 2)
            act_stack(act, 0)
            act_causal(act)
            act.wait_ge(q_zeroed, 4)
            act_stack(act, 1)

        @block.vector
        def _(dve):
            v = nc.vector
            dve.wait_ge(x0_loaded, 16)
            dve_enter(dve, 0, 0)
            dve.wait_ge(first_loaded, FIRST)
            scale_tables(dve, 0)
            for p in range(2):
                if p == 1:
                    dve_enter(dve, 1, 0)
                v.memset(carry[:, :, :], 0.0)
                dve_stack(dve, p)
                dve.wait_ge(S["y2_done"], NT * (p + 1))
                v.scalar_tensor_tensor(x[:, :, :, :], y[:, :, NT:NT + T, :], 0.5, x[:, :, :, :],
                                       ALU.mult, ALU.add).then_inc(stack_done, 1)
                dve.wait_ge(stack_done, p + 1)
                if p == 0:
                    dve_causal(dve)
                    dve.wait_ge(S["ca_x_added"], 1 + 2 * APAIRS * B)

        @block.gpsimd
        def _(pool):
            g = nc.gpsimd
            g.memset(minus_half[:, :], -0.5)
            g.memset(eps_t[:, :], LN_EPS).then_inc(powers_ready, 1)
            pool.wait_ge(powers_ready, 1)
            for p in range(2):
                if p == 1:
                    pool_enter(pool, 1, 0)
                g.memset(q_t[0:W, :, 1:HEADS:2, :], 0.0).then_inc(q_zeroed, 1)
                pool.wait_ge(q_zeroed, 2 * p + 1)
                g.memset(q_t[W:P, :, 0:HEADS:2, :], 0.0).then_inc(q_zeroed, 1)
                pool.wait_ge(q_zeroed, 2 * p + 2)
                if p == 0:
                    pool_enter(pool, 0, 0)
                pool_stack(pool, p)
                if p == 0:
                    pool.wait_ge(stack_done, 1)
                    pool_causal(pool)


def kernel(L0_attn_resid, L0_attn_W_Q, L0_attn_W_K, L0_attn_W_V, L0_attn_W_out, L0_attn_b_out,
           L0_ffn_wqkv, L0_ffn_q_scale, L0_ffn_k_scale, L0_ffn_wo, L0_ffn_ln_g, L0_ffn_ln_b,
           L0_ffn_w1, L0_ffn_b1, L0_ffn_w2, L0_ffn_b2):
    import numpy as np
    import concourse.bacc as bacc
    from concourse import mybir as mb
    from concourse.bass_utils import run_bass_kernel_spmd

    f = np.float32
    batches, tokens, dim = L0_attn_resid.shape
    depth, inner3 = L0_ffn_wqkv.shape[0], L0_ffn_wqkv.shape[2]
    dh = L0_ffn_q_scale.shape[1]
    hid = L0_ffn_w2.shape[1]
    heads, adh = L0_attn_W_Q.shape[1:]

    half_idx = np.arange(0, dh, 2, dtype=f)
    inv_freq = (f(1.0) / f(10000.0) ** (half_idx / f(dh))).astype(f)
    t = np.arange(tokens, dtype=f)
    freqs = t[:, None] * inv_freq[None, :]
    power = (t - f(tokens // 2)) / f(dh // 2)
    xpos = ((half_idx + f(0.4 * dh)) / f(1.4 * dh))[None, :].astype(f) ** power[:, None]
    cos, sin = np.cos(freqs), np.sin(freqs)
    pair = lambda a, b: np.concatenate([a, b], axis=1)
    rot_cos = np.stack([8 * pair(cos * xpos, cos * xpos), pair(cos / xpos, cos / xpos)], 1).astype(f)
    rot_sin = np.stack([8 * pair(-sin * xpos, sin * xpos), pair(-sin / xpos, sin / xpos)], 1).astype(f)

    w = dim // 2
    i, j = np.arange(w)[:, None], np.arange(w)[None, :]
    own, before = np.where(j <= i, 0.0, MASKED), np.where(j >= i, 0.0, MASKED)
    nothing = np.full((w, w), MASKED)
    second = np.concatenate([before, own], axis=1)
    masks = np.stack([np.concatenate([np.concatenate([own, nothing], 1), second], 0),
                      np.concatenate([np.concatenate([own, before], 1), second], 0)], 1).astype(f)
    i, j = np.arange(dim)[:, None], np.arange(dim)[None, :]
    not_first = np.ones((dim, 2, depth, tokens // dim), f)
    not_first[dim // 2:, 0, :, 0] = 0.0
    not_first[:, 1, :, 0] = 0.0

    rows = lambda a: np.broadcast_to(a, (dim, *a.shape))
    b1 = np.zeros((depth, 2, -(-hid // dim) * dim), f)
    b1[:, :, :hid] = np.asarray(L0_ffn_b1).reshape(depth, 2, hid)
    arrays = {
        "x_in": L0_attn_resid,
        "wq_t": np.transpose(L0_attn_W_Q, (2, 1, 0)),
        "wk_t": np.transpose(L0_attn_W_K, (2, 1, 0)),
        "wv": np.reshape(L0_attn_W_V, (dim, heads * adh)),
        "w_out": np.transpose(L0_attn_W_out, (1, 0, 2)).reshape(heads * adh // dim, dim, dim).transpose(1, 0, 2),
        "b_out": rows(np.asarray(L0_attn_b_out)),
        "wqkv": L0_ffn_wqkv,
        "qk_scale": rows(np.stack([L0_ffn_q_scale, L0_ffn_k_scale], 1)),
        "wo": L0_ffn_wo,
        "ln_g": np.transpose(L0_ffn_ln_g), "ln_b": np.transpose(L0_ffn_ln_b),
        "w1": L0_ffn_w1,
        "b1": b1.reshape(depth, 2, -1, dim).transpose(3, 0, 1, 2),
        "w2": L0_ffn_w2, "b2": rows(np.asarray(L0_ffn_b2)),
        "rot_cos": rot_cos, "rot_sin": rot_sin,
        "local_mask": masks, "not_first": not_first.reshape(dim, 2, -1),
        "causal_mask": np.where(j <= i, 0.0, MASKED).astype(f),
        "identity": np.eye(dim, dtype=f),
    }
    arrays = {k: np.ascontiguousarray(a) for k, a in arrays.items()}
    nc = bacc.Bacc("TRN2", target_bir_lowering=False, num_devices=1)
    args = [nc.dram_tensor(f"in_{k}", a.shape, mb.dt.from_np(a.dtype), kind="ExternalInput").ap()
            for k, a in arrays.items()]
    result = nc.dram_tensor("result", (batches, tokens, dim), mb.dt.float32, kind="ExternalOutput").ap()
    build_program(nc, *args, result)
    r = run_bass_kernel_spmd(nc, [{f"in_{k}": a for k, a in arrays.items()}], core_ids=[0])
    return r.results[0]["result"]
```

```python
from contextlib import ExitStack

import concourse.bass as bass
from concourse import mybir

F32 = mybir.dt.float32
BF16 = mybir.dt.bfloat16
F32R = mybir.dt.float32r
ACT = mybir.ActivationFunctionType
ALU = mybir.AluOpType
AX = mybir.AxisListType

P = 128
BANK = 512
GROUP = BANK // P
LN_EPS = 1e-5
NORM_FLOOR = 1e-24
MASKED = -1e30


def build_program(nc, x_in, wq_t, wk_t, wv, w_out, b_out, wqkv, qk_scale, wo, ln_g, ln_b,
                  w1, b1, w2, b2, rot_cos, rot_sin, local_mask, not_first, causal_mask, identity,
                  out):
    B, TOKENS, DIM = x_in.shape
    T = TOKENS // P
    DEPTH, _, INNER3 = wqkv.shape
    INNER = INNER3 // 3
    DH = qk_scale.shape[3]
    HEADS = INNER // DH
    PAIRS = HEADS // 2
    HID = w2.shape[1]
    HC = (HID + P - 1) // P
    HROWS = [min(P, HID - P * j) for j in range(HC)]
    NT = DEPTH * T
    W = P // 2
    AH = wq_t.shape[1]
    ADH = wq_t.shape[0]
    APAIRS = AH // 2
    CAUSAL_SCALE = float(ADH) ** -0.5
    assert DIM == P and DH == W and ADH == W and B * P == BANK and INNER == BANK

    with ExitStack() as ctx:
        def sb(name, shape, dt=F32, at=ctx):
            return at.enter_context(nc.sbuf_tensor(name, shape, dt))

        def sem(name):
            return ctx.enter_context(nc.semaphore(name))

        x = sb("x", [P, B, T, P])
        ident = sb("ident", [P, P])
        ident_bf = sb("ident_bf", [P, P], BF16)
        wqkv_sb = sb("wqkv_sb", [P, DEPTH, 3 * INNER])
        wo_sb = sb("wo_sb", [P, DEPTH, PAIRS, P])
        w2_sb = sb("w2_sb", [P, DEPTH, HC, P])
        g_col = sb("g_col", [P, DEPTH])
        b_col = sb("b_col", [P, DEPTH])
        b1_col = sb("b1_col", [P, DEPTH, 2, HC])
        b2_row = sb("b2_row", [P, DEPTH, P])
        bout_row = sb("bout_row", [P, P])
        scale_row = sb("scale_row", [P, DEPTH, 2, DH])
        cos_t = sb("cos_t", [P, NT, 2, DH])
        sin_t = sb("sin_t", [P, NT, 2, DH])
        lmask = sb("lmask", [P, NT, P], BF16)
        notfirst = sb("notfirst", [P, 2, NT])
        cmask = sb("cmask", [P, P], BF16)
        minus_half = sb("minus_half", [P, 2 * HEADS])
        eps_t = sb("eps_t", [P, T])
        spare = sb("spare", [P, 1])
        warm = sb("warm", [P, 2])
        stats = sb("stats", [P, T, 6])
        mv = sb("mv", [P, T, 2])
        veps = sb("veps", [P, T])
        rstd = sb("rstd", [P, T])

        ca_stat = sb("ca_stat", [P, B, T, 6])
        ca_mv = sb("ca_mv", [P, B, T, 2])
        ca_veps = sb("ca_veps", [P, B, T])
        ca_rstd = sb("ca_rstd", [P, B, T])

        local = ExitStack()
        y = sb("y", [P, B, NT + T, P], at=local)
        a_in = sb("a_in", [P, B, P], at=local)
        h_t = sb("h_t", [P, B, P], at=local)
        h_last = sb("h_last", [P, P], at=local)
        sq = sb("sq", [P, 2, HEADS, DH], at=local)
        qn = sb("qn", [P, 2, HEADS, DH], at=local)
        qkr = sb("qkr", [P, 2, HEADS, DH], at=local)
        ss = sb("ss", [P, 2 * HEADS], at=local)
        rn = sb("rn", [P, 2 * HEADS], at=local)
        q_t = sb("q_t", [P, B, HEADS, P], at=local)
        k_t = sb("k_t", [P, B, PAIRS, 3, W], at=local)
        v_cur = sb("v_cur", [P, B, INNER], at=local)
        v_mix = sb("v_mix", [P, B, INNER], at=local)
        probs = sb("probs", [P, 2, HEADS, P], at=local)
        probs_t = sb("probs_t", [P, HEADS, P], at=local)
        nmax = sb("nmax", [P, 2, HEADS], at=local)
        rsum = sb("rsum", [P, 2, HEADS], at=local)
        rinv = sb("rinv", [P, 2, HEADS], at=local)
        z_t = sb("z_t", [P, PAIRS, P], at=local)
        y1 = sb("y1", [P, B, P], at=local)
        h2 = sb("h2", [P, B, P], at=local)
        carry = sb("carry", [1, B, W], at=local)
        hn = sb("hn", [P, B, P], at=local)
        hn_t = sb("hn_t", [P, B, P], at=local)
        w1_cur = sb("w1_cur", [P, 2 * HID], at=local)
        u_t = sb("u_t", [P, HC, B * P], at=local)
        local.close()

        causal = ExitStack()
        xn_all = sb("xn_all", [P, B, T, P], at=causal)
        xn = sb("xn", [P, T, P], at=causal)
        wq_sb, wk_sb = q_t[0:ADH, 0:B // 2, :, :], q_t[0:ADH, B // 2:B, :, :]
        assert AH == B // 2 * HEADS
        ca_pt = sb("ca_pt", [P, 2, 2, T, P], at=causal)
        m_sb = sb("m_sb", [P, AH, 2, P], F32R, at=causal)
        m_cur = sb("m_cur", [P, 2, 2, 2, P], F32R, at=causal)
        wv_sb = sb("wv_sb", [P, AH * ADH], at=causal)
        wout_sb = sb("wout_sb", [P, APAIRS, P], at=causal)
        xn_t = sb("xn_t", [P, T * P], at=causal)
        xn_parts = sb("xn_parts", [P, 2, T * P], F32R, at=causal)
        qm = sb("qm", [P, 2, 2, 2, T * P], F32R, at=causal)
        va = sb("va", [P, 2, T, P], at=causal)
        ca_p = sb("ca_p", [P, 2, 2, T * P], at=causal)
        ca_nmax = sb("ca_nmax", [P, 2, T, 2], at=causal)
        ca_rsum = sb("ca_rsum", [P, 2, T, 2], at=causal)
        ca_inv = sb("ca_inv", [P, T // 2, 2], at=causal)
        ca_rinv = sb("ca_rinv", [P, T // 2, 2, ADH], at=causal)
        ca_rt = sb("ca_rt", [P, BANK], at=causal)
        ca_z = sb("ca_z", [P, BANK], at=causal)
        causal.close()

        def bank(name, n=1):
            return ctx.enter_context(nc.psum_tensor(name, [P, n * BANK], F32))

        ps_qk = bank("ps_qk", 2)
        ps_v = bank("ps_v")
        ps_t = bank("ps_t")
        ps_s = bank("ps_s", 2)
        ps_w = bank("ps_w")
        ps_z = bank("ps_z")

        x0_loaded, x_loaded = sem("x0_loaded"), sem("x_loaded")
        first_loaded, const_loaded = sem("first_loaded"), sem("const_loaded")
        wqk_loaded, heads_loaded = sem("wqk_loaded"), sem("heads_loaded")
        stored = sem("stored")
        tables_ready, masks_ready, powers_ready = sem("tables_ready"), sem("masks_ready"), sem("powers_ready")
        q_zeroed = sem("q_zeroed")
        stack_done = sem("stack_done")
        names = """
            ln_stats ln_aggr ln_veps ln_rstd ln_out
            a_copied a_turned h_saved h_ready qk_made v_made squared summed clamped normed_r qk_normed
            rot_sin_done rot_cos_done rotated q_turned k_turned q_ready k_kept k_ready v_kept v_ready
            s_made max_ready exp_done rinv_ready p_ready p_lo_turned p_hi_turned pt_lo pt_hi
            z_made z_ready o_made y1_ready
            first_row h2_copied carry_copied c_stats c_agg c_eps c_rstd hn_ready t3_made hn_t_ready
            w1_copied gv_made gelu_done u_done w2_made bias_added y2_done
            m_made m_hi m_lo m_copied ca_stats ca_aggr ca_veps ca_rstd ca_xn ca_bias xn_copied
            ca_turned ca_xn_hi ca_xn_lo ca_xn_t ca_proj ca_q_hi ca_q_ready ca_v_ready
            ca_s ca_max ca_exp ca_pt ca_pt_dve ca_pt_act ca_pv
            ca_inverted ca_rinv_ready ca_r_made ca_rt_ready ca_z_ready ca_o ca_x_added""".split()
        S = {n: sem(n) for n in names}

        def wait(eng, s, n):
            if not isinstance(n, int) or n > 0:
                eng.wait_ge(s, n)

        FIRST = 16 * 6
        CONSTS = 16 * (8 + 2 * (DEPTH - 1) + DEPTH - 1 + HC)

        def live(i, lag):
            return not isinstance(i, int) or lag <= i < NT + lag

        def stack(eng, body):
            for i in range(4):
                body(i, True)
            with eng.Fori(4, NT - 1) as i:
                body(i, True)
            for i in range(NT - 1, NT + 3):
                body(i, False)

        def wide_banks(j):
            return ((ps_s[:, 0:BANK], ps_s[:, BANK:2 * BANK]), (ps_w, ps_z), (ps_v, ps_t))[j]

        def pe_stack(pe, p):
            def turn_tile(i):
                pe.wait_ge(S["a_copied"], 48 * (NT * p + i + 1))
                for b in range(B):
                    mm = pe.transpose(ps_v[:, P * b:P * b + P], a_in[:, b, :], ident[:])
                mm.then_inc(S["a_turned"], 1)

            def body(i, more):
                step = NT * p + i
                if isinstance(i, int) and i == 1 and p == 0:
                    pe.wait_ge(const_loaded, CONSTS)
                    pe.wait_ge(masks_ready, 1)
                nA, nB, mC, mD = step * B, (step - 1) * B, step - 2, step - 3

                def project_qk(k):
                    if k == 0:
                        pe.wait_ge(S["h_ready"], step + 1)
                    wait(pe, S["qk_normed"], nA + k)
                    for c_ in range(2):
                        mm = pe.matmul(ps_qk[:, INNER * c_:INNER * c_ + INNER], h_t[:, k, :],
                                       wqkv_sb[:, i // T, INNER * c_:INNER * c_ + INNER],
                                       start=True, stop=True)
                    mm.then_inc(S["qk_made"], 1)

                def scores(k):
                    pe.wait_ge(S["q_ready"], nB + k + 1)
                    pe.wait_ge(S["k_ready"], nB + k + 1)
                    wait(pe, S["exp_done"], nB + k)
                    if k == B - 1 and live(i, 2):
                        pe.wait_ge(S["u_done"], mC * HC + 1)
                    for g in range(HEADS // GROUP):
                        pe.matmul(ps_s[:, BANK * g:BANK * g + BANK], ident_bf[:],
                                  lmask[:, i - 1, :].unsqueeze(1).broadcast_to([P, GROUP, P]),
                                  start=True, stop=False, skip_group_check=True)
                    for h in range(HEADS):
                        keys = k_t[:, k, h // 2, :, :]
                        for w in range(2):
                            mm = pe.matmul(ps_s[W * w:W * w + W, P * h:P * h + P],
                                           q_t[:, k, h, W * w:W * w + W],
                                           keys[:, 0:2, :] if w else keys[:, 0:3:2, :],
                                           start=False, stop=True, skip_group_check=True)
                    mm.then_inc(S["s_made"], 1)

                def turn_probs(k, ia, ib):
                    pe.wait_ge(S["p_ready"], ib + 1)
                    wait(pe, S["y1_ready"], ib)
                    if k == 0 and live(i, 3):
                        pe.wait_ge(S["y2_done"], mD + 1)
                    for h in range(HEADS):
                        if h == GROUP and k == 0 and live(i, 1):
                            pe.wait_ge(S["k_ready"], ia + 1)
                        elif h == GROUP and k and live(i, 0):
                            wait(pe, S["k_ready"], ia)
                        dst = (ps_w, ps_z)[h // GROUP]
                        mm = pe.transpose(dst[:, P * (h % GROUP):P * (h % GROUP) + P],
                                          probs[:, (k - 1) % 2, h, :], ident[:])
                        if h % GROUP == GROUP - 1:
                            mm.then_inc(S[("p_lo_turned", "p_hi_turned")[h // GROUP]], 1)

                def values(k, ib):
                    b = (k - 1) % B
                    pe.wait_ge(S["v_ready"], ib + 1)
                    for h in range(HEADS):
                        if h % GROUP == 0:
                            pe.wait_ge(S["pt_hi" if h else "pt_lo"], ib + 1)
                        r = W * (h % 2)
                        for w in range(2):
                            v = (v_mix, v_cur)[w]
                            mm = pe.matmul(ps_w[r:r + W, P * (h // 2) + W * w:P * (h // 2) + W * w + W],
                                           v[:, b, DH * h:DH * h + DH], probs_t[:, h, W * w:W * w + W],
                                           start=True, stop=True, skip_group_check=True)
                    mm.then_inc(S["z_made"], 1)

                def project_v(k, ia):
                    wait(pe, S["v_ready"], ia)
                    if k:
                        left, tile = h_t[:, k - 1, :], i
                    else:
                        pe.wait_ge(S["h_saved"], step)
                        left, tile = h_last[:, :], i - 1
                    pe.matmul(ps_v[:, :], left, wqkv_sb[:, tile // T, 2 * INNER:3 * INNER],
                              start=True, stop=True).then_inc(S["v_made"], 1)

                def turn_qk(ia):
                    pe.wait_ge(S["rotated"], ia + 1)
                    for c_, dst, free, done in ((0, ps_t, "q_ready", "q_turned"),
                                                (1, ps_z, "k_ready", "k_turned")):
                        wait(pe, S[free], ia)
                        for j in range(PAIRS):
                            mm = pe.transpose(dst[:, P * j:P * j + P],
                                              qkr[:, c_, 2 * j:2 * j + 2, :], ident[:])
                        mm.then_inc(S[done], 1)

                def project_out(k, ib):
                    tile = i - 1 if k else i - 2
                    pe.wait_ge(S["z_ready"], ib + 1)
                    for j in range(PAIRS):
                        mm = pe.matmul(ps_w[:, 0:P], z_t[:, j, :], wo_sb[:, tile // T, j, :],
                                       start=(j == 0), stop=(j == PAIRS - 1))
                    mm.then_inc(S["o_made"], 1)

                def turn_hidden():
                    pe.wait_ge(S["hn_ready"], mC + 1)
                    if live(i, 1):
                        pe.wait_ge(S["exp_done"], nB + B - 1)
                    for b in range(B):
                        mm = pe.transpose(ps_s[:, P * b:P * b + P], hn[:, b, :], ident[:])
                    mm.then_inc(S["t3_made"], 1)

                def widen(j):
                    if j == 0:
                        pe.wait_ge(S["hn_t_ready"], mC + 1)
                        pe.wait_ge(S["w1_copied"], 16 * mC + 16)
                    if j == 1:
                        if live(i, 1):
                            pe.wait_ge(S["y1_ready"], nB + B - 1)
                        if live(i, 0):
                            pe.wait_ge(S["k_ready"], nA + B - 1)
                    if j == 2:
                        if more:
                            pe.wait_ge(S["h_ready"], step + 2)
                        if live(i, 0):
                            pe.wait_ge(S["v_ready"], nA + B - 1)
                            pe.wait_ge(S["q_ready"], nA + B - 1)
                    for c_, dst in enumerate(wide_banks(j)):
                        mm = pe.matmul(dst[0:HROWS[j], :],
                                       w1_cur[:, HID * c_ + P * j:HID * c_ + P * j + HROWS[j]],
                                       hn_t[:, :, :], start=True, stop=True)
                    mm.then_inc(S["gv_made"], 1)

                def narrow():
                    pe.wait_ge(S["u_done"], (mD + 1) * HC)
                    for b in range(B):
                        for j in range(HC):
                            mm = pe.matmul(ps_w[:, P * b:P * b + P], u_t[0:HROWS[j], j, P * b:P * b + P],
                                           w2_sb[0:HROWS[j], (i - 3) // T, j, :],
                                           start=(j == 0), stop=(j == HC - 1))
                    mm.then_inc(S["w2_made"], 1)

                if isinstance(i, int) and i == 0:
                    turn_tile(0)
                for k in range(B):
                    ia, ib = nA + k - 1, nB + k - 1
                    late_a, late_b = live(i, 0 if k else 1), live(i, 1 if k else 2)
                    if k == B - 1 and live(i, 2):
                        turn_hidden()
                    if live(i, 0):
                        project_qk(k)
                    if k == 0:
                        if live(i, 3):
                            narrow()
                        if late_a:
                            turn_qk(ia)
                    if k < B - 1 and live(i, 1):
                        scores(k)
                    if k == B - 1 and live(i, 2):
                        widen(0)
                    if late_b:
                        turn_probs(k, ia, ib)
                    if k and late_a:
                        project_v(k, ia)
                    if late_b:
                        values(k, ib)
                    if k == 0 and late_a:
                        project_v(k, ia)
                    if k and late_a:
                        turn_qk(ia)
                    if late_b:
                        project_out(k, ib)
                if live(i, 1):
                    scores(B - 1)
                if more:
                    pe.wait_ge(S["v_ready"], nA + B - 1)
                    turn_tile(i + 1)
                if live(i, 2):
                    widen(1)
                    widen(2)

            stack(pe, body)

        def act_stack(act, p):
            sc = nc.scalar

            def place_tile(i):
                act.wait_ge(S["a_turned"], NT * p + i + 1)
                src = ps_v[:, :].rearrange("p (b t) -> p b t", b=B)
                sc.copy(h_t[:, :, 1:P], src[:, :, 1:P])
                sc.activation(h_t[:, :, 0], src[:, :, 0], ACT.Copy, scale=notfirst[:, 0, bass.ds(i, 1)])\
                  .then_inc(S["h_ready"], 1)

            EARLY = 2

            def body(i, more):
                step = NT * p + i
                nA, nB, mC = step * B, (step - 1) * B, step - 2

                def square(k):
                    act.wait_ge(S["qk_made"], nA + k + 1)
                    wait(act, S["summed"], nA + k)
                    sc.activation(sq[:, :, :, :], ps_qk[:, :], ACT.Square).then_inc(S["squared"], 1)

                def exponentials(k, h0, h1):
                    act.wait_ge(S["max_ready"], nB + k + 1)
                    for h in range(h0, h1):
                        e = sc.activation(probs[:, k % 2, h, :], ps_s[:, P * h:P * h + P], ACT.Exp,
                                          bias=nmax[:, k % 2, h:h + 1],
                                          accum_out=rsum[:, k % 2, h:h + 1])
                    if h1 == HEADS:
                        e.then_inc(S["exp_done"], 1)

                def first_row():
                    act.wait_ge(S["y1_ready"], (mC + 1) * B)
                    wait(act, S["carry_copied"], 16 * mC)
                    wait(act, S["hn_ready"], mC)
                    sc.activation(h2[0:1, :, W:P], carry[:, :, :], ACT.Copy,
                                  scale=notfirst[0:1, 1, bass.ds(i - 2, 1)]).then_inc(S["first_row"], 1)

                def p_out(ib):
                    act.wait_ge(S["p_hi_turned"], ib + 1)
                    sc.copy(probs_t[:, GROUP:HEADS, :], ps_z[:, :]).then_inc(S["pt_hi"], 1)

                def z_out(ib):
                    act.wait_ge(S["z_made"], ib + 1)
                    sc.copy(z_t[:, :, :], ps_w[:, :]).then_inc(S["z_ready"], 1)

                def v_out(k, ia):
                    b = (k - 1) % B
                    act.wait_ge(S["v_made"], ia + 1)
                    if isinstance(i, int) and (i == 0 or (i == 1 and k == 0)):
                        sc.copy(v_mix[W:P, b, :], ps_v[W:P, :]).then_inc(S["v_kept"], 1)
                    else:
                        sc.copy(v_mix[W:P, b, :], v_cur[W:P, b, :]).then_inc(S["v_kept"], 1)
                    sc.copy(v_mix[0:W, b, :], ps_v[0:W, :])
                    act.wait_ge(S["v_kept"], ia + 1)
                    sc.copy(v_cur[:, b, :], ps_v[:, :]).then_inc(S["v_ready"], 1)

                def k_out(j):
                    b, n = j % B, nA + j
                    act.wait_ge(S["k_turned"], n + 1)
                    src = ps_z[:, :].rearrange("p (j w t) -> p j w t", j=PAIRS, w=2)
                    first = isinstance(i, int) and (i == 0 or (i == 1 and j < 0))
                    sc.copy(k_t[:, b, :, 2, :], src[:, :, 1, :] if first else k_t[:, b, :, 1, :])\
                      .then_inc(S["k_kept"], 1)
                    act.wait_ge(S["k_kept"], n + 1)
                    sc.copy(k_t[:, b, :, 0:2, :], src).then_inc(S["k_ready"], 1)

                def q_out(j):
                    b, n = j % B, nA + j
                    act.wait_ge(S["q_turned"], n + 1)
                    src = ps_t[:, :].rearrange("p (j t) -> p j t", j=PAIRS)
                    sc.copy(q_t[0:W, b, 0:HEADS:2, :], src[0:W])
                    sc.copy(q_t[W:P, b, 1:HEADS:2, :], src[W:P]).then_inc(S["q_ready"], 1)

                def gelu(j):
                    act.wait_ge(S["gv_made"], mC * HC + j + 1)
                    if j == 0:
                        wait(act, S["w2_made"], mC)
                    sc.activation(u_t[0:HROWS[j], j, :], wide_banks(j)[1][0:HROWS[j], :], ACT.Gelu,
                                  bias=b1_col[0:HROWS[j], bass.ds((i - 2) // T, 1), 1, j])\
                      .then_inc(S["gelu_done"], 1)

                if isinstance(i, int) and i == 1 and p == 0:
                    act.wait_ge(const_loaded, CONSTS)
                if isinstance(i, int) and i == 0:
                    place_tile(0)
                for k in range(B):
                    ia, ib = nA + k - 1, nB + k - 1
                    late_a, late_b = live(i, 0 if k else 1), live(i, 1 if k else 2)
                    last = k == B - 1
                    if last and live(i, 2):
                        act.wait_ge(S["t3_made"], mC + 1)
                        lay = (i - 2) // T
                        sc.activation(hn_t[:, :, :], ps_s[:, 0:BANK], ACT.Identity,
                                      scale=g_col[:, bass.ds(lay, 1)], bias=b_col[:, bass.ds(lay, 1)])\
                          .then_inc(S["hn_t_ready"], 1)
                    if last and live(i, 0):
                        k_out(B - 3)
                    if live(i, 0):
                        square(k)
                    if k == 1 and live(i, 2):
                        first_row()
                    if last and live(i, 0):
                        wait(act, S["v_made"], nA)
                        sc.copy(h_last[:, :], h_t[:, B - 1, :]).then_inc(S["h_saved"], 1)
                    if last and live(i, 2):
                        sc.activation(warm[:, 0:1], eps_t[:, 0:1], ACT.Gelu)
                        gelu(0)
                    if k == 0 and live(i, 1):
                        k_out(-1)
                        q_out(-1)
                    if k == B - 2 and live(i, 0):
                        k_out(0)
                        q_out(0)
                    if late_b:
                        p_out(ib)
                    if last and live(i, 0):
                        q_out(B - 3)
                    if not last and live(i, 1):
                        exponentials(k, 0, EARLY)
                    if late_b:
                        z_out(ib)
                    if not last and live(i, 1):
                        exponentials(k, EARLY, HEADS)
                    if late_a:
                        v_out(k, ia)
                    if last and live(i, 0):
                        k_out(B - 2)
                        q_out(B - 2)
                if more:
                    act.wait_ge(S["h_saved"], step + 1)
                    place_tile(i + 1)
                if live(i, 2):
                    gelu(1)
                    gelu(2)
                if live(i, 1):
                    sc.activation(warm[:, 1:2], eps_t[:, 0:1], ACT.Exp)
                    exponentials(B - 1, 0, HEADS)

            stack(act, body)

        def make_masks(dve):
            v = nc.vector
            dve.wait_ge(const_loaded, CONSTS)
            v.tensor_copy(ident_bf[:, :], ident[:, :])
            v.tensor_copy(cmask[:, :], probs[:, 1, 0, :])
            masks = lmask[:, :, :].rearrange("p (l t) k -> p l t k", l=DEPTH)
            for lay in range(DEPTH):
                v.tensor_copy(masks[:, lay, 0, :], probs[:, 0, 0, :])
                last = v.tensor_copy(masks[:, lay, 1:T, :],
                                     probs[:, 0, 1, :].unsqueeze(1).broadcast_to([P, T - 1, P]))
            last.then_inc(masks_ready, 1)

        def scale_tables(dve, lay):
            v = nc.vector
            half, tiles = DH // 2, slice(lay * T, lay * T + T)
            v.tensor_tensor(cos_t[:, tiles, :, :], cos_t[:, tiles, :, :],
                            scale_row[:, lay, :, :].unsqueeze(1).broadcast_to([P, T, 2, DH]), ALU.mult)
            for lo, hi in ((0, half), (half, 0)):
                last = v.tensor_tensor(sin_t[:, tiles, :, lo:lo + half], sin_t[:, tiles, :, lo:lo + half],
                                       scale_row[:, lay, :, hi:hi + half].unsqueeze(1)
                                       .broadcast_to([P, T, 2, half]), ALU.mult)
            last.then_inc(tables_ready, 1)
            dve.wait_ge(tables_ready, lay + 1)

        def dve_stack(dve, p):
            v = nc.vector

            def body(i, more):
                step = NT * p + i
                nA, nB, mC, mD = step * B, (step - 1) * B, step - 2, step - 3

                def sum_squares(k):
                    dve.wait_ge(S["squared"], nA + k + 1)
                    wait(dve, S["normed_r"], nA + k)
                    v.tensor_reduce(ss[:, :], sq[:, :, :, :].rearrange("p c h d -> p (c h) d"),
                                    AX.X, ALU.add).then_inc(S["summed"], 1)
                    dve.wait_ge(S["summed"], nA + k + 1)
                    v.tensor_scalar(ss[:, :], ss[:, :], NORM_FLOOR, None, ALU.max).then_inc(S["clamped"], 1)

                def norm(k):
                    dve.wait_ge(S["normed_r"], nA + k + 1)
                    wait(dve, S["rotated"], nA + k)
                    r = rn[:, :].rearrange("p (c h) -> p c h", c=2).unsqueeze(3)
                    v.tensor_tensor(qn[:, :, :, :], ps_qk[:, :].rearrange("p (c h d) -> p c h d", c=2, h=HEADS),
                                    r.broadcast_to([P, 2, HEADS, DH]), ALU.mult).then_inc(S["qk_normed"], 1)

                def rotate_sin(k):
                    dve.wait_ge(S["qk_normed"], nA + k + 1)
                    wait(dve, S["k_turned"], nA + k)
                    half = DH // 2
                    for lo, hi in ((0, half), (half, 0)):
                        rot = v.tensor_tensor(
                            qkr[:, :, :, lo:lo + half], qn[:, :, :, hi:hi + half],
                            sin_t[:, i, :, lo:lo + half].unsqueeze(2).broadcast_to([P, 2, HEADS, half]),
                            ALU.mult)
                    rot.then_inc(S["rot_sin_done"], 1)

                def rotate_cos(k):
                    dve.wait_ge(S["rot_sin_done"], nA + k + 1)
                    v.tensor_tensor(qn[:, :, :, :], qn[:, :, :, :],
                                    cos_t[:, i, :, :].unsqueeze(2).broadcast_to([P, 2, HEADS, DH]),
                                    ALU.mult).then_inc(S["rot_cos_done"], 1)

                def row_max(k):
                    dve.wait_ge(S["s_made"], nB + k + 1)
                    wait(dve, S["exp_done"], nB + k - 1)
                    v.tensor_reduce(nmax[:, k % 2, :], ps_s[:, :].rearrange("p (h c) -> p h c", h=HEADS),
                                    AX.X, ALU.max, negate=True).then_inc(S["max_ready"], 1)

                def invert(k):
                    dve.wait_ge(S["exp_done"], nB + k + 1)
                    wait(dve, S["p_ready"], nB + k - 1)
                    v.reciprocal(rinv[:, k % 2, :], rsum[:, k % 2, :]).then_inc(S["rinv_ready"], 1)

                def probs_out(ib):
                    dve.wait_ge(S["p_lo_turned"], ib + 1)
                    v.tensor_copy(probs_t[:, 0:GROUP, :], ps_w[:, :]).then_inc(S["pt_lo"], 1)

                def add_attention(k, ib):
                    b, tile = (k - 1) % B, i - 1 if k else i - 2
                    dve.wait_ge(S["o_made"], ib + 1)
                    if k == 1 and live(i, 2):
                        dve.wait_ge(S["bias_added"], mC + 1)
                        dve.wait_ge(S["h2_copied"], 32 * (mC + 1))
                        dve.wait_ge(S["carry_copied"], 16 * (mC + 1))
                    v.tensor_tensor(y1[:, b, :], y[:, b, tile, :], ps_w[:, 0:P],
                                    ALU.add).then_inc(S["y1_ready"], 1)

                def hidden_stats():
                    dve.wait_ge(S["h2_copied"], 32 * (mC + 1))
                    dve.wait_ge(S["first_row"], mC + 1)
                    for b in range(B):
                        st = v.bn_stats(stats[:, b, :], h2[:, b, :])
                    st.then_inc(S["c_stats"], 1)
                    dve.wait_ge(S["c_stats"], mC + 1)
                    v.memset(spare[:, :], 0.0)
                    for b in range(B):
                        st = v.bn_aggr(mv[:, b, :], stats[:, b, :])
                    st.then_inc(S["c_agg"], 1)

                def norm_hidden():
                    dve.wait_ge(S["c_rstd"], mC + 1)
                    for b in range(B):
                        st = v.tensor_scalar(hn[:, b, :], h2[:, b, :], mv[:, b, 0:1],
                                             rstd[:, b:b + 1], ALU.subtract, ALU.mult)
                    st.then_inc(S["hn_ready"], 1)

                def gate(j):
                    dve.wait_ge(S["gelu_done"], mC * HC + j + 1)
                    v.scalar_tensor_tensor(u_t[0:HROWS[j], j, :], wide_banks(j)[0][0:HROWS[j], :],
                                           b1_col[0:HROWS[j], bass.ds((i - 2) // T, 1), 0, j],
                                           u_t[0:HROWS[j], j, :], ALU.add, ALU.mult)\
                     .then_inc(S["u_done"], 1)

                def add_ffn():
                    dve.wait_ge(S["w2_made"], mD + 1)
                    dve.wait_ge(S["bias_added"], mD + 1)
                    v.tensor_tensor(y[:, :, i + T - 3, :], y[:, :, i + T - 3, :],
                                    ps_w[:, :].rearrange("p (b f) -> p b f", b=B),
                                    ALU.add).then_inc(S["y2_done"], 1)

                for k in range(B):
                    ib = nB + k - 1
                    late_b = live(i, 1 if k else 2)
                    last = k == B - 1
                    if k == B - 2 and live(i, 2):
                        hidden_stats()
                    if isinstance(i, int) and i == 0:
                        if p == 0 and k == 0:
                            dve.wait_ge(x_loaded, 16 * B)
                        dve_enter_stats(dve, p, k + 1)
                    if live(i, 0):
                        sum_squares(k)
                    if isinstance(i, int) and i == 0:
                        dve_enter_norm(dve, p, k + 1)
                    if k == 0 and live(i, 3):
                        add_ffn()
                    if late_b:
                        probs_out(ib)
                    if not last and live(i, 1):
                        row_max(k)
                    if last and live(i, 2):
                        gate(0)
                    if live(i, 0):
                        norm(k)
                    if k == B - 2 and live(i, 2):
                        norm_hidden()
                    if last and late_b:
                        add_attention(k, ib)
                    if live(i, 0):
                        rotate_sin(k)
                    if not last and live(i, 1):
                        invert(k)
                    if not last and late_b:
                        add_attention(k, ib)
                    if live(i, 0):
                        rotate_cos(k)
                    if isinstance(i, int) and i == 0:
                        if p == 0 and k == 0:
                            make_masks(dve)
                        if p == 0 and k == B - 1:
                            scale_tables(dve, 1)
                if live(i, 1):
                    row_max(B - 1)
                if live(i, 2):
                    gate(1)
                    gate(2)
                if live(i, 1):
                    invert(B - 1)

            stack(dve, body)

        CHUNKS = [(0,)] + [tuple(range(t, min(t + 2, T))) for t in range(1, T, 2)]
        assert len(CHUNKS) == B + 1

        def dve_enter_stats(dve, p, c):
            v = nc.vector
            n, cols = len(CHUNKS) * p + c, [(t, b) for t in CHUNKS[c] for b in range(B)]
            for j, (t, b) in enumerate(cols):
                st = v.bn_stats(stats[:, j, :], x[:, b, t, :])
            st.then_inc(S["ln_stats"], 1)
            dve.wait_ge(S["ln_stats"], n + 1)
            for j in range(len(cols)):
                st = v.bn_aggr(mv[:, j, :], stats[:, j, :])
            st.then_inc(S["ln_aggr"], 1)

        def dve_enter_norm(dve, p, c):
            v = nc.vector
            n, cols = len(CHUNKS) * p + c, [(t, b) for t in CHUNKS[c] for b in range(B)]
            dve.wait_ge(S["ln_rstd"], n + 1)
            for j, (t, b) in enumerate(cols):
                st = v.tensor_scalar(y[:, b, t, :], x[:, b, t, :], mv[:, j, 0:1], rstd[:, j:j + 1],
                                     ALU.subtract, ALU.mult)
            st.then_inc(S["ln_out"], 1)
            dve.wait_ge(S["ln_out"], n + 1)

        def pool_enter(pool, p, c):
            n, m = len(CHUNKS) * p + c, B * len(CHUNKS[c])
            pool.wait_ge(S["ln_aggr"], n + 1)
            nc.gpsimd.tensor_tensor(veps[:, 0:m], mv[:, 0:m, 1], eps_t[:, 0:m], ALU.add)\
              .then_inc(S["ln_veps"], 1)
            pool.wait_ge(S["ln_veps"], n + 1)
            nc.gpsimd.tensor_tensor(rstd[:, 0:m], veps[:, 0:m], minus_half[:, 0:m], ALU.pow)\
              .then_inc(S["ln_rstd"], 1)

        def pool_stack(pool, p):
            g = nc.gpsimd

            def body(i, more):
                step = NT * p + i
                nA, nB, mC = step * B, (step - 1) * B, step - 2

                def power(k):
                    pool.wait_ge(S["clamped"], nA + k + 1)
                    wait(pool, S["qk_normed"], nA + k)
                    g.tensor_tensor(rn[:, :], ss[:, :], minus_half[:, :], ALU.pow)\
                     .then_inc(S["normed_r"], 1)

                def scale_probs(k):
                    pool.wait_ge(S["rinv_ready"], nB + k + 1)
                    g.tensor_tensor(probs[:, k % 2, :, :], probs[:, k % 2, :, :],
                                    rinv[:, k % 2, :].unsqueeze(2).broadcast_to([P, HEADS, P]),
                                    ALU.mult).then_inc(S["p_ready"], 1)

                def add_rotated(k):
                    pool.wait_ge(S["rot_cos_done"], nA + k + 1)
                    g.tensor_tensor(qkr[:, :, :, :], qn[:, :, :, :], qkr[:, :, :, :], ALU.add)\
                     .then_inc(S["rotated"], 1)

                def add_bias():
                    pool.wait_ge(S["y1_ready"], (mC + 1) * B)
                    g.tensor_tensor(y[:, :, i + T - 2, :], y1[:, :, :],
                                    b2_row[:, bass.ds((i - 2) // T, 1), :].broadcast_to([P, B, P]),
                                    ALU.add).then_inc(S["bias_added"], 1)

                def hidden_rstd():
                    pool.wait_ge(S["c_agg"], mC + 1)
                    g.tensor_tensor(veps[:, 0:B], mv[:, 0:B, 1], eps_t[:, 0:B], ALU.add).then_inc(S["c_eps"], 1)
                    pool.wait_ge(S["c_eps"], mC + 1)
                    g.tensor_tensor(rstd[:, 0:B], veps[:, 0:B], minus_half[:, 0:B], ALU.pow)\
                     .then_inc(S["c_rstd"], 1)

                for k in range(B):
                    if isinstance(i, int) and i == 0:
                        pool_enter(pool, p, k + 1)
                    if live(i, 0):
                        power(k)
                    if k == B - 2 and live(i, 2):
                        hidden_rstd()
                    if k == 1 and live(i, 2):
                        add_bias()
                    if k < B - 1 and live(i, 1):
                        scale_probs(k)
                    if live(i, 0):
                        add_rotated(k)
                if live(i, 1):
                    scale_probs(B - 1)

            stack(pool, body)

        HALF = T // 2
        UNITS = 2 * T
        assert HALF == GROUP and T * P == 2 * BANK

        PARTS = ((0, 0), (0, 1), (1, 0))

        def groups(i):
            return (i + GROUP) // GROUP

        def groups_before(i, h=0, g=0):
            return sum(2 * groups(m) for m in range(i)) + h * groups(i) + g

        def start_bank(g):
            return (ps_s[:, 0:BANK], ps_s[:, BANK:2 * BANK], ps_v, ps_t, ps_w, ps_z)[g]

        EV = groups_before(T) // 2

        def causal(eng, start, pair_body, flush):
            with eng.Fori(0, B) as b:
                start(b, APAIRS * b)
                pair_body(b, 0, APAIRS * b, 0, True, False)
                with eng.Fori(0, (APAIRS - 2) // 2) as j:
                    pair_body(b, 2 * j + 1, APAIRS * b + 2 * j + 1, 1, True, True)
                    pair_body(b, 2 * j + 2, APAIRS * b + 2 * j + 2, 0, True, True)
                pair_body(b, APAIRS - 1, APAIRS * b + APAIRS - 1, 1, False, True)
                flush(b, APAIRS * b + APAIRS)

        def pe_causal(pe):
            pe.wait_ge(wqk_loaded, 16 * 2)
            for h in range(AH):
                dst = (ps_qk, ps_s)[h // (2 * GROUP)]
                c0 = P * (h % (2 * GROUP))
                pe.matmul(dst[:, c0:c0 + P], wq_sb[:, h // HEADS, h % HEADS, :],
                          wk_sb[:, h // HEADS, h % HEADS, :], start=True, stop=True)\
                  .then_inc(S[{0: "ca_r_made", 1: "ca_turned", 2: "ca_proj"}.get(h, "m_made")], 1)

            def scores(n, par, i, h, tail):
                dst = (ps_qk, ps_s)[h]
                if i == 0:
                    pe.wait_ge(S["ca_q_ready"], 4 * n + 4)
                if i or tail:
                    pe.wait_ge(S["ca_exp"], 1 + UNITS * n + 2 * i + h - 1)
                keys = (i + 1) * P
                for c0 in range(0, keys, BANK):
                    c1 = c0 + max(2 * P, min(keys - c0, BANK))
                    for m, (part_q, part_x) in enumerate(PARTS):
                        pe.matmul(dst[:, c0:c1], qm[:, par, h, part_q, P * i:P * i + P],
                                  xn_parts[:, part_x, c0:c1],
                                  start=(m == 0), stop=(m == len(PARTS) - 1 and keys > c0 + BANK),
                                  skip_group_check=True)
                pe.matmul(dst[:, P * i:P * i + P], ident_bf[:], cmask[:], start=False, stop=True,
                          skip_group_check=True).then_inc(S["ca_s"], 1)

            def turn(n, i, h):
                pe.wait_ge(S["ca_exp"], 1 + UNITS * n + 2 * i + h + 1)
                for g in range(groups(i)):
                    k = groups_before(i, h, g)
                    dst, read = ((ps_v, "ca_pt_dve"), (ps_t, "ca_pt_act"))[k % 2]
                    pe.wait_ge(S[read], 1 + EV * n + k // 2)
                    for kt in range(GROUP * g, min(i + 1, GROUP * g + GROUP)):
                        mm = pe.transpose(dst[:, P * (kt % GROUP):P * (kt % GROUP) + P],
                                          ca_p[:, i % 2, h, P * kt:P * kt + P], ident[:])
                    mm.then_inc(S["ca_pt"], 1)

            def values(n, par, i):
                k = groups_before(i + 1)
                pe.wait_ge(S["ca_pt_dve"], 1 + EV * n + (k + 1) // 2)
                pe.wait_ge(S["ca_pt_act"], 1 + EV * n + k // 2)
                if i == 0:
                    pe.wait_ge(S["ca_v_ready"], 2 * n + 2)
                if i % HALF == 0:
                    pe.wait_ge(S["ca_z_ready"], 1 + 2 * n + i // HALF)
                for kt in range(i + 1):
                    for h in range(2):
                        mm = pe.matmul(ps_z[W * h:W * h + W, P * (i % HALF):P * (i % HALF) + P],
                                       va[:, par, kt, W * h:W * h + W], ca_pt[:, i % 2, h, kt, :],
                                       start=(kt == 0), stop=(kt == i), skip_group_check=True)
                mm.then_inc(S["ca_pv"], 1)

            def spread_inverses(n, half):
                pe.wait_ge(S["ca_rinv_ready"], 2 * n + half + 1)
                for i in range(HALF * half, HALF * half + HALF):
                    mm = pe.transpose(ps_w[:, P * (i % HALF):P * (i % HALF) + P],
                                      ca_rinv[:, i % HALF, :, :], ident[:])
                mm.then_inc(S["ca_r_made"], 1)

            def project_out(n, pair, half):
                pe.wait_ge(S["ca_z_ready"], 1 + 2 * n + half + 1)
                for i in range(HALF):
                    mm = pe.matmul(ps_w[:, P * i:P * i + P], ca_z[:, P * i:P * i + P],
                                   wout_sb[:, pair, :], start=True, stop=True)
                mm.then_inc(S["ca_o"], 1)

            def project(n, pair, par, g, dst=ps_w):
                if g == 0:
                    pe.wait_ge(S["m_copied"], 16 * n + 16)
                if g < 4:
                    for m, (part_m, part_x) in enumerate(PARTS):
                        mm = pe.matmul(dst[:, 0:BANK], m_cur[:, par, g // 2, part_m, :],
                                       xn_parts[:, part_x, BANK * (g % 2):BANK * (g % 2) + BANK],
                                       start=(m == 0), stop=(m == len(PARTS) - 1))
                else:
                    for kt in range(GROUP * (g - 4), GROUP * (g - 3)):
                        mm = pe.matmul(dst[:, P * (kt % GROUP):P * (kt % GROUP) + P],
                                       xn_t[:, P * kt:P * kt + P],
                                       wv_sb[:, bass.ds(pair * P, P)], start=True, stop=True)
                mm.then_inc(S["ca_proj"], 1)

            def start(b, n):
                pe.wait_ge(S["ca_exp"], 1 + UNITS * n)
                pe.wait_ge(S["ca_z_ready"], 1 + 2 * n)
                pe.wait_ge(S["xn_copied"], 16 * b + 16)
                for t in range(T):
                    mm = pe.transpose(ps_qk[:, P * t:P * t + P], xn[:, t, :], ident[:])
                mm.then_inc(S["ca_turned"], 1)
                pe.wait_ge(S["ca_xn_lo"], b + 1)
                pe.wait_ge(S["ca_pt_dve"], 1 + EV * n)
                pe.wait_ge(S["ca_pt_act"], 1 + EV * n)
                for g in range(4):
                    project(n, 0, 0, g, start_bank(g))
                pe.wait_ge(S["ca_xn_t"], b + 1)
                pe.wait_ge(S["ca_x_added"], 1 + 2 * n)
                pe.wait_ge(heads_loaded, 16 * 2)
                for g in (4, 5):
                    project(n, 0, 0, g, start_bank(g))

            def pair_body(b, pair, n, par, ahead, tail):
                for i in range(T):
                    for h in range(2):
                        scores(n, par, i, h, tail)
                        if i == 3 and h == 0 and ahead:
                            if tail:
                                pe.wait_ge(S["ca_x_added"], 1 + 2 * n)
                            else:
                                pe.wait_ge(S["ca_v_ready"], 2 * n + 2)
                            project(n + 1, pair + 1, 1 - par, 0)
                        if i == 4 and h == 0 and ahead:
                            pe.wait_ge(S["ca_q_ready"], 4 * n + 5)
                            project(n + 1, pair + 1, 1 - par, 1)
                        if i:
                            turn(n, i - 1, h)
                        elif tail:
                            turn(n - 1, T - 1, h)
                        if i == 7 and h == 0 and ahead:
                            pe.wait_ge(S["ca_q_ready"], 4 * n + 8)
                            project(n + 1, pair + 1, 1 - par, 4)
                    if i == 0 and tail:
                        values(n - 1, 1 - par, T - 2)
                    if i == 1 and tail:
                        values(n - 1, 1 - par, T - 1)
                        pe.wait_ge(S["ca_v_ready"], 2 * n + 2)
                        spread_inverses(n - 1, 1)
                    if i == 2 and tail:
                        project_out(n - 1, pair - 1, 1)
                    if i == 6:
                        project_out(n, pair, 0)
                    if i >= 2:
                        values(n, par, i - 2)
                    if i == 4 and ahead:
                        pe.wait_ge(S["ca_q_ready"], 4 * n + 6)
                        project(n + 1, pair + 1, 1 - par, 2)
                    if i == 5:
                        if ahead:
                            pe.wait_ge(S["ca_q_ready"], 4 * n + 7)
                        else:
                            pe.wait_ge(S["ca_x_added"], 1 + 2 * n)
                        spread_inverses(n, 0)
                    if i == 6 and ahead:
                        pe.wait_ge(S["ca_x_added"], 1 + 2 * n + 1)
                        project(n + 1, pair + 1, 1 - par, 3)
                    if i == 7 and ahead:
                        pe.wait_ge(S["ca_v_ready"], 2 * n + 3)
                        project(n + 1, pair + 1, 1 - par, 5)

            def flush(b, n):
                for h in range(2):
                    turn(n - 1, T - 1, h)
                values(n - 1, 1, T - 2)
                values(n - 1, 1, T - 1)
                pe.wait_ge(S["ca_x_added"], 1 + 2 * n - 1)
                spread_inverses(n - 1, 1)
                project_out(n - 1, APAIRS - 1, 1)

            causal(pe, start, pair_body, flush)

        def act_causal(act):
            sc = nc.scalar
            act.wait_ge(S["m_made"], AH - 3)
            act.wait_ge(stack_done, B)
            for g, done in enumerate(("m_hi", "m_hi", "ca_pt_act", "ca_exp")):
                src = (ps_qk, ps_s)[g // 2][:, BANK * (g % 2):BANK * (g % 2) + BANK]
                sc.copy(m_sb[:, GROUP * g:GROUP * g + GROUP, 0, :],
                        src.rearrange("p (h k) -> p h k", h=GROUP)).then_inc(S[done], 1)

            def evacuate(n, i, h):
                for g in range(groups(i)):
                    k = groups_before(i, h, g)
                    if k % 2:
                        act.wait_ge(S["ca_pt"], 2 * EV * n + k + 1)
                        k1 = min(i + 1, GROUP * g + GROUP)
                        sc.copy(ca_pt[:, i % 2, h, GROUP * g:k1, :], ps_t[:, 0:P * (k1 - GROUP * g)])\
                          .then_inc(S["ca_pt_act"], 1)

            def q_out(n, par, g, src=ps_w):
                act.wait_ge(S["ca_proj"], 1 + 6 * n + g + 1)
                sc.activation(qm[:, par, g // 2, 0, BANK * (g % 2):BANK * (g % 2) + BANK], src[:, 0:BANK],
                              ACT.Copy, scale=CAUSAL_SCALE).then_inc(S["ca_q_hi"], 1)

            def spread_out(n, half):
                act.wait_ge(S["ca_r_made"], 1 + 2 * n + half + 1)
                sc.copy(ca_rt[:, :], ps_w[:, :]).then_inc(S["ca_rt_ready"], 1)

            def start(b, n):
                act.wait_ge(S["ca_turned"], 1 + b + 1)
                sc.copy(xn_parts[:, 0, :], ps_qk[:, :]).then_inc(S["ca_xn_hi"], 1)
                act.wait_ge(S["ca_xn_lo"], b + 1)
                sc.copy(xn_t[:, :], ps_qk[:, :]).then_inc(S["ca_xn_t"], 1)
                for g in range(4):
                    q_out(n, 0, g, start_bank(g))

            def pair_body(b, pair, n, par, ahead, tail):
                for i in range(T):
                    for h in range(2):
                        act.wait_ge(S["ca_max"], UNITS * n + 2 * i + h + 1)
                        sc.activation(ca_p[:, i % 2, h, 0:(i + 1) * P], (ps_qk, ps_s)[h][:, 0:(i + 1) * P],
                                      ACT.Exp, bias=ca_nmax[:, par, i, h:h + 1],
                                      accum_out=ca_rsum[:, par, i, h:h + 1]).then_inc(S["ca_exp"], 1)
                        if i == 3 and h == 0 and ahead:
                            q_out(n + 1, 1 - par, 0)
                        if i == 4 and h == 0 and ahead:
                            q_out(n + 1, 1 - par, 1)
                        if i:
                            evacuate(n, i - 1, h)
                        elif tail:
                            evacuate(n - 1, T - 1, h)
                    if i == 1 and tail:
                        spread_out(n - 1, 1)
                    if i == 4 and ahead:
                        q_out(n + 1, 1 - par, 2)
                    if i == 5:
                        spread_out(n, 0)
                    if i == 6 and ahead:
                        q_out(n + 1, 1 - par, 3)

            def flush(b, n):
                for h in range(2):
                    evacuate(n - 1, T - 1, h)
                spread_out(n - 1, 1)

            causal(act, start, pair_body, flush)

        def add_stack(dve, p, b):
            nc.vector.scalar_tensor_tensor(x[:, b, :, :], y[:, b, NT:NT + T, :], 0.5, x[:, b, :, :],
                                           ALU.mult, ALU.add).then_inc(stack_done, 1)
            dve.wait_ge(stack_done, B * p + b + 1)

        def dve_causal(dve):
            v = nc.vector
            def statistics(b):
                for t in range(T):
                    st = v.bn_stats(ca_stat[:, b, t, :], x[:, b, t, :])
                st.then_inc(S["ca_stats"], 1)
                dve.wait_ge(S["ca_stats"], b + 1)
                for t in range(T):
                    st = v.bn_aggr(ca_mv[:, b, t, :], ca_stat[:, b, t, :])
                st.then_inc(S["ca_aggr"], 1)

            add_stack(dve, 0, 0)
            statistics(0)
            for b in range(1, B):
                add_stack(dve, 0, b)
            for b in range(1, B):
                statistics(b)
            dve.wait_ge(S["m_made"], AH - 3)
            for g, (ready, n, done) in enumerate((("m_hi", 1, "ca_x_added"), ("m_hi", 2, "ca_pt_dve"),
                                                  ("ca_pt_act", 1, "m_lo"), ("ca_exp", 1, "ca_z_ready"))):
                dve.wait_ge(S[ready], n)
                src = (ps_qk, ps_s)[g // 2][:, BANK * (g % 2):BANK * (g % 2) + BANK]
                heads = slice(GROUP * g, GROUP * g + GROUP)
                v.tensor_tensor(m_sb[:, heads, 1, :], src.rearrange("p (h k) -> p h k", h=GROUP),
                                m_sb[:, heads, 0, :], ALU.subtract).then_inc(S[done], 1)

            def q_rest(n, par, g, src=ps_w):
                dve.wait_ge(S["ca_q_hi"], 4 * n + g + 1)
                cols = slice(BANK * (g % 2), BANK * (g % 2) + BANK)
                v.scalar_tensor_tensor(qm[:, par, g // 2, 1, cols], src[:, 0:BANK], CAUSAL_SCALE,
                                       qm[:, par, g // 2, 0, cols], ALU.mult, ALU.subtract)\
                 .then_inc(S["ca_q_ready"], 1)

            def evacuate(n, i, h):
                for g in range(groups(i)):
                    k = groups_before(i, h, g)
                    if k % 2 == 0:
                        dve.wait_ge(S["ca_pt"], 2 * EV * n + k + 1)
                        k1 = min(i + 1, GROUP * g + GROUP)
                        v.tensor_copy(ca_pt[:, i % 2, h, GROUP * g:k1, :], ps_v[:, 0:P * (k1 - GROUP * g)])\
                         .then_inc(S["ca_pt_dve"], 1)

            def v_out(n, par, g, src=ps_w):
                dve.wait_ge(S["ca_proj"], 1 + 6 * n + g + 1)
                v.tensor_copy(va[:, par, GROUP * (g - 4):GROUP * (g - 3), :], src[:, :])\
                 .then_inc(S["ca_v_ready"], 1)

            def invert(n, par, half):
                dve.wait_ge(S["ca_exp"], 1 + UNITS * n + UNITS // 2 * (half + 1))
                wait(dve, S["ca_r_made"], 1 + 2 * n + half)
                v.reciprocal(ca_inv[:, :, :], ca_rsum[:, par, HALF * half:HALF * half + HALF, :])\
                 .then_inc(S["ca_inverted"], 1)
                dve.wait_ge(S["ca_inverted"], 2 * n + half + 1)
                v.tensor_copy(ca_rinv[:, :, :, :], ca_inv[:, :, :].unsqueeze(3).broadcast_to([P, HALF, 2, W]))\
                 .then_inc(S["ca_rinv_ready"], 1)

            def z_out(n, half):
                dve.wait_ge(S["ca_rt_ready"], 2 * n + half + 1)
                dve.wait_ge(S["ca_pv"], T * n + HALF * (half + 1))
                v.tensor_tensor(ca_z[:, :], ps_z[:, :], ca_rt[:, :], ALU.mult).then_inc(S["ca_z_ready"], 1)

            def x_add(b, n, half):
                dve.wait_ge(S["ca_o"], 2 * n + half + 1)
                dve.wait_ge(S["ca_bias"], 1)
                dve.wait_ge(S["ca_x_added"], 1 + 2 * n + half)
                tiles = x[:, bass.ds(b, 1), HALF * half:HALF * half + HALF, :]
                v.tensor_tensor(tiles, tiles, ps_w[:, :], ALU.add).then_inc(S["ca_x_added"], 1)

            def start(b, n):
                dve.wait_ge(S["ca_xn_hi"], b + 1)
                v.tensor_tensor(xn_parts[:, 1, :], ps_qk[:, :], xn_parts[:, 0, :], ALU.subtract)\
                 .then_inc(S["ca_xn_lo"], 1)
                for g in range(4):
                    q_rest(n, 0, g, start_bank(g))
                for g in (4, 5):
                    v_out(n, 0, g, start_bank(g))

            def pair_body(b, pair, n, par, ahead, tail):
                for i in range(T):
                    for h in range(2):
                        dve.wait_ge(S["ca_s"], UNITS * n + 2 * i + h + 1)
                        v.tensor_reduce(ca_nmax[:, par, i, h:h + 1], (ps_qk, ps_s)[h][:, 0:(i + 1) * P],
                                        AX.X, ALU.max, negate=True).then_inc(S["ca_max"], 1)
                        if h and i in (3, 4) and ahead:
                            q_rest(n + 1, 1 - par, i - 3)
                        if i:
                            evacuate(n, i - 1, h)
                        elif tail:
                            evacuate(n - 1, T - 1, h)
                        if i == 5 and h == 0:
                            invert(n, par, 0)
                        if i == 7 and h == 0 and ahead:
                            v_out(n + 1, 1 - par, 4)
                    if i == 0 and tail:
                        invert(n - 1, 1 - par, 1)
                    if i == 1 and tail:
                        z_out(n - 1, 1)
                    if i == 2 and tail:
                        x_add(b, n - 1, 1)
                    if i == 5:
                        z_out(n, 0)
                    if i == 6:
                        x_add(b, n, 0)
                    if i in (4, 6) and ahead:
                        q_rest(n + 1, 1 - par, i // 2)
                    if i == 7 and ahead:
                        v_out(n + 1, 1 - par, 5)

            def flush(b, n):
                for h in range(2):
                    evacuate(n - 1, T - 1, h)
                invert(n - 1, 1, 1)
                z_out(n - 1, 1)
                x_add(b, n - 1, 1)

            causal(dve, start, pair_body, flush)

        def pool_causal(pool):
            g = nc.gpsimd

            for b in range(B):
                pool.wait_ge(S["ca_aggr"], b + 1)
                g.tensor_tensor(ca_veps[:, b, :], ca_mv[:, b, :, 1], eps_t[:, :], ALU.add).then_inc(S["ca_veps"], 1)
                pool.wait_ge(S["ca_veps"], b + 1)
                g.tensor_tensor(ca_rstd[:, b, :], ca_veps[:, b, :], minus_half[:, 0:T], ALU.pow)\
                 .then_inc(S["ca_rstd"], 1)
                pool.wait_ge(S["ca_rstd"], b + 1)
                for t in range(T):
                    st = g.tensor_scalar(xn_all[:, b, t, :], x[:, b, t, :], ca_mv[:, b, t, 0:1],
                                         ca_rstd[:, b, t:t + 1], ALU.subtract, ALU.mult)
                st.then_inc(S["ca_xn"], 1)
            pool.wait_ge(S["ca_xn"], B)
            tokens = x[:, :, :, :].rearrange("p b t d -> p (b t) d")
            g.tensor_tensor(tokens, tokens, bout_row[:, :].unsqueeze(1).broadcast_to([P, B * T, P]),
                            ALU.add).then_inc(S["ca_bias"], 1)

        tables = [(table[:, lay * T:lay * T + T, :, :], base.rearrange("(t p) c d -> p t c d", p=P))
                  for lay in range(DEPTH) for table, base in ((cos_t, rot_cos), (sin_t, rot_sin))]

        def load_rest(sp):
            for b in range(B):
                sp.dma_start(x[:, b, 1:T, :], x_in[b, P:, :].rearrange("(t p) d -> p t d", p=P))\
                  .then_inc(x_loaded, 16)
            rest = [(probs[:, 0, 0:2, :], local_mask), (probs[:, 1, 0, :], causal_mask),
                    (wo_sb[:, :, :, :], wo.rearrange("l (j k) n -> k l j n", k=P)),
                    (g_col[:, :], ln_g), (b_col[:, :], ln_b), (b1_col[:, :, :, :], b1),
                    (b2_row[:, :, :], b2), (bout_row[:, :], b_out), *tables[2:],
                    *((wqkv_sb[:, lay, :], wqkv[lay, :, :]) for lay in range(1, DEPTH)),
                    *((w2_sb[0:HROWS[j], :, j, :],
                       w2[:, P * j:P * j + HROWS[j], :].rearrange("l k n -> k l n")) for j in range(HC))]
            assert len(rest) * 16 == CONSTS
            for dst, src in rest:
                sp.dma_start(dst, src).then_inc(const_loaded, 16)

        def sp_stack(sp, p):
            def fetch_tile(i):
                step = NT * p + i
                wait(sp, S["a_turned"], step)
                before = i - 1 if not isinstance(i, int) or i else 0
                for dst, src in ((a_in[:, :, 0:W], y[:, :, i, 0:W]),
                                 (a_in[1:P, :, W:P], y[0:P - 1, :, i, W:P]),
                                 (a_in[0:1, :, W:P], y[P - 1:P, :, before, W:P])):
                    sp.dma_start(dst, src).then_inc(S["a_copied"], 16)

            def body(i, more):
                step = NT * p + i
                mC = step - 2
                if isinstance(i, int) and i < 2:
                    sp.wait_ge(S["ln_out"], len(CHUNKS) * p + 1 if i == 0 else len(CHUNKS) * (p + 1))
                if isinstance(i, int) and i == 0:
                    fetch_tile(0)
                    if p == 0:
                        load_rest(sp)
                    sp.wait_ge(S["ln_out"], len(CHUNKS) * p + 2)
                if more:
                    fetch_tile(i + 1)
                if live(i, 2):
                    lay = (i - 2) // T
                    lay = lay if isinstance(lay, int) else sp.snap(lay)
                    wait(sp, S["gv_made"], mC * HC)
                    sp.dma_start(w1_cur[:, :], w1[bass.ds(lay, 1), :, :].rearrange("l k n -> k (l n)"))\
                      .then_inc(S["w1_copied"], 16)
                    sp.wait_ge(S["y1_ready"], (mC + 1) * B)
                    sp.wait_ge(S["first_row"], mC + 1)
                    sp.dma_start(h2[:, :, 0:W], y1[:, :, 0:W]).then_inc(S["h2_copied"], 16)
                    sp.dma_start(h2[1:P, :, W:P], y1[0:P - 1, :, W:P]).then_inc(S["h2_copied"], 16)
                    sp.dma_start(carry[:, :, :], y1[P - 1:P, :, W:P]).then_inc(S["carry_copied"], 16)

            stack(sp, body)

        def sp_causal(sp):
            def start(b, n):
                sp.wait_ge(S["ca_xn"], b + 1)
                sp.wait_ge(S["ca_turned"], 1 + b)
                sp.dma_start(xn[:, :, :], xn_all[:, bass.ds(b, 1), :, :].rearrange("p b t d -> p (b t) d"))\
                  .then_inc(S["xn_copied"], 16)
                sp.wait_ge(S["m_lo"], 1)
                sp.wait_ge(S["ca_exp"], 1 + UNITS * n)
                sp.wait_ge(S["ca_z_ready"], 1 + 2 * n)
                sp.wait_ge(S["ca_proj"], 1 + 6 * n)
                sp.dma_start(m_cur[:, 0, :, :, :].bitcast(F32), m_sb[:, 0:2, :, :].bitcast(F32))\
                  .then_inc(S["m_copied"], 16)

            def pair_body(b, pair, n, par, ahead, tail):
                if ahead:
                    sp.wait_ge(S["ca_proj"], 1 + 6 * n + 1)
                    sp.dma_start(m_cur[:, 1 - par, :, :, :].bitcast(F32),
                                 m_sb[:, bass.ds(2 * pair + 2, 2), :, :].bitcast(F32))\
                      .then_inc(S["m_copied"], 16)

            causal(sp, start, pair_body, lambda b, n: None)

        block = ctx.enter_context(nc.Block())

        @block.sync
        def _(sp):
            sp.dma_start(x[:, :, 0, :], x_in[:, 0:P, :].rearrange("b p d -> p b d")).then_inc(x0_loaded, 16)
            first = [(ident[:, :], identity), (scale_row[:, :, :, :], qk_scale), *tables[0:2],
                     (notfirst[:, :, :], not_first), (wqkv_sb[:, 0, :], wqkv[0, :, :])]
            assert len(first) * 16 == FIRST
            for dst, src in first:
                sp.dma_start(dst, src).then_inc(first_loaded, 16)
            sp_stack(sp, 0)
            sp.wait_ge(S["gv_made"], NT * HC)
            for dst, src in ((wq_sb, wq_t), (wk_sb, wk_t)):
                sp.dma_start(dst, src.rearrange("k (a h) n -> k a h n", h=HEADS)).then_inc(wqk_loaded, 16)
            sp.wait_ge(stack_done, B)
            for dst, src in ((wv_sb[:, :], wv), (wout_sb[:, :, :], w_out)):
                sp.dma_start(dst, src).then_inc(heads_loaded, 16)
            sp_causal(sp)
            sp_stack(sp, 1)
            for b in range(B):
                sp.wait_ge(stack_done, B + b + 1)
                sp.dma_start(out[b, :, :].rearrange("(t p) d -> p t d", p=P), x[:, b, :, :]).then_inc(stored, 16)
            sp.wait_ge(S["carry_copied"], 16 * 2 * NT)
            sp.wait_ge(stored, 16 * B)

        @block.tensor
        def _(pe):
            pe.wait_ge(first_loaded, FIRST)
            pe_stack(pe, 0)
            pe_causal(pe)
            pe_stack(pe, 1)

        @block.scalar
        def _(act):
            act.wait_ge(first_loaded, FIRST)
            act.wait_ge(powers_ready, 1)
            act.wait_ge(q_zeroed, 2)
            act_stack(act, 0)
            act_causal(act)
            act.wait_ge(q_zeroed, 4)
            act_stack(act, 1)

        @block.vector
        def _(dve):
            v = nc.vector
            dve.wait_ge(x0_loaded, 16)
            dve_enter_stats(dve, 0, 0)
            dve_enter_norm(dve, 0, 0)
            dve.wait_ge(first_loaded, FIRST)
            scale_tables(dve, 0)
            for p in range(2):
                if p == 1:
                    dve_enter_stats(dve, 1, 0)
                    dve_enter_norm(dve, 1, 0)
                v.memset(carry[:, :, :], 0.0)
                dve_stack(dve, p)
                dve.wait_ge(S["y2_done"], NT * (p + 1))
                if p == 1:
                    for b in range(B):
                        add_stack(dve, 1, b)
                else:
                    dve_causal(dve)
                    dve.wait_ge(S["ca_x_added"], 1 + 2 * APAIRS * B)

        @block.gpsimd
        def _(pool):
            g = nc.gpsimd
            g.memset(minus_half[:, :], -0.5)
            g.memset(eps_t[:, :], LN_EPS).then_inc(powers_ready, 1)
            pool.wait_ge(powers_ready, 1)
            for p in range(2):
                if p == 1:
                    pool_enter(pool, 1, 0)
                g.memset(q_t[0:W, :, 1:HEADS:2, :], 0.0).then_inc(q_zeroed, 1)
                pool.wait_ge(q_zeroed, 2 * p + 1)
                g.memset(q_t[W:P, :, 0:HEADS:2, :], 0.0).then_inc(q_zeroed, 1)
                pool.wait_ge(q_zeroed, 2 * p + 2)
                if p == 0:
                    pool_enter(pool, 0, 0)
                pool_stack(pool, p)
                if p == 0:
                    pool_causal(pool)


def kernel(L0_attn_resid, L0_attn_W_Q, L0_attn_W_K, L0_attn_W_V, L0_attn_W_out, L0_attn_b_out,
           L0_ffn_wqkv, L0_ffn_q_scale, L0_ffn_k_scale, L0_ffn_wo, L0_ffn_ln_g, L0_ffn_ln_b,
           L0_ffn_w1, L0_ffn_b1, L0_ffn_w2, L0_ffn_b2):
    import numpy as np
    import concourse.bacc as bacc
    from concourse import mybir as mb
    from concourse.bass_utils import run_bass_kernel_spmd

    f = np.float32
    batches, tokens, dim = L0_attn_resid.shape
    depth, inner3 = L0_ffn_wqkv.shape[0], L0_ffn_wqkv.shape[2]
    dh = L0_ffn_q_scale.shape[1]
    hid = L0_ffn_w2.shape[1]
    heads, adh = L0_attn_W_Q.shape[1:]

    half_idx = np.arange(0, dh, 2, dtype=f)
    inv_freq = (f(1.0) / f(10000.0) ** (half_idx / f(dh))).astype(f)
    t = np.arange(tokens, dtype=f)
    freqs = t[:, None] * inv_freq[None, :]
    power = (t - f(tokens // 2)) / f(dh // 2)
    xpos = ((half_idx + f(0.4 * dh)) / f(1.4 * dh))[None, :].astype(f) ** power[:, None]
    cos, sin = np.cos(freqs), np.sin(freqs)
    pair = lambda a, b: np.concatenate([a, b], axis=1)
    rot_cos = np.stack([8 * pair(cos * xpos, cos * xpos), pair(cos / xpos, cos / xpos)], 1).astype(f)
    rot_sin = np.stack([8 * pair(-sin * xpos, sin * xpos), pair(-sin / xpos, sin / xpos)], 1).astype(f)

    w = dim // 2
    i, j = np.arange(w)[:, None], np.arange(w)[None, :]
    own, before = np.where(j <= i, 0.0, MASKED), np.where(j >= i, 0.0, MASKED)
    nothing = np.full((w, w), MASKED)
    second = np.concatenate([before, own], axis=1)
    masks = np.stack([np.concatenate([np.concatenate([own, nothing], 1), second], 0),
                      np.concatenate([np.concatenate([own, before], 1), second], 0)], 1).astype(f)
    i, j = np.arange(dim)[:, None], np.arange(dim)[None, :]
    not_first = np.ones((dim, 2, depth, tokens // dim), f)
    not_first[dim // 2:, 0, :, 0] = 0.0
    not_first[:, 1, :, 0] = 0.0

    rows = lambda a: np.broadcast_to(a, (dim, *a.shape))
    b1 = np.zeros((depth, 2, -(-hid // dim) * dim), f)
    b1[:, :, :hid] = np.asarray(L0_ffn_b1).reshape(depth, 2, hid)
    arrays = {
        "x_in": L0_attn_resid,
        "wq_t": np.transpose(L0_attn_W_Q, (2, 1, 0)),
        "wk_t": np.transpose(L0_attn_W_K, (2, 1, 0)),
        "wv": np.reshape(L0_attn_W_V, (dim, heads * adh)),
        "w_out": np.transpose(L0_attn_W_out, (1, 0, 2)).reshape(heads * adh // dim, dim, dim).transpose(1, 0, 2),
        "b_out": rows(np.asarray(L0_attn_b_out)),
        "wqkv": L0_ffn_wqkv,
        "qk_scale": rows(np.stack([L0_ffn_q_scale, L0_ffn_k_scale], 1)),
        "wo": L0_ffn_wo,
        "ln_g": np.transpose(L0_ffn_ln_g), "ln_b": np.transpose(L0_ffn_ln_b),
        "w1": L0_ffn_w1,
        "b1": b1.reshape(depth, 2, -1, dim).transpose(3, 0, 1, 2),
        "w2": L0_ffn_w2, "b2": rows(np.asarray(L0_ffn_b2)),
        "rot_cos": rot_cos, "rot_sin": rot_sin,
        "local_mask": masks, "not_first": not_first.reshape(dim, 2, -1),
        "causal_mask": np.where(j <= i, 0.0, MASKED).astype(f),
        "identity": np.eye(dim, dtype=f),
    }
    arrays = {k: np.ascontiguousarray(a) for k, a in arrays.items()}
    nc = bacc.Bacc("TRN2", target_bir_lowering=False, num_devices=1)
    args = [nc.dram_tensor(f"in_{k}", a.shape, mb.dt.from_np(a.dtype), kind="ExternalInput").ap()
            for k, a in arrays.items()]
    result = nc.dram_tensor("result", (batches, tokens, dim), mb.dt.float32, kind="ExternalOutput").ap()
    build_program(nc, *args, result)
    r = run_bass_kernel_spmd(nc, [{f"in_{k}": a for k, a in arrays.items()}], core_ids=[0])
    return r.results[0]["result"]
```
